# Optimizing a Trainium2 kernel written in Bass

```python
import numpy as np
import jax
import jax.numpy as jnp

def _softmax(x, axis=-1):
    return jax.nn.softmax(x, axis=axis)

def _gelu(x):
    return jax.nn.gelu(x, approximate=True)

def _silu(x):
    return jax.nn.silu(x)

def _sigmoid(x):
    return jax.nn.sigmoid(x)

def _layernorm(x, axis=-1, eps=1e-05):
    m = jnp.mean(x, axis=axis, keepdims=True)
    v = jnp.var(x, axis=axis, keepdims=True)
    return (x - m) / jnp.sqrt(v + eps)

def _scatter_add(tgt, idx, src, axis=0):
    return tgt.at[idx].add(src)

def _segment_sum(src, seg, n):
    return jax.ops.segment_sum(src, seg, n)
kernel_name = 'mk_cond_seq_d2_seqx_r8_b96f96'

def setup_inputs(seed: int=0):
    np.random.seed(seed)
    _w = jnp.asarray

    def _rec_inputs():
        import jax
        import jax.numpy as jnp
        _rk = jax.random.key(seed)
        x = 1.648e-05 + 1 * jax.random.normal(jax.random.fold_in(_rk, 1), (2, 512, 144), jnp.float32)
        _lenS = 512 - jax.random.randint(jax.random.fold_in(_rk, 7), (2,), 0, max(1, 512 // 4) + 1, jnp.int32)
        _lenS2 = 512 - jax.random.randint(jax.random.fold_in(_rk, 8), (2,), 0, max(1, 512 // 4) + 1, jnp.int32)
        cond_1152 = 0.00914911 + 1.00357 * jax.random.normal(jax.random.fold_in(_rk, 11), (2, 144), jnp.float32)
        return (x, cond_1152)
    x, cond_1152 = _rec_inputs()

    def _L0_cond_setup():
        import jax, jax.numpy as jnp
        import numpy as np
        B, S, D = (8, 128, 144)
        H = 16
        HD = D // H
        HID = int(D * 4.0)
        LN_EPS = 1e-05

        def layer_norm(x, w, b):
            m = jnp.mean(x, axis=-1, keepdims=True)
            v = jnp.mean(jnp.square(x - m), axis=-1, keepdims=True)
            return (x - m) * jax.lax.rsqrt(v + LN_EPS) * w + b

        def modulate(x, shift, scale):
            return x * (1.0 + scale[:, None, :]) + shift[:, None, :]

        def attention(x, wq, wk, wv, wo, wo_b):
            b, s, d = x.shape
            q = (x @ wq).reshape(b, s, H, HD).transpose(0, 2, 1, 3)
            k = (x @ wk).reshape(b, s, H, HD).transpose(0, 2, 1, 3)
            v = (x @ wv).reshape(b, s, H, HD).transpose(0, 2, 1, 3)
            scale = 1.0 / np.sqrt(HD).astype(np.float32)
            att = jnp.einsum('bhqd,bhkd->bhqk', q, k) * scale
            att = jax.nn.softmax(att, axis=-1)
            out = jnp.einsum('bhqk,bhkd->bhqd', att, v)
            out = out.transpose(0, 2, 1, 3).reshape(b, s, d)
            return out @ wo + wo_b
        key = jax.random.key(seed)
        ks = jax.random.split(key, 16)
        s = 0.02
        return {'x': jax.random.normal(ks[0], (B, S, D), jnp.float32), 'c': jax.random.normal(ks[1], (B, D), jnp.float32), 'ln1_w': jnp.ones((D,), jnp.float32), 'ln1_b': jnp.zeros((D,), jnp.float32), 'wq': jax.random.normal(ks[2], (D, D), jnp.float32) * s, 'wk': jax.random.normal(ks[3], (D, D), jnp.float32) * s, 'wv': jax.random.normal(ks[4], (D, D), jnp.float32) * s, 'wo': jax.random.normal(ks[5], (D, D), jnp.float32) * s, 'wo_b': jnp.zeros((D,), jnp.float32), 'ln2_w': jnp.ones((D,), jnp.float32), 'ln2_b': jnp.zeros((D,), jnp.float32), 'fc1_w': jax.random.normal(ks[6], (D, HID), jnp.float32) * s, 'fc1_b': jnp.zeros((HID,), jnp.float32), 'fc2_w': jax.random.normal(ks[7], (HID, D), jnp.float32) * s, 'fc2_b': jnp.zeros((D,), jnp.float32), 'ada_w': jax.random.normal(ks[8], (D, 6 * D), jnp.float32) * s, 'ada_b': jnp.zeros((6 * D,), jnp.float32)}
    _L0_cond_all = _L0_cond_setup()
    _L0_cond_in = {k: v for k, v in _L0_cond_all.items() if k in ('ln1_w', 'ln1_b', 'wq', 'wk', 'wv', 'wo', 'wo_b', 'ln2_w', 'ln2_b', 'fc1_w', 'fc1_b', 'fc2_w', 'fc2_b', 'ada_w', 'ada_b')}
    del _L0_cond_all

    def _L1_cond_setup():
        import jax, jax.numpy as jnp
        import numpy as np
        NUM_HEADS = 16
        NUM_EXPERTS = 4
        TOP_K = 2
        LN_EPS = 1e-06

        def _ln(h):
            mu = jnp.mean(h, axis=-1, keepdims=True)
            var = jnp.var(h, axis=-1, keepdims=True)
            return (h - mu) * jax.lax.rsqrt(var + LN_EPS)

        def _modulate(h, shift, scale):
            return h * (1.0 + scale[:, None, :]) + shift[:, None, :]
        key = jax.random.key(seed)
        ks = jax.random.split(key, 12)
        B, N, C = (8, 128, 144)
        H = 4 * C
        E = NUM_EXPERTS
        s = 0.02
        return {'x': jax.random.normal(ks[0], (B, N, C), jnp.float32), 'c': jax.random.normal(ks[1], (B, C), jnp.float32), 'w_adaln': jax.random.normal(ks[2], (C, 6 * C), jnp.float32) * s, 'b_adaln': jnp.zeros((6 * C,), jnp.float32), 'w_qkv': jax.random.normal(ks[3], (C, 3 * C), jnp.float32) * s, 'b_qkv': jnp.zeros((3 * C,), jnp.float32), 'w_proj': jax.random.normal(ks[4], (C, C), jnp.float32) * s, 'b_proj': jnp.zeros((C,), jnp.float32), 'w_gate': jax.random.normal(ks[5], (C, E), jnp.float32) * s, 'w1': jax.random.normal(ks[6], (E, C, H), jnp.float32) * s, 'b1': jnp.zeros((E, H), jnp.float32), 'w2': jax.random.normal(ks[7], (E, H, C), jnp.float32) * s, 'b2': jnp.zeros((E, C), jnp.float32)}
    _L1_cond_all = _L1_cond_setup()
    _L1_cond_in = {k: v for k, v in _L1_cond_all.items() if k in ('w_adaln', 'b_adaln', 'w_qkv', 'b_qkv', 'w_proj', 'b_proj', 'w_gate', 'w1', 'b1', 'w2', 'b2')}
    del _L1_cond_all
    return {'x': x, 'cond_1152': cond_1152, 'L0_cond_ln1_w': _L0_cond_in['ln1_w'], 'L0_cond_ln1_b': _L0_cond_in['ln1_b'], 'L0_cond_wq': _L0_cond_in['wq'], 'L0_cond_wk': _L0_cond_in['wk'], 'L0_cond_wv': _L0_cond_in['wv'], 'L0_cond_wo': _L0_cond_in['wo'], 'L0_cond_wo_b': _L0_cond_in['wo_b'], 'L0_cond_ln2_w': _L0_cond_in['ln2_w'], 'L0_cond_ln2_b': _L0_cond_in['ln2_b'], 'L0_cond_fc1_w': _L0_cond_in['fc1_w'], 'L0_cond_fc1_b': _L0_cond_in['fc1_b'], 'L0_cond_fc2_w': _L0_cond_in['fc2_w'], 'L0_cond_fc2_b': _L0_cond_in['fc2_b'], 'L0_cond_ada_w': _L0_cond_in['ada_w'], 'L0_cond_ada_b': _L0_cond_in['ada_b'], 'L1_cond_w_adaln': _L1_cond_in['w_adaln'], 'L1_cond_b_adaln': _L1_cond_in['b_adaln'], 'L1_cond_w_qkv': _L1_cond_in['w_qkv'], 'L1_cond_b_qkv': _L1_cond_in['b_qkv'], 'L1_cond_w_proj': _L1_cond_in['w_proj'], 'L1_cond_b_proj': _L1_cond_in['b_proj'], 'L1_cond_w_gate': _L1_cond_in['w_gate'], 'L1_cond_w1': _L1_cond_in['w1'], 'L1_cond_b1': _L1_cond_in['b1'], 'L1_cond_w2': _L1_cond_in['w2'], 'L1_cond_b2': _L1_cond_in['b2']}

def reference(x, cond_1152, L0_cond_ln1_w, L0_cond_ln1_b, L0_cond_wq, L0_cond_wk, L0_cond_wv, L0_cond_wo, L0_cond_wo_b, L0_cond_ln2_w, L0_cond_ln2_b, L0_cond_fc1_w, L0_cond_fc1_b, L0_cond_fc2_w, L0_cond_fc2_b, L0_cond_ada_w, L0_cond_ada_b, L1_cond_w_adaln, L1_cond_b_adaln, L1_cond_w_qkv, L1_cond_b_qkv, L1_cond_w_proj, L1_cond_b_proj, L1_cond_w_gate, L1_cond_w1, L1_cond_b1, L1_cond_w2, L1_cond_b2):
    import jax
    import jax.numpy as jnp

    def _L0_cond_ref(x, c, ln1_w, ln1_b, wq, wk, wv, wo, wo_b, ln2_w, ln2_b, fc1_w, fc1_b, fc2_w, fc2_b, ada_w, ada_b):
        import jax, jax.numpy as jnp
        import numpy as np
        B, S, D = (8, 128, 144)
        H = 16
        HD = D // H
        HID = int(D * 4.0)
        LN_EPS = 1e-05

        def layer_norm(x, w, b):
            m = jnp.mean(x, axis=-1, keepdims=True)
            v = jnp.mean(jnp.square(x - m), axis=-1, keepdims=True)
            return (x - m) * jax.lax.rsqrt(v + LN_EPS) * w + b

        def modulate(x, shift, scale):
            return x * (1.0 + scale[:, None, :]) + shift[:, None, :]

        def attention(x, wq, wk, wv, wo, wo_b):
            b, s, d = x.shape
            q = (x @ wq).reshape(b, s, H, HD).transpose(0, 2, 1, 3)
            k = (x @ wk).reshape(b, s, H, HD).transpose(0, 2, 1, 3)
            v = (x @ wv).reshape(b, s, H, HD).transpose(0, 2, 1, 3)
            scale = 1.0 / np.sqrt(HD).astype(np.float32)
            att = jnp.einsum('bhqd,bhkd->bhqk', q, k) * scale
            att = jax.nn.softmax(att, axis=-1)
            out = jnp.einsum('bhqk,bhkd->bhqd', att, v)
            out = out.transpose(0, 2, 1, 3).reshape(b, s, d)
            return out @ wo + wo_b
        mod = jax.nn.silu(c) @ ada_w + ada_b
        sh_msa, sc_msa, g_msa, sh_mlp, sc_mlp, g_mlp = jnp.split(mod, 6, axis=1)
        h = modulate(layer_norm(x, ln1_w, ln1_b), sh_msa, sc_msa)
        x = x + g_msa[:, None, :] * attention(h, wq, wk, wv, wo, wo_b)
        h = modulate(layer_norm(x, ln2_w, ln2_b), sh_mlp, sc_mlp)
        h = jax.nn.gelu(h @ fc1_w + fc1_b, approximate=False) @ fc2_w + fc2_b
        x = x + g_mlp[:, None, :] * h
        return x

    def _L1_cond_ref(x, c, w_adaln, b_adaln, w_qkv, b_qkv, w_proj, b_proj, w_gate, w1, b1, w2, b2):
        import jax, jax.numpy as jnp
        import numpy as np
        NUM_HEADS = 16
        NUM_EXPERTS = 4
        TOP_K = 2
        LN_EPS = 1e-06

        def _ln(h):
            mu = jnp.mean(h, axis=-1, keepdims=True)
            var = jnp.var(h, axis=-1, keepdims=True)
            return (h - mu) * jax.lax.rsqrt(var + LN_EPS)

        def _modulate(h, shift, scale):
            return h * (1.0 + scale[:, None, :]) + shift[:, None, :]
        B, N, C = x.shape
        nh = NUM_HEADS
        hd = C // nh
        mod = jax.nn.silu(c) @ w_adaln + b_adaln
        sh_msa, sc_msa, g_msa, sh_mlp, sc_mlp, g_mlp = jnp.split(mod, 6, axis=-1)
        h = _modulate(_ln(x), sh_msa, sc_msa)
        qkv = (h @ w_qkv + b_qkv).reshape(B, N, 3, nh, hd).transpose(2, 0, 3, 1, 4)
        q, k, v = (qkv[0], qkv[1], qkv[2])
        attn = jax.nn.softmax(jnp.einsum('bhqd,bhkd->bhqk', q, k) * hd ** (-0.5), axis=-1)
        o = jnp.einsum('bhqk,bhkd->bhqd', attn, v).transpose(0, 2, 1, 3).reshape(B, N, C)
        o = o @ w_proj + b_proj
        x = x + g_msa[:, None, :] * o
        xn = _modulate(_ln(x), sh_mlp, sc_mlp)
        xf = xn.reshape(-1, C)
        gate_logits = xf @ w_gate
        topk_logits, topk_idx = jax.lax.top_k(gate_logits, TOP_K)
        gates = jax.nn.softmax(topk_logits, axis=-1)
        cw = jnp.sum(jax.nn.one_hot(topk_idx, NUM_EXPERTS, dtype=xf.dtype) * gates[..., None], axis=1)
        hmid = jax.nn.gelu(jnp.einsum('tc,ech->eth', xf, w1) + b1[:, None, :], approximate=True)
        eo = jnp.einsum('eth,ehc->etc', hmid, w2) + b2[:, None, :]
        moe = jnp.einsum('te,etc->tc', cw, eo).reshape(B, N, C)
        return x + g_mlp[:, None, :] * moe
    x = _L0_cond_ref(x, cond_1152, L0_cond_ln1_w, L0_cond_ln1_b, L0_cond_wq, L0_cond_wk, L0_cond_wv, L0_cond_wo, L0_cond_wo_b, L0_cond_ln2_w, L0_cond_ln2_b, L0_cond_fc1_w, L0_cond_fc1_b, L0_cond_fc2_w, L0_cond_fc2_b, L0_cond_ada_w, L0_cond_ada_b)
    x = _L1_cond_ref(x, cond_1152, L1_cond_w_adaln, L1_cond_b_adaln, L1_cond_w_qkv, L1_cond_b_qkv, L1_cond_w_proj, L1_cond_b_proj, L1_cond_w_gate, L1_cond_w1, L1_cond_b1, L1_cond_w2, L1_cond_b2)
    return x

_drawn_inputs = setup_inputs


def setup_inputs(seed=0):
    import zlib

    import numpy as np

    out = dict(_drawn_inputs(seed))
    spreads = {'L0_cond_ln1_w': (1.0, 0.6),
     'L0_cond_ln1_b': (0.0, 0.8),
     'L0_cond_wo_b': (0.0, 0.429),
     'L0_cond_ln2_w': (1.0, 0.6),
     'L0_cond_ln2_b': (0.0, 0.8),
     'L0_cond_fc1_b': (0.0, 0.8),
     'L0_cond_fc2_b': (0.0, 0.468),
     'L0_cond_ada_b': (0.0, 0.47),
     'L1_cond_b_adaln': (0.0, 0.556),
     'L1_cond_b_qkv': (0.0, 0.8),
     'L1_cond_b_proj': (0.0, 0.433),
     'L1_cond_b1': (0.0, 0.8),
     'L1_cond_b2': (0.0, 0.666)}
    factors = {'L0_cond_wq': 8.0,
     'L0_cond_wk': 8.0,
     'L0_cond_wv': 8.0,
     'L0_cond_wo': 8.0,
     'L0_cond_fc1_w': 4.701,
     'L0_cond_fc2_w': 4.464,
     'L1_cond_w_adaln': 3.063,
     'L1_cond_w_qkv': 8.0,
     'L1_cond_w_proj': 8.0,
     'L1_cond_w_gate': 5.761,
     'L1_cond_w1': 7.785,
     'L1_cond_w2': 7.29}
    for name, (base, spread) in spreads.items():
        noise = np.random.default_rng([zlib.crc32(name.encode()), seed]).standard_normal(out[name].shape)
        drawn = base * np.exp(spread * noise) if base else spread * noise
        out[name] = jnp.asarray(drawn.astype(out[name].dtype))
    for name, factor in factors.items():
        out[name] = (out[name] * factor).astype(out[name].dtype)
    return out
```

```python
import concourse.bass as bass
from concourse import mybir
from contextlib import ExitStack

fp32 = mybir.dt.float32
bf16 = mybir.dt.bfloat16
ALU = mybir.AluOpType
ACT = mybir.ActivationFunctionType
AX = mybir.AxisListType

P = 128
B, S, D = 2, 512, 144
T = S // P
C = B * T
NH, HD = 16, 9
G4 = 4
NHG = NH // G4
NPAIR = B * NH // 2
DT = D - P
NPART = 6
TR_ = NPART * DT
HID = 4 * D
E = 4
NM0 = -(-HID // P)
NM1 = E * HID // P
PW = 64
MXC = NPART * HD
NA = 6 * D + 4 * TR_
EPS = (1e-5, 1e-6)
Q_PART = ((0, 1, 2), (3, 4), (5,))
K_PART = ((0, 3, 5), (1, 4), (2,))
SECT = (0, 1, 3, 4)


def two_blocks(nc, x, cond_t, ident, cols_main, cols_tail, ada, rows, wqkv, wqkv_tail, wo,
               w1, w1_tail, gate, gate_tail, w2, b1_cols, out):
    ctx = ExitStack()
    with ctx:
        def sb(name, shape, dt=fp32):
            return ctx.enter_context(nc.sbuf_tensor(name, shape, dt))

        def sem(name):
            return ctx.enter_context(nc.semaphore(name))

        A_PROB, A_KT, A_QT, A_QK = 0, 16384, 16384 + 8192, 16384 + 8192 + 4096
        arena = sb("arena", [P, A_QK + 8192])

        def f32(off, n):
            return arena[:, off:off + n]

        def b16(off, n):
            return arena[:, off:off + n].bitcast(bf16)

        prob = f32(A_PROB, 16384).rearrange("p (u h c q) -> p u h c q", u=2, h=G4, c=T)
        kT = b16(A_KT, 8192).rearrange("p (b h s) -> p b h s", b=B, h=NH)
        qT = b16(A_QT, 4096).rearrange("p (b r s) -> p b r s", b=B, r=NH // 2)
        qk = b16(A_QK, 8192).rearrange("p (k b t h c) -> p k b t h c", k=2, b=B, t=T, h=NH)
        o = A_PROB + NM1 * S
        z = f32(o, C * 224).rearrange("p (b t d) -> p b t d", b=B, t=T)
        o += C * 224
        hT = f32(o, C * P).rearrange("p (b s) -> p b s", b=B)
        o += C * P
        hR = b16(o, C * P // 2).rearrange("p (b s) -> p b s", b=B)
        o += C * P // 2
        t_h = f32(o, C * P).rearrange("p (b s) -> p b s", b=B)
        o += C * P
        t_a = b16(o, C * P // 2).rearrange("p (b s) -> p b s", b=B)
        o += C * P // 2
        t_b = f32(o, C * P).rearrange("p (b s) -> p b s", b=B)
        o += C * P
        t_c = b16(o, C * P // 2).rearrange("p (b s) -> p b s", b=B)
        o += C * P // 2
        assert o <= A_KT
        big = f32(A_PROB + NM1 * S, 3 * C * E * E).rearrange("p (n c e j) -> p n c e j", n=3, c=C, e=E)
        o = A_PROB
        ada_m = f32(o, 2 * NA).rearrange("p (l f) -> p l f", l=2)
        o += 2 * NA
        ada_t = f32(o, 2 * NA).rearrange("p (l f) -> p l f", l=2)
        o += 2 * NA
        rows_s = f32(o, 7 * D)
        o += 7 * D
        wo_m = f32(o, 2 * D).rearrange("p (l d) -> p l d", l=2)
        o += 2 * D
        wo_t = f32(o, 2 * D).rearrange("p (l d) -> p l d", l=2)
        o += 2 * D
        w2_raw = f32(o, NM0 * D).rearrange("p (m d) -> p m d", m=NM0)
        o += NM0 * D
        cb_m = f32(o, B * P).rearrange("p (b s) -> p b s", b=B)
        o += B * P
        cb_t = f32(o, B * P).rearrange("p (b s) -> p b s", b=B)
        o += B * P
        gates = f32(o, 4 * B * D).rearrange("p (s b d) -> p s b d", s=4, b=B)
        o += 4 * B * D
        assert o <= A_PROB + NM1 * S
        NW = 2 * 3 * D + HID + E
        w_src = f32(A_QT, NW)
        w_a = b16(A_QT + NW, NW // 2)
        w_b = f32(A_QK, NW)
        w_c = b16(A_QK + NW, NW // 2)
        NE = E * HID
        e_src = f32(A_QT, NE)
        e_a = b16(A_QT + NE, HID // 2)
        e_b = f32(A_QT + NE + HID // 2, HID)
        e_c = b16(A_QT + NE + HID // 2 + HID, HID // 2)
        hm0 = f32(A_PROB, B * NM0 * S).rearrange("p (b m s) -> p b m s", b=B, m=NM0)
        hm1 = [f32(A_PROB, NM1 * S).rearrange("p (m s) -> p m s", m=NM1),
               f32(A_KT, NM1 * S).rearrange("p (m s) -> p m s", m=NM1)]
        w1e = f32(A_QK, NE)
        w2e = f32(A_QK + NE, NM1 * D).rearrange("p (m d) -> p m d", m=NM1)
        b2_row = f32(A_QK + NE + NM1 * D, E * D).rearrange("p (e d) -> p e d", e=E)

        X = sb("X", [P, C, D])
        qkv = sb("qkv", [P, C, 3 * D])
        o_tok = sb("o_tok", [P, C, D])
        wq_m = sb("wq_m", [P, 2, 3 * D])
        w_tail = sb("w_tail", [P, NW], bf16)
        we_tail = sb("we_tail", [P, NE], bf16)
        w1d = sb("w1d", [P, HID])
        gate_m = sb("gate_m", [P, E])
        wog_m = sb("wog_m", [P, 2, B, D])
        wog_t = sb("wog_t", [DT, 2, B, D])
        w2g = sb("w2g", [P, NM0, B, D])
        gbias = sb("gbias", [P, 3, B, D])
        g_last = sb("g_last", [P, B, D])
        bqkv_row = sb("bqkv_row", [P, 3 * D])
        b1c = sb("b1c", [P, NM0 + NM1])
        vS = sb("vS", [P, 2, T, G4, 32])
        oS = sb("oS", [P, S])
        idf = sb("idf", [P, P])
        idb = sb("idb", [P, P], bf16)
        cm = sb("cm", [P, 12])
        ct = sb("ct", [TR_, 16])
        c_m = sb("c_m", [P, 5, B])
        c_t = sb("c_t", [DT, 5, B])
        mod_m = sb("mod_m", [P, 2, 4, B])
        mod_t = sb("mod_t", [TR_, 2, 4, B])
        sc1_m = sb("sc1_m", [P, 2, 2, B])
        sc1_t = sb("sc1_t", [TR_, 2, 2, B])
        ab_m = sb("ab_m", [P, 2, 2, 2, B])
        ab_t = sb("ab_t", [TR_, 2, 2, 2, B])
        st6 = sb("st6", [P, B, T, 6])
        mv = sb("mv", [P, B, T, 2])
        ln4 = sb("ln4", [P, 6, B, T])
        mx = sb("mx", [P, 2, T, 2])
        nmx = sb("nmx", [P, T, 2])
        rc = sb("rc", [P, T, G4])
        spl = sb("spl", [P, 2, T, G4 * HD])
        spg = sb("spg", [P, 2, T, G4 * HD])
        lg = sb("lg", [P, C, E])
        lw = sb("lw", [P, C, E])
        cw = sb("cw", [P, C, E])
        sm = sb("sm", [P, 4, C])
        below = sb("below", [P, E, E])
        acc = o_tok
        oT = hT
        oTt = t_h
        ps = ctx.enter_context(nc.psum_tensor("ps", [P, 8, 512], fp32))
        psb = [ps[:, n, :].bitcast(bf16) for n in range(8)]
        TRB, PVB = 7, 6

        NAMES = """x_in0 x_in1 cond_in consts_in ada_in rows_in wo_in w2d_in wq_in wt_in w1d_in misc_in et_in
        we_in out_done id_b silu_a silu_v mod_mm mod_v cb_v gate_mm gates_v gated kt_zero qk_pad vs_pad
        wt_v et_v ln_stats ln_aggr ln_ve ln_log ln_y ln_newton ln_z ln_zt ln_ht ln_r
        qkv_mm qkv_ev xb o_tr oT_ev oTt_ev proj_mm x_new fc1_mm gelu fc2_mm lg_mm route bias2 moe_mm
        moe_acc fin""".split()
        s = {n: sem(n) for n in NAMES}
        AT = """st ex sm mx nstep tq tk evq evk pv oev ot on vs spv spa spp qz""".split()
        a = [{n: sem(f"{n}{l}") for n in AT} for l in range(2)]
        block = ctx.enter_context(nc.Block())

        def pos(i, k):
            q, r = divmod(k, 4)
            hg = i + q
            return min(max(hg, 0), NHG - 1) if isinstance(i, int) else hg, r // 2, r % 2

        LOOP0, LOOPN = 4, 8

        def halves(eng, half):
            for h in range(-3, LOOP0):
                half(0, h, True)
            with eng.Fori(0, LOOPN // 4) as i:
                for k in range(LOOP0, LOOP0 + 4):
                    half(i, k, False)
            for h in range(LOOP0 + LOOPN, NPAIR + 2):
                half(0, h, True)

        def has(i, k, peeled, lo=0):
            return not peeled or lo <= 4 * i + k < NPAIR

        @block.sync
        def _(sp):
            sp.dma_start(X[:, 0:T, :], x[0:S, :].rearrange("(c p) d -> p c d", p=P)).then_inc(s["x_in0"], 16)
            sp.dma_start(X[:, T:C, :], x[S:B * S, :].rearrange("(c p) d -> p c d", p=P)).then_inc(s["x_in1"], 16)
            sp.dma_start(idf[:, :], ident).then_inc(s["consts_in"], 16)
            sp.dma_start(wq_m[:, :, :], wqkv.rearrange("l p f -> p l f")).then_inc(s["wq_in"], 16)
            sp.dma_start(w1d[:, :], w1[0:P, 0:HID]).then_inc(s["w1d_in"], 16)
            sp.dma_start(w2_raw[:, 0:NM0 - 1, :], w2[0:(NM0 - 1) * P, :].rearrange("(m p) d -> p m d", p=P)).then_inc(s["w2d_in"], 16)
            sp.dma_start(w2_raw[0:64, NM0 - 1, :], w2[(NM0 - 1) * P:HID, :]).then_inc(s["w2d_in"], 16)
            sp.wait_ge(a[0]["on"], 16)
            sp.dma_start(e_src[0:TR_, :], w1_tail[:, HID:HID + NE]).then_inc(s["et_in"], 16)
            sp.wait_ge(a[1]["tq"], NPAIR)
            sp.dma_start(w1e, w1[0:P, HID:HID + NE]).then_inc(s["we_in"], 16)
            sp.dma_start(w2e, w2[HID:HID + NE, :].rearrange("(m p) d -> p m d", p=P)).then_inc(s["we_in"], 16)
            sp.dma_start(b2_row.rearrange("p e d -> p (e d)"), rows[:, 7 * D:11 * D].partition_broadcast(P)).then_inc(s["we_in"], 16)
            for c in range(C):
                sp.wait_ge(s["fin"], 2 * (c + 1))
                sp.dma_start(out[c * P:(c + 1) * P, :], X[:, c, :]).then_inc(s["out_done"], 16)
            sp.wait_ge(s["out_done"], 16 * C)

        def split_pool(pool, l, hg, b):
            for kq, where in ((0, Q_PART), (1, K_PART)):
                v = qkv[:, b * T:(b + 1) * T, bass.ds(kq * D + hg * (G4 * HD), G4 * HD)]
                v4 = v.rearrange("p t (h d) -> p t h d", h=G4)
                r = spg[:, kq]
                r4 = r.rearrange("p t (h d) -> p t h d", h=G4)

                def put(g):
                    return qk[:, kq, b, :, bass.ds(hg * G4, G4), g * HD:(g + 1) * HD]
                yield v4, r4, put, where

        @block.gpsimd
        def _(pool):
            pool.dma_start(ada_m[:, :, :], ada[:, 0:P, :].rearrange("l p f -> p l f")).then_inc(s["ada_in"], 16)
            pool.dma_start(ada_t[0:DT, :, :], ada[:, P:D, :].rearrange("l p f -> p l f")).then_inc(s["ada_in"], 16)
            pool.dma_start(rows_s[:, :], rows[:, 0:7 * D].partition_broadcast(P)).then_inc(s["rows_in"], 16)
            pool.dma_start(wo_m[:, :, :], wo[:, 0:P, :].rearrange("l p f -> p l f")).then_inc(s["wo_in"], 16)
            pool.dma_start(wo_t[0:DT, :, :], wo[:, P:D, :].rearrange("l p f -> p l f")).then_inc(s["wo_in"], 16)
            pool.dma_start(bqkv_row[:, :], rows[:, 11 * D:14 * D].partition_broadcast(P)).then_inc(s["rows_in"], 16)
            kz = kT.rearrange("p b (r two) s -> p (b r) two s", two=2)
            pool.memset(kz[64:128, :, 0, :].bitcast(fp32), 0.0).then_inc(s["kt_zero"], 1)
            pool.wait_ge(s["kt_zero"], 1)
            pool.memset(kz[0:64, :, 1, :].bitcast(fp32), 0.0).then_inc(s["kt_zero"], 1)
            pool.wait_ge(s["kt_zero"], 2)
            pool.memset(vS[:, :, :, :, :], 0.0).then_inc(s["vs_pad"], 1)
            pool.wait_ge(s["vs_pad"], 1)
            pool.memset(vS[:, :, :, :, 0:1], 1.0).then_inc(s["vs_pad"], 1)
            pool.wait_ge(s["gates_v"], 4)
            pool.wait_ge(s["wo_in"], 32)
            for l in range(2):
                for b in range(B):
                    pool.tensor_tensor(wog_m[:, l, b, :], wo_m[:, l, :], gates[:, 2 * l, b, :], ALU.mult).then_inc(s["gated"], 1)
                    pool.tensor_tensor(wog_t[:, l, b, :], wo_t[0:DT, l, :], gates[0:DT, 2 * l, b, :], ALU.mult).then_inc(s["gated"], 1)
            for n, sec in enumerate((0, 2, 1)):
                for b in range(B):
                    pool.tensor_tensor(gbias[:, n, b, :], rows_s[:, (4 + n) * D:(5 + n) * D], gates[:, sec, b, :], ALU.mult).then_inc(s["gated"], 1)
            pool.wait_ge(s["w2d_in"], 32)
            for b in range(B):
                for m in range(NM0):
                    r = P if m < NM0 - 1 else HID - P * (NM0 - 1)
                    pool.tensor_tensor(w2g[0:r, m, b, :], w2_raw[0:r, m, :], gates[0:r, 1, b, :], ALU.mult).then_inc(s["gated"], 1)
            pool.tensor_copy(g_last[:, :, :], gates[:, 3, :, :]).then_inc(s["gated"], 1)

            def add_bias(n):
                for c in range(C):
                    pool.tensor_tensor(X[:, c, :], X[:, c, :], gbias[:, n, c // T, :], ALU.add).then_inc(s["xb"], 1)

            for l in range(2):
                q = a[l]
                pool.wait_ge(s["ln_z"], 32 * l + 16)
                if l == 0:
                    pool.wait_ge(s["gated"], GATED)
                add_bias(l)
                pool.wait_ge(s["qkv_ev"], 8 * l + 8)

                def stage_v(i, u, first):
                    if not first:
                        pool.wait_ge(q["pv"], 8 * i + 4 * u - 4)
                    v = qkv[:, u * T:(u + 1) * T, bass.ds(2 * D + i * (G4 * HD), G4 * HD)]
                    pool.tensor_copy(vS[:, u, :, :, 1:1 + HD], v.rearrange("p t (h d) -> p t h d", h=G4)).then_inc(q["vs"], 1)

                def split_group(i, u, n):
                    at = 14 * n
                    for v4, r4, put, w in split_pool(pool, l, i, u):
                        p0, p1, p2 = w
                        pool.tensor_copy(put(p0[0]), v4).then_inc(q["spp"], 1)
                        pool.tensor_copy(put(p0[1]), v4).then_inc(q["spp"], 1)
                        pool.wait_ge(q["spp"], at + 1)
                        pool.tensor_copy(put(p0[2]), v4).then_inc(q["spp"], 1)
                        pool.tensor_tensor(r4, v4, put(p0[0]), ALU.subtract).then_inc(q["spp"], 1)
                        pool.wait_ge(q["spp"], at + 4)
                        pool.tensor_copy(put(p1[0]), r4).then_inc(q["spp"], 1)
                        pool.wait_ge(q["spp"], at + 5)
                        pool.tensor_copy(put(p1[1]), r4).then_inc(q["spp"], 1)
                        pool.tensor_tensor(put(p2[0]), r4, put(p1[0]), ALU.subtract).then_inc(q["spp"], 1)
                        at = at + 7

                pool.wait_ge(s["qk_pad"], 2)

                def round_of(i, first):
                    for u in range(B):
                        split_group(i, u, 2 * i + (u - 2))
                        stage_v(i - 1, u, first)

                round_of(1, True)
                with pool.Fori(2, NHG) as i:
                    round_of(i, False)
                for u in range(B):
                    stage_v(NHG - 1, u, False)
                if l == 0:
                    pool.wait_ge(s["ln_z"], 32)
                    add_bias(2)

        @block.scalar
        def _(act):
            act.dma_start(c_m[:, 0, :], cond_t[0:P, :]).then_inc(s["cond_in"], 16)
            act.dma_start(c_t[:, 0, :], cond_t[P:D, :]).then_inc(s["cond_in"], 16)
            act.dma_start(cm[:, :], cols_main).then_inc(s["consts_in"], 16)
            act.dma_start(ct[:, :], cols_tail).then_inc(s["consts_in"], 16)
            act.dma_start(w_src[0:TR_, 0:2 * 3 * D].rearrange("p (l f) -> p l f", l=2), wqkv_tail.rearrange("l p f -> p l f")).then_inc(s["wt_in"], 16)
            act.dma_start(w_src[0:TR_, 6 * D:6 * D + HID], w1_tail[:, 0:HID]).then_inc(s["wt_in"], 16)
            act.dma_start(w_src[0:TR_, 6 * D + HID:NW], gate_tail).then_inc(s["wt_in"], 16)
            act.dma_start(b1c[:, :], b1_cols).then_inc(s["misc_in"], 16)
            act.dma_start(gate_m[:, :], gate).then_inc(s["misc_in"], 16)
            act.wait_ge(s["cond_in"], 32)
            act.activation(c_m[:, 1, :], c_m[:, 0, :], ACT.Exp, scale=-1.0).then_inc(s["silu_a"], 1)
            act.activation(c_t[:, 1, :], c_t[:, 0, :], ACT.Exp, scale=-1.0).then_inc(s["silu_a"], 1)

            def norm_part(n):
                for b in range(B):
                    act.wait_ge(s["ln_ve"], 2 * n + b + 1)
                    act.activation(ln4[:, 1, b, :], ln4[:, 0, b, :], ACT.Ln).then_inc(s["ln_log"], 1)
                    act.wait_ge(s["ln_log"], 2 * n + b + 1)
                    act.activation(ln4[:, 2, b, :], ln4[:, 1, b, :], ACT.Exp, scale=-0.5).then_inc(s["ln_y"], 1)
                for b in range(B):
                    if n == 0:
                        act.wait_ge(s["mod_v"], 8)
                    act.wait_ge(s["ln_zt"], 4 * n + 2 * b + 1)
                    act.activation(hT[:, b, :], ps[:, b, :], ACT.Identity,
                                   scale=ab_m[:, n // 2, n % 2, 0, b:b + 1],
                                   bias=ab_m[:, n // 2, n % 2, 1, b:b + 1]).then_inc(s["ln_ht"], 1)

            for l in range(2):
                q = a[l]
                norm_part(2 * l)
                if l == 0:
                    for c in range(C):
                        act.wait_ge(s["qkv_mm"], c + 1)
                        act.activation(qkv[:, c, :], ps[:, 4 + c % 4, 0:3 * D], ACT.Copy).then_inc(s["qkv_ev"], 1)
                for b in range(B):
                    for kq, where in ((0, Q_PART), (1, K_PART)):
                        v4 = qkv[:, b * T:(b + 1) * T, kq * D:kq * D + G4 * HD].rearrange("p t (h d) -> p t h d", h=G4)
                        act.wait_ge(s["qkv_ev"], 8 * l + 4 * b + 4)
                        if l == 0:
                            act.wait_ge(s["wt_v"], 4)
                        for g in where[0][1:]:
                            act.activation(qk[:, kq, b, :, 0:G4, g * HD:(g + 1) * HD], v4, ACT.Copy).then_inc(q["spa"], 1)
                        act.wait_ge(q["spv"], 8 * b + 4 * kq + 2)
                        g = where[1][1]
                        act.activation(qk[:, kq, b, :, 0:G4, g * HD:(g + 1) * HD],
                                       spl[:, kq].rearrange("p t (h d) -> p t h d", h=G4), ACT.Copy).then_inc(q["spa"], 1)

                def half(i, k, peeled):
                    hg, b, pp = pos(i, k)
                    for j in range(T):
                        if has(i, k, peeled):
                            if j == 0 and not (peeled and 4 * i + k < 4):
                                act.wait_ge(q["pv"], 8 * i + 2 * (k - pp) - 4)
                            if l == 0 and peeled and k == 0 and j == 0:
                                act.wait_ge(s["gated"], GATED)
                            act.wait_ge(q["st"], 16 * i + 4 * k + j + 1)
                            act.activation(prob[:, b, 2 * pp:2 * pp + 2, j, :], ps[:, 2 * (j % 2):2 * (j % 2) + 2, :],
                                           ACT.Exp, scale=1.0 / 3.0).then_inc(q["ex"], 1)
                        if j == 1 and has(i, k + 3, peeled):
                            hg3, b3, p3 = pos(i, k + 3)
                            act.wait_ge(q["tk"], 4 * i + k + 4)
                            if l == 0 and peeled and k == -3:
                                act.wait_ge(s["kt_zero"], 2)
                                act.wait_ge(s["wt_v"], 4)
                            for hh in range(2):
                                act.activation(kT[64 * hh:64 * hh + 64, b3, bass.ds(4 * hg3 + 2 * p3 + hh, 1), :],
                                               psb[TRB][64 * hh:64 * hh + 64, 0:S].rearrange("p (a s) -> p a s", a=1),
                                               ACT.Copy).then_inc(q["evk"], 1)
                            act.activation(qT[:, b3, bass.ds(2 * hg3 + p3, 1), :],
                                           psb[TRB][:, S:2 * S].rearrange("p (a s) -> p a s", a=1),
                                           ACT.Copy).then_inc(q["evk"], 1)
                        if j == 2 and k % 2 == 1 and (not peeled or 4 * i + k >= 3):
                            g = 2 * i + (k - 3) // 2
                            act.wait_ge(q["pv"], 4 * g + 4)
                            act.activation(oS[:, :], ps[:, PVB, :], ACT.Copy).then_inc(q["oev"], 1)

                halves(act, half)
                for b in range(B):
                    act.wait_ge(s["o_tr"], 4 * l + 2 * b + 1)
                    act.activation(oT[:, b, :], ps[:, b, :], ACT.Copy).then_inc(s["oT_ev"], 1)
                norm_part(2 * l + 1)
                if l == 0:
                    for n in range(B * NM0):
                        b, m = divmod(n, NM0)
                        r = P if m < NM0 - 1 else HID - P * (NM0 - 1)
                        act.wait_ge(s["fc1_mm"], n + 1)
                        if n == 0:
                            act.wait_ge(s["misc_in"], 32)
                        act.activation(hm0[0:r, b, m, :], ps[0:r, 4 + n % 4, :], ACT.Gelu, bias=b1c[0:r, m:m + 1]).then_inc(s["gelu"], 1)
                else:
                    act.wait_ge(s["route"], 2)
                    act.activation(lw[:, :, :], lw[:, :, :], ACT.Exp).then_inc(s["route"], 1)
                    for n in range(B * NM1):
                        b, m = divmod(n, NM1)
                        act.wait_ge(s["fc1_mm"], B * NM0 + n + 1)
                        act.activation(hm1[b][:, m, :], ps[:, 4 + n % 4, :], ACT.Gelu_apprx_tanh,
                                       bias=b1c[:, NM0 + m:NM0 + m + 1]).then_inc(s["gelu"], 1)

        @block.vector
        def _(v):
            def parts_of_weights(src, ta, tb, tc, dst, name, at):
                v.tensor_copy(ta, src).then_inc(s[name], 1)
                v.wait_ge(s[name], at + 1)
                v.scalar_tensor_tensor(tb, ta, ct[:, 14:15], src, ALU.mult, ALU.add).then_inc(s[name], 1)
                v.wait_ge(s[name], at + 2)
                v.tensor_copy(tc, tb).then_inc(s[name], 1)
                v.wait_ge(s[name], at + 3)
                v.scalar_tensor_tensor(dst, tc, ct[:, 15:16], tb, ALU.mult, ALU.add).then_inc(s[name], 1)

            v.wait_ge(s["silu_a"], 2)
            v.tensor_scalar(c_m[:, 2, :], c_m[:, 1, :], 1.0, None, ALU.add).then_inc(s["silu_v"], 1)
            v.tensor_scalar(c_t[:, 2, :], c_t[:, 1, :], 1.0, None, ALU.add).then_inc(s["silu_v"], 1)
            v.wait_ge(s["silu_v"], 2)
            v.reciprocal(c_m[:, 3, :], c_m[:, 2, :]).then_inc(s["silu_v"], 1)
            v.reciprocal(c_t[:, 3, :], c_t[:, 2, :]).then_inc(s["silu_v"], 1)
            v.wait_ge(s["silu_v"], 4)
            v.tensor_tensor(c_m[:, 4, :], c_m[:, 0, :], c_m[:, 3, :], ALU.mult).then_inc(s["silu_v"], 1)
            v.tensor_tensor(c_t[:, 4, :], c_t[:, 0, :], c_t[:, 3, :], ALU.mult).then_inc(s["silu_v"], 1)

            def stats(n):
                for b in range(B):
                    for t in range(T):
                        if n == 0:
                            v.wait_ge(s[f"x_in{b}"], 16)
                        else:
                            v.wait_ge(s["x_new"], 8 * (n - 1) + b * T + t + 1)
                        v.bn_stats(st6[:, b, t, :], X[:, b * T + t, :]).then_inc(s["ln_stats"], 1)
                    for t in range(T):
                        v.wait_ge(s["ln_stats"], 8 * n + 4 * b + t + 1)
                        v.bn_aggr(mv[:, b, t, :], st6[:, b, t, :]).then_inc(s["ln_aggr"], 1)
                    v.wait_ge(s["ln_aggr"], 8 * n + 4 * b + 4)
                    v.tensor_scalar(ln4[:, 0, b, :], mv[:, b, :, 1], EPS[n // 2], None, ALU.add).then_inc(s["ln_ve"], 1)

            def normalise(n):
                for b in range(B):
                    v.wait_ge(s["ln_y"], 2 * n + b + 1)
                    at = 8 * n + 4 * b
                    v.tensor_tensor(ln4[:, 3, b, :], ln4[:, 2, b, :], ln4[:, 2, b, :], ALU.mult).then_inc(s["ln_newton"], 1)
                    v.wait_ge(s["ln_newton"], at + 1)
                    v.tensor_tensor(ln4[:, 4, b, :], ln4[:, 3, b, :], ln4[:, 0, b, :], ALU.mult).then_inc(s["ln_newton"], 1)
                    v.wait_ge(s["ln_newton"], at + 2)
                    v.tensor_scalar(ln4[:, 3, b, :], ln4[:, 4, b, :], -0.5, 1.5, ALU.mult, ALU.add).then_inc(s["ln_newton"], 1)
                    v.wait_ge(s["ln_newton"], at + 3)
                    v.tensor_tensor(ln4[:, 5, b, :], ln4[:, 3, b, :], ln4[:, 2, b, :], ALU.mult).then_inc(s["ln_newton"], 1)
                    v.wait_ge(s["ln_newton"], at + 4)
                    for t in range(T):
                        c = b * T + t
                        v.tensor_scalar(z[:, b, t, 0:P], X[:, c, 0:P], mv[:, b, t, 0:1], ln4[:, 5, b, t:t + 1],
                                        ALU.subtract, ALU.mult).then_inc(s["ln_z"], 1)
                        v.tensor_scalar(z[:, b, t, P:P + TR_].rearrange("p (g d) -> p g d", g=NPART),
                                        X[:, c, P:D].rearrange("p (g d) -> p g d", g=1).to_broadcast([P, NPART, DT]),
                                        mv[:, b, t, 0:1], ln4[:, 5, b, t:t + 1],
                                        ALU.subtract, ALU.mult).then_inc(s["ln_z"], 1)

            def tails(n):
                for b in range(B):
                    at = 10 * n + 5 * b
                    v.wait_ge(s["ln_zt"], 4 * n + 2 * b + 2)
                    v.tensor_scalar(t_h[0:TR_, b, :], ps[0:TR_, 2 + b, :], ab_t[:, n // 2, n % 2, 0, b:b + 1],
                                    ab_t[:, n // 2, n % 2, 1, b:b + 1], ALU.mult, ALU.add).then_inc(s["ln_r"], 1)
                    v.wait_ge(s["ln_r"], at + 1)
                    v.tensor_copy(t_a[0:TR_, b, :], t_h[0:TR_, b, :]).then_inc(s["ln_r"], 1)
                    v.wait_ge(s["ln_r"], at + 2)
                    v.scalar_tensor_tensor(t_b[0:TR_, b, :], t_a[0:TR_, b, :], ct[:, 12:13], t_h[0:TR_, b, :],
                                           ALU.mult, ALU.add).then_inc(s["ln_r"], 1)
                    v.wait_ge(s["ln_r"], at + 3)
                    v.tensor_copy(t_c[0:TR_, b, :], t_b[0:TR_, b, :]).then_inc(s["ln_r"], 1)
                    v.wait_ge(s["ln_r"], at + 4)
                    v.scalar_tensor_tensor(hR[0:TR_, b, :], t_c[0:TR_, b, :], ct[:, 13:14], t_b[0:TR_, b, :],
                                           ALU.mult, ALU.add).then_inc(s["ln_r"], 1)

            def modulation():
                v.wait_ge(s["mod_mm"], 1)
                v.wait_ge(s["consts_in"], 48)
                for d, bias, n, r in ((mod_m, cm, 0, P), (mod_t, ct, 16, TR_)):
                    v.tensor_tensor(d[:, :, :, :].rearrange("p l s b -> p (l s) b"),
                                    ps[0:r, 4, n:n + 16].rearrange("p (g b) -> p g b", b=B),
                                    bias[:, 0:8].rearrange("p (g b) -> p g b", b=1).to_broadcast([r, 8, B]),
                                    ALU.add).then_inc(s["mod_v"], 1)
                v.wait_ge(s["mod_v"], 2)
                for d, sc in ((mod_m, sc1_m), (mod_t, sc1_t)):
                    v.tensor_scalar(sc[:, :, :, :].rearrange("p l n b -> p (l n) b"),
                                    d[:, :, :, :].rearrange("p l (n two) b -> p (l n) two b", two=2)[:, :, 1, :],
                                    1.0, None, ALU.add).then_inc(s["mod_v"], 1)
                v.wait_ge(s["mod_v"], 4)
                for d, sc, ab, col in ((mod_m, sc1_m, ab_m, cm), (mod_t, sc1_t, ab_t, ct)):
                    for n in range(2):
                        v.tensor_scalar(ab[:, 0, n, 0, :], sc[:, 0, n, :], col[:, 8 + 2 * n:9 + 2 * n], None,
                                        ALU.mult).then_inc(s["mod_v"], 1)
                        v.scalar_tensor_tensor(ab[:, 0, n, 1, :], sc[:, 0, n, :], col[:, 9 + 2 * n:10 + 2 * n],
                                               d[:, 0, 2 * n, :], ALU.mult, ALU.add).then_inc(s["mod_v"], 1)
                        v.tensor_copy(ab[:, 1, n, 0, :], sc[:, 1, n, :]).then_inc(s["mod_v"], 1)
                        v.tensor_copy(ab[:, 1, n, 1, :], d[:, 1, 2 * n, :]).then_inc(s["mod_v"], 1)

            MODV = 4 + 16
            stats(0)
            v.wait_ge(s["silu_v"], 6)
            v.tensor_copy(cb_m, c_m[:, 4, :].rearrange("p (b o) -> p b o", o=1).to_broadcast([P, B, P])).then_inc(s["cb_v"], 1)
            v.tensor_copy(cb_t[0:DT], c_t[:, 4, :].rearrange("p (b o) -> p b o", o=1).to_broadcast([DT, B, P])).then_inc(s["cb_v"], 1)
            v.wait_ge(s["consts_in"], 48)
            v.tensor_copy(idb[:, :], idf[:, :]).then_inc(s["id_b"], 1)
            normalise(0)
            modulation()
            v.wait_ge(s["wt_in"], 48)
            parts_of_weights(w_src[0:TR_], w_a[0:TR_], w_b[0:TR_], w_c[0:TR_], w_tail[0:TR_, :], "wt_v", 0)
            v.wait_ge(s["wt_v"], 4)
            v.memset(qk.rearrange("p k b t h c -> p (k b t h) c")[:, :, MXC:PW], 0.0).then_inc(s["qk_pad"], 1)
            v.wait_ge(s["qk_pad"], 1)
            v.memset(qk[:, 1].rearrange("p b t h c -> p (b t h) c")[:, :, MXC:MXC + 3], 1.0).then_inc(s["qk_pad"], 1)
            v.wait_ge(s["mod_v"], MODV)

            for l in range(2):
                q = a[l]
                if l == 1:
                    stats(2)
                    normalise(2)
                tails(2 * l)
                if l == 0:
                    for g in range(4):
                        v.wait_ge(s["gate_mm"], g + 1)
                        v.wait_ge(s["rows_in"], 32)
                        v.tensor_tensor(gates[:, g, :, :], ps[:, g, 0:B * D].rearrange("p (b d) -> p b d", b=B),
                                        rows_s[:, g * D:(g + 1) * D].rearrange("p (o d) -> p o d", o=1).to_broadcast([P, B, D]),
                                        ALU.add).then_inc(s["gates_v"], 1)
                if l == 1:
                    v.memset(qk[:, 0].rearrange("p b t h c -> p (b t h) c")[:, :, MXC:MXC + 3], 0.0).then_inc(q["qz"], 1)
                    for c in range(C):
                        v.wait_ge(s["qkv_mm"], 8 + c + 1)
                        if c == 0:
                            v.wait_ge(s["rows_in"], 32)
                        v.tensor_tensor(qkv[:, c, :], ps[:, 4 + c % 4, 0:3 * D], bqkv_row[:, :], ALU.add).then_inc(s["qkv_ev"], 1)
                for b in range(B):
                    v.wait_ge(s["qkv_ev"], 8 * l + 4 * b + 4)
                    for kq, where in ((0, Q_PART), (1, K_PART)):
                        at = 8 * b + 4 * kq
                        v4 = qkv[:, b * T:(b + 1) * T, kq * D:kq * D + G4 * HD].rearrange("p t (h d) -> p t h d", h=G4)
                        r4 = spl[:, kq].rearrange("p t (h d) -> p t h d", h=G4)

                        def put(g):
                            return qk[:, kq, b, :, 0:G4, g * HD:(g + 1) * HD]
                        v.tensor_copy(put(where[0][0]), v4).then_inc(q["spv"], 1)
                        v.wait_ge(q["spv"], at + 1)
                        if b == 1:
                            v.wait_ge(q["spa"], 3 * (kq + 1))
                        v.tensor_tensor(r4, v4, put(where[0][0]), ALU.subtract).then_inc(q["spv"], 1)
                        v.wait_ge(q["spv"], at + 2)
                        v.tensor_copy(put(where[1][0]), r4).then_inc(q["spv"], 1)
                        v.wait_ge(q["spv"], at + 3)
                        v.tensor_tensor(put(where[2][0]), r4, put(where[1][0]), ALU.subtract).then_inc(q["spv"], 1)

                def half(i, k, peeled):
                    n4 = 4 * i + k
                    hg1, b1, p1 = pos(i, k + 1)
                    qm = qk[:, 0, b1, :, bass.ds(4 * hg1 + 2 * p1, 2), :]
                    m1 = mx[:, (k + 1) % 2]
                    do_q = has(i, k + 1, peeled)
                    for n in range(8):
                        if has(i, k + 2, peeled):
                            v.wait_ge(q["sm"], 32 * i + 8 * (k + 2) + n + 1)
                            v.reduce_max(mx[:, k % 2, n // 2, n % 2:n % 2 + 1], ps[:, 4 + n % 2, :], AX.X).then_inc(q["mx"], 1)
                        at = 16 * i + 4 * (k + 1)
                        if do_q and n == 0:
                            v.wait_ge(q["mx"], 32 * i + 8 * (k + 1) + 8)
                            v.tensor_scalar(qm[:, :, :, MXC], m1, -1.0, None, ALU.mult).then_inc(q["nstep"], 1)
                        if do_q and n == 1:
                            v.wait_ge(q["nstep"], at + 1)
                            v.scalar_tensor_tensor(nmx[:, :, :], m1, -1.0, qm[:, :, :, MXC], ALU.mult, ALU.subtract).then_inc(q["nstep"], 1)
                        if do_q and n == 2:
                            v.wait_ge(q["nstep"], at + 2)
                            v.tensor_copy(qm[:, :, :, MXC + 1], nmx[:, :, :]).then_inc(q["nstep"], 1)
                        if do_q and n == 3:
                            v.wait_ge(q["nstep"], at + 3)
                            v.tensor_tensor(qm[:, :, :, MXC + 2], nmx[:, :, :], qm[:, :, :, MXC + 1], ALU.subtract).then_inc(q["nstep"], 1)
                        if do_q and n == 5:
                            v.wait_ge(q["tq"], n4 + 2)
                            v.tensor_copy(qT[:, b1, bass.ds(2 * hg1 + p1, 1), :],
                                          psb[TRB][:, 0:S].rearrange("p (a s) -> p a s", a=1)).then_inc(q["evq"], 1)
                        if k % 2 == 0 and (not peeled or n4 >= 4):
                            hgo, bo, _ = pos(i, k - 4)
                            g = 2 * i + (k - 4) // 2
                            pv = ps[:, PVB, :].rearrange("p (t h c) -> p t h c", t=T, h=G4)
                            if n == 1:
                                v.wait_ge(q["ot"], g + 1)
                                v.reciprocal(rc[:, :, :], pv[:, :, :, 0]).then_inc(q["on"], 1)
                            if n == 3:
                                v.wait_ge(q["on"], 2 * g + 1)
                                v.tensor_tensor(o_tok[:, bo * T:(bo + 1) * T, bass.ds(hgo * (G4 * HD), G4 * HD)].rearrange("p t (h d) -> p t h d", h=G4),
                                                pv[:, :, :, 1:1 + HD],
                                                rc[:, :, :].rearrange("p t (h o) -> p t h o", o=1).to_broadcast([P, T, G4, HD]),
                                                ALU.mult).then_inc(q["on"], 1)

                halves(v, half)
                half(0, NPAIR + 2, True)
                for b in range(B):
                    v.wait_ge(s["o_tr"], 4 * l + 2 * b + 2)
                    v.tensor_copy(oTt[0:DT, b, :], ps[0:DT, 2 + b, :]).then_inc(s["oTt_ev"], 1)
                for c in range(C):
                    v.wait_ge(s["proj_mm"], 8 * l + c + 1)
                    v.wait_ge(s["xb"], 16 * l + c + 1)
                    v.tensor_tensor(X[:, c, :], ps[:, 4 + c % 4, 0:D], X[:, c, :], ALU.add).then_inc(s["x_new"], 1)
                stats(2 * l + 1)
                normalise(2 * l + 1)
                tails(2 * l + 1)
                if l == 0:
                    v.wait_ge(s["et_in"], 16)
                    for e in range(E):
                        cs = slice(e * HID, (e + 1) * HID)
                        parts_of_weights(e_src[0:TR_, cs], e_a[0:TR_], e_b[0:TR_], e_c[0:TR_], we_tail[0:TR_, cs], "et_v", 4 * e)
                        v.wait_ge(s["et_v"], 4 * e + 4)
                    for c in range(C):
                        v.wait_ge(s["fc2_mm"], c + 1)
                        v.wait_ge(s["xb"], 8 + c + 1)
                        v.tensor_tensor(X[:, c, :], ps[:, c % 4, 0:D], X[:, c, :], ALU.add).then_inc(s["x_new"], 1)

            v.memset(below[:, :, :], 0.0).then_inc(s["bias2"], 1)
            for e in range(1, E):
                v.wait_ge(s["bias2"], e)
                v.memset(below[:, e, 0:e], 1.0).then_inc(s["bias2"], 1)
            v.wait_ge(s["lg_mm"], 1)
            v.tensor_copy(lg[:, :, :], ps[:, 0, 0:C * E].rearrange("p (c e) -> p c e", c=C)).then_inc(s["route"], 1)
            v.wait_ge(s["route"], 1)
            v.reduce_max(sm[:, 0, :], lg[:, :, :], AX.X).then_inc(s["moe_acc"], 1)
            v.wait_ge(s["moe_acc"], 1)
            v.tensor_tensor(lw[:, :, :], lg[:, :, :], sm[:, 0, :].rearrange("p (c o) -> p c o", o=1).to_broadcast([P, C, E]),
                            ALU.subtract).then_inc(s["route"], 1)
            r = 1

            def chain(ins):
                nonlocal r
                ins.then_inc(s["moe_acc"], 1)
                r += 1
                v.wait_ge(s["moe_acc"], r)
            v.wait_ge(s["bias2"], E)
            for e in range(E):
                other = lg[:, :, :]
                own = lg[:, :, e:e + 1].to_broadcast([P, C, E])
                chain(v.tensor_tensor(big[:, 0, :, e, :], other, own, ALU.is_gt))
                chain(v.tensor_tensor(big[:, 1, :, e, :], other, own, ALU.is_equal))
                chain(v.tensor_tensor(big[:, 1, :, e, :], big[:, 1, :, e, :],
                                      below[:, e:e + 1, :].to_broadcast([P, C, E]), ALU.mult))
            chain(v.tensor_tensor(big[:, 2, :, :, :], big[:, 0, :, :, :], big[:, 1, :, :, :], ALU.add))
            chain(v.reduce_sum(cw[:, :, :], big[:, 2, :, :, :], AX.X))
            chain(v.tensor_scalar(cw[:, :, :], cw[:, :, :], 2.0, None, ALU.is_lt))
            v.wait_ge(s["route"], 3)
            chain(v.tensor_tensor(cw[:, :, :], cw[:, :, :], lw[:, :, :], ALU.mult))
            chain(v.reduce_sum(sm[:, 1, :], cw[:, :, :], AX.X))
            chain(v.reciprocal(sm[:, 2, :], sm[:, 1, :]))
            chain(v.tensor_tensor(cw[:, :, :], cw[:, :, :], sm[:, 2, :].rearrange("p (c o) -> p c o", o=1).to_broadcast([P, C, E]), ALU.mult))
            v.wait_ge(s["we_in"], 48)
            for e in range(E):
                for c in range(C):
                    if e == 0:
                        v.tensor_scalar(acc[:, c, :], b2_row[:, 0, :], cw[:, c, 0:1], None, ALU.mult).then_inc(s["bias2"], 1)
                    else:
                        v.wait_ge(s["bias2"], E + (e - 1) * C + c + 1)
                        v.scalar_tensor_tensor(acc[:, c, :], b2_row[:, e, :], cw[:, c, e:e + 1], acc[:, c, :],
                                               ALU.mult, ALU.add).then_inc(s["bias2"], 1)
            for c in range(C):
                v.wait_ge(s["bias2"], E + (E - 1) * C + c + 1)
                for e in range(E):
                    n = c * E + e
                    v.wait_ge(s["moe_mm"], n + 1)
                    if e:
                        v.wait_ge(s["moe_acc"], r + n)
                    v.scalar_tensor_tensor(acc[:, c, :], ps[:, e, 0:D],
                                           cw[:, c, e:e + 1], acc[:, c, :], ALU.mult, ALU.add).then_inc(s["moe_acc"], 1)
                v.wait_ge(s["moe_acc"], r + (c + 1) * E)
                v.tensor_tensor(acc[:, c, :], acc[:, c, :], g_last[:, c // T, :], ALU.mult).then_inc(s["fin"], 1)
                v.wait_ge(s["fin"], 2 * c + 1)
                v.tensor_tensor(X[:, c, :], acc[:, c, :], X[:, c, :], ALU.add).then_inc(s["fin"], 1)

        @block.tensor
        def _(pe):
            mm = nc.tensor.matmul
            pe.wait_ge(s["ada_in"], 32)
            pe.wait_ge(s["silu_v"], 6)
            for l in range(2):
                for n, sec in enumerate(SECT):
                    at = (4 * l + n) * B
                    cs = slice(sec * D, sec * D + P)
                    mm(ps[:, 4, at:at + B], ada_m[:, l, cs], c_m[:, 4, :], start=True, stop=False)
                    last = mm(ps[:, 4, at:at + B], ada_t[0:DT, l, cs], c_t[:, 4, :], start=False, stop=True)
                for n in range(len(SECT)):
                    at = 16 + (4 * l + n) * B
                    cs = slice(6 * D + n * TR_, 6 * D + (n + 1) * TR_)
                    mm(ps[0:TR_, 4, at:at + B], ada_m[:, l, cs], c_m[:, 4, :], start=True, stop=False)
                    last = mm(ps[0:TR_, 4, at:at + B], ada_t[0:DT, l, cs], c_t[:, 4, :], start=False, stop=True)
            last.then_inc(s["mod_mm"], 1)

            def transpose_z(n):
                for b in range(B):
                    pe.wait_ge(s["ln_z"], 16 * n + 8 * b + 8)
                    if n == 0:
                        pe.wait_ge(s["consts_in"], 48)
                    for t in range(T):
                        last = pe.transpose(ps[:, b, t * P:(t + 1) * P], z[:, b, t, 0:P], idf[:, :])
                    last.then_inc(s["ln_zt"], 1)
                    for t in range(T):
                        last = pe.transpose(ps[0:TR_, 2 + b, t * P:(t + 1) * P], z[:, b, t, P:P + TR_], idf[:, :])
                    last.then_inc(s["ln_zt"], 1)

            def normed(n, b):
                pe.wait_ge(s["ln_ht"], 2 * n + b + 1)
                pe.wait_ge(s["ln_r"], 5 * (2 * n + b + 1))

            for l in range(2):
                q = a[l]
                transpose_z(2 * l)
                if l == 0:
                    pe.wait_ge(s["wq_in"], 16)
                    pe.wait_ge(s["wt_v"], 4)
                    pe.wait_ge(s["mod_v"], 2)
                for c in range(C):
                    b, t = divmod(c, T)
                    normed(2 * l, b)
                    if c >= 4:
                        pe.wait_ge(s["qkv_ev"], 8 * l + c - 3)
                    mm(ps[:, 4 + c % 4, 0:3 * D], hT[:, b, t * P:(t + 1) * P], wq_m[:, l, :], start=True, stop=False)
                    mm(ps[:, 4 + c % 4, 0:3 * D], hR[0:TR_, b, t * P:(t + 1) * P],
                       w_tail[0:TR_, 3 * D * l:3 * D * (l + 1)], start=False, stop=True).then_inc(s["qkv_mm"], 1)
                if l == 0:
                    pe.wait_ge(s["cb_v"], 2)
                    for g in range(4):
                        cs = slice((2 + 3 * (g % 2)) * D, (3 + 3 * (g % 2)) * D)
                        for b in range(B):
                            mm(ps[:, g, b * D:(b + 1) * D], cb_m[:, b, :], ada_m[:, g // 2, cs], start=True, stop=False)
                            last = mm(ps[:, g, b * D:(b + 1) * D], cb_t[0:DT, b, :], ada_t[0:DT, g // 2, cs], start=False, stop=True)
                        last.then_inc(s["gate_mm"], 1)

                def ready_kq(i, k, peeled):
                    n3 = 4 * i + k + 3
                    if not has(i, k + 3, peeled):
                        return
                    if not (peeled and n3 == 0):
                        pe.wait_ge(q["evk"], 12 * i + 3 * (k + 3))
                    if not (peeled and n3 < 3):
                        pe.wait_ge(q["evq"], 4 * i + k + 1)
                    if peeled and n3 < 4:
                        b3 = n3 // 2
                        pe.wait_ge(q["spv"], 8 * b3 + 8)
                        pe.wait_ge(q["spa"], 6 * b3 + 6)
                        if l == 1:
                            pe.wait_ge(q["qz"], 1)
                        else:
                            pe.wait_ge(s["qk_pad"], 2)
                        pe.wait_ge(s["qkv_ev"], 8 * l + 8)
                        pe.wait_ge(s["id_b"], 1)
                    else:
                        pe.wait_ge(q["spp"], 14 * (2 * i + (k + 3) // 2 - 1))

                def ready_max(i, k, peeled):
                    if not has(i, k + 1, peeled):
                        return
                    pe.wait_ge(q["nstep"], 16 * i + 4 * (k + 1) + 4)
                    pe.wait_ge(q["evk"], min(12 * i + 3 * (k + 4), 3 * NPAIR) if peeled else 12 * i + 3 * (k + 4))

                def half(i, k, peeled):
                    n4 = 4 * i + k
                    hg, b, pp = pos(i, k)
                    hg1, b1, p1 = pos(i, k + 1)
                    hg2, b2, p2 = pos(i, k + 2)
                    hg3, b3, p3 = pos(i, k + 3)
                    odd = k % 2 == 1
                    for j in range(T):
                        if has(i, k, peeled):
                            if j == 0:
                                pe.wait_ge(q["evq"], n4 + 1)
                                if l == 0 and peeled and k == 0:
                                    pe.wait_ge(s["gates_v"], 4)
                            if not (peeled and n4 == 0 and j < 2):
                                pe.wait_ge(q["ex"], 16 * i + 4 * k + j - 1)
                            for hh in range(2):
                                last = mm(ps[:, 2 * (j % 2) + hh, :],
                                          kT[:, b, bass.ds(4 * hg + 2 * pp + hh, 1), j * P:(j + 1) * P],
                                          qT[:, b, bass.ds(2 * hg + pp, 1), :], start=True, stop=True)
                            last.then_inc(q["st"], 1)
                        if has(i, k + 2, peeled):
                            if j == 0:
                                pe.wait_ge(q["evk"], 12 * i + 3 * (k + 3))
                            for hh in range(2):
                                n = 2 * j + hh
                                if not (peeled and n4 == -2 and n < 2):
                                    pe.wait_ge(q["mx"], 32 * i + 8 * (k + 2) + n - 1)
                                if hh == 1 and j == 0:
                                    ready_kq(i, k, peeled)
                                if hh == 1 and j == 2:
                                    ready_max(i, k, peeled)
                                mm(ps[:, 4 + hh, :], qT[:, b2, bass.ds(2 * hg2 + p2, 1), j * P:(j + 1) * P],
                                   kT[:, b2, bass.ds(4 * hg2 + 2 * p2 + hh, 1), :], start=True, stop=True).then_inc(q["sm"], 1)
                        if j == 0 and has(i, k + 3, peeled):
                            if not has(i, k + 2, peeled):
                                ready_kq(i, k, peeled)
                            for w, kq in ((0, 1), (1, 0)):
                                for t in range(T):
                                    last = pe.transpose(psb[TRB][:, w * S + t * P:w * S + (t + 1) * P],
                                                        qk[:, kq, b3, t, bass.ds(4 * hg3 + 2 * p3, 2), :], idb[:, :])
                            last.then_inc(q["tk"], 1)
                        if j == 2 and has(i, k + 1, peeled):
                            if not has(i, k + 2, peeled):
                                ready_max(i, k, peeled)
                            for t in range(T):
                                last = pe.transpose(psb[TRB][:, t * P:(t + 1) * P],
                                                    qk[:, 0, b1, t, bass.ds(4 * hg1 + 2 * p1, 2), :], idb[:, :])
                            last.then_inc(q["tq"], 1)
                        if (j < 2) == odd and (not peeled or n4 >= 2 + odd):
                            g = 2 * i + (k - 2 - odd) // 2
                            u = ((k - 2 - odd) // 2) % 2
                            c = j + 2 if odd else j - 2
                            if c == 0:
                                pe.wait_ge(q["vs"], g + 1)
                                if not (peeled and n4 == 2):
                                    pe.wait_ge(q["on"], 2 * g)
                            pe.wait_ge(q["ex"], 8 * g + 5 + c)
                            if c == 0 and l == 0:
                                pe.wait_ge(s["vs_pad"], 2)
                            for h in range(G4):
                                last = mm(ps[32 * h:32 * h + 32, PVB, :], vS[:, u, c, h, :], prob[:, u, h, c, :],
                                          start=(c == 0), stop=(c == T - 1), tile_position=(0, 32 * h))
                            last.then_inc(q["pv"], 1)
                        if j == 3 and odd and (not peeled or n4 >= 3):
                            g = 2 * i + (k - 3) // 2
                            pe.wait_ge(q["oev"], g + 1)
                            for t in range(T):
                                last = pe.transpose(ps[:, PVB, t * P:(t + 1) * P], oS[:, t * P:(t + 1) * P], idf[:, :])
                            last.then_inc(q["ot"], 1)

                halves(pe, half)
                pe.wait_ge(q["on"], 16)
                for b in range(B):
                    for t in range(T):
                        last = pe.transpose(ps[:, b, t * P:(t + 1) * P], o_tok[:, b * T + t, 0:P], idf[:, :])
                    last.then_inc(s["o_tr"], 1)
                    for t in range(T):
                        last = pe.transpose(ps[0:DT, 2 + b, t * P:(t + 1) * P], o_tok[:, b * T + t, P:D], idf[:, :])
                    last.then_inc(s["o_tr"], 1)
                pe.wait_ge(s["gated"], 8)
                for c in range(C):
                    b, t = divmod(c, T)
                    pe.wait_ge(s["oT_ev"], 2 * l + b + 1)
                    pe.wait_ge(s["oTt_ev"], 2 * l + b + 1)
                    if c >= 4:
                        pe.wait_ge(s["x_new"], 16 * l + c - 3)
                    mm(ps[:, 4 + c % 4, 0:D], oT[:, b, t * P:(t + 1) * P], wog_m[:, l, b, :], start=True, stop=False)
                    mm(ps[:, 4 + c % 4, 0:D], oTt[0:DT, b, t * P:(t + 1) * P], wog_t[:, l, b, :],
                       start=False, stop=True).then_inc(s["proj_mm"], 1)
                transpose_z(2 * l + 1)

                if l == 0:
                    pe.wait_ge(s["w1d_in"], 16)
                    for n in range(B * NM0):
                        b, m = divmod(n, NM0)
                        r = P if m < NM0 - 1 else HID - P * (NM0 - 1)
                        normed(1, b)
                        pe.wait_ge(s["x_new"], 8)
                        if n >= 4:
                            pe.wait_ge(s["gelu"], n - 3)
                        mm(ps[0:r, 4 + n % 4, :], w1d[:, m * P:m * P + r], hT[:, b, :], start=True, stop=False)
                        mm(ps[0:r, 4 + n % 4, :], w_tail[0:TR_, 6 * D + m * P:6 * D + m * P + r], hR[0:TR_, b, :],
                           start=False, stop=True).then_inc(s["fc1_mm"], 1)
                    pe.wait_ge(s["gated"], 8 + 6 + 2 * NM0)
                    for c in range(C):
                        b, t = divmod(c, T)
                        pe.wait_ge(s["gelu"], NM0 * (b + 1))
                        if c >= 4:
                            pe.wait_ge(s["x_new"], 8 + c - 3)
                        for m in range(NM0):
                            r = P if m < NM0 - 1 else HID - P * (NM0 - 1)
                            last = mm(ps[:, c % 4, 0:D], hm0[0:r, b, m, t * P:(t + 1) * P], w2g[0:r, m, b, :],
                                      start=(m == 0), stop=(m == NM0 - 1))
                        last.then_inc(s["fc2_mm"], 1)
                else:
                    pe.wait_ge(s["misc_in"], 32)
                    for c in range(C):
                        b, t = divmod(c, T)
                        normed(3, b)
                        normed(3, 1)
                        mm(ps[:, 0, c * E:(c + 1) * E], hT[:, b, t * P:(t + 1) * P], gate_m[:, :], start=True, stop=False)
                        last = mm(ps[:, 0, c * E:(c + 1) * E], hR[0:TR_, b, t * P:(t + 1) * P],
                                  w_tail[0:TR_, 6 * D + HID:NW], start=False, stop=True)
                    last.then_inc(s["lg_mm"], 1)
                    pe.wait_ge(s["we_in"], 48)
                    pe.wait_ge(s["et_v"], 4 * E)
                    pe.wait_ge(s["x_new"], 24)

                    def up(b):
                        for m in range(NM1):
                            n = b * NM1 + m
                            if n >= 4:
                                pe.wait_ge(s["gelu"], B * NM0 + n - 3)
                            mm(ps[:, 4 + n % 4, :], w1e[:, m * P:(m + 1) * P], hT[:, b, :], start=True, stop=False)
                            mm(ps[:, 4 + n % 4, :], we_tail[0:TR_, m * P:(m + 1) * P], hR[0:TR_, b, :],
                               start=False, stop=True).then_inc(s["fc1_mm"], 1)

                    def down(b):
                        for c in range(b * T, (b + 1) * T):
                            t = c % T
                            for e in range(E):
                                if c >= 1:
                                    pe.wait_ge(s["moe_acc"], ROUTE + (c - 1) * E + e + 1)
                                else:
                                    pe.wait_ge(s["route"], 1)
                                lo, hi = e * HID, (e + 1) * HID
                                while lo < hi:
                                    m, r0 = divmod(lo, P)
                                    r1 = min(P, r0 + hi - lo)
                                    pe.wait_ge(s["gelu"], B * NM0 + b * NM1 + m + 1)
                                    last = mm(ps[:, e, 0:D],
                                              hm1[b][r0:r1, m, t * P:(t + 1) * P], w2e[r0:r1, m, :],
                                              start=(lo == e * HID), stop=(lo + r1 - r0 == hi))
                                    lo += r1 - r0
                                last.then_inc(s["moe_mm"], 1)
                    up(0)
                    down(0)
                    up(1)
                    down(1)


GATED = 8 + 6 + 2 * NM0 + 1
ROUTE = 1 + 3 * E + 7


_INS = ["x", "cond_t", "ident", "cols_main", "cols_tail", "ada", "rows", "wqkv", "wqkv_tail", "wo",
        "w1", "w1_tail", "gate", "gate_tail", "w2", "b1_cols"]


def _lay_out(i):
    import numpy as np
    f = {k: np.asarray(v) for k, v in i.items()}
    L0, L1 = "L0_cond_", "L1_cond_"

    def tail(w):
        return np.tile(w[P:D], (NPART, 1))

    def columns(vs):
        w = np.stack(vs, axis=1)
        return w[0:P], tail(w)

    ada_b = [f[L0 + "ada_b"], f[L1 + "b_adaln"]]
    vs = [v[sec * D:(sec + 1) * D] for v in ada_b for sec in SECT]
    vs += [f[L0 + n] for n in ("ln1_w", "ln1_b", "ln2_w", "ln2_b")]
    main, tails = columns(vs)
    part = np.repeat(np.arange(NPART), DT)
    x_of, w_of = np.zeros(NPART, int), np.zeros(NPART, int)
    for n in range(3):
        x_of[list(Q_PART[n])] = n
        w_of[list(K_PART[n])] = n
    pick = np.stack([-(k[part] >= n).astype(np.float32) for k in (x_of, w_of) for n in (1, 2)], axis=1)
    wq0 = np.concatenate([f[L0 + n] for n in ("wq", "wk", "wv")], axis=1)
    wqkv = [wq0, f[L1 + "w_qkv"]]
    w1 = np.concatenate([f[L0 + "fc1_w"], f[L1 + "w1"].transpose(1, 0, 2).reshape(D, E * HID)], axis=1)
    b1 = np.concatenate([f[L0 + "fc1_b"], np.zeros(NM0 * P - HID, np.float32), f[L1 + "b1"].reshape(-1)])
    rows = np.concatenate([ada_b[0][2 * D:3 * D], ada_b[0][5 * D:6 * D], ada_b[1][2 * D:3 * D], ada_b[1][5 * D:6 * D],
                           f[L0 + "wo_b"], f[L1 + "b_proj"], f[L0 + "fc2_b"], f[L1 + "b2"].reshape(-1),
                           f[L1 + "b_qkv"]])[None]
    ada = [np.concatenate([w] + [np.tile(w[:, sec * D + P:(sec + 1) * D], (1, NPART)) for sec in SECT], axis=1)
           for w in (f[L0 + "ada_w"], f[L1 + "w_adaln"])]
    return {
        "x": f["x"].reshape(B * S, D), "cond_t": f["cond_1152"].T, "ident": np.eye(P, dtype=np.float32),
        "cols_main": main, "cols_tail": np.concatenate([tails, pick], axis=1),
        "ada": np.stack(ada), "rows": rows,
        "wqkv": np.stack([w[0:P] for w in wqkv]), "wqkv_tail": np.stack([tail(w) for w in wqkv]),
        "wo": np.stack([f[L0 + "wo"], f[L1 + "w_proj"]]), "w1": w1, "w1_tail": tail(w1),
        "gate": f[L1 + "w_gate"][0:P], "gate_tail": tail(f[L1 + "w_gate"]),
        "w2": np.concatenate([f[L0 + "fc2_w"], f[L1 + "w2"].reshape(E * HID, D)], axis=0),
        "b1_cols": b1.reshape(-1, P).T,
    }


def kernel(**inputs):
    import numpy as _np
    import concourse.bacc as _bacc
    from concourse import mybir as _mybir
    from concourse.bass_utils import run_bass_kernel_spmd as _run

    nc = _bacc.Bacc("TRN2", target_bir_lowering=False, num_devices=1)
    laid = _lay_out(inputs)
    arrays, args = {}, []
    for name in _INS:
        arr = _np.ascontiguousarray(laid[name])
        arrays[f"in_{name}"] = arr
        args.append(nc.dram_tensor(f"in_{name}", arr.shape, _mybir.dt.from_np(arr.dtype), kind="ExternalInput").ap())
    args.append(nc.dram_tensor("out_0", (B * S, D), _mybir.dt.float32, kind="ExternalOutput").ap())
    two_blocks(nc, *args)
    r = _run(nc, [arrays], core_ids=[0])
    return r.results[0]["out_0"].reshape(B, S, D)
```

```python
import concourse.bass as bass
from concourse import mybir
from contextlib import ExitStack

fp32 = mybir.dt.float32
bf16 = mybir.dt.bfloat16
ALU = mybir.AluOpType
ACT = mybir.ActivationFunctionType
AX = mybir.AxisListType

P = 128
B, S, D = 2, 512, 144
T = S // P
C = B * T
NH, HD = 16, 9
G4 = 4
NHG = NH // G4
NPAIR = B * NH // 2
DT = D - P
NPART = 6
TR_ = NPART * DT
HID = 4 * D
E = 4
NM0 = -(-HID // P)
NM1 = E * HID // P
PW = 64
MXC = NPART * HD
NA = 6 * D + 4 * TR_
EPS = (1e-5, 1e-6)
Q_PART = ((0, 1, 2), (3, 4), (5,))
K_PART = ((0, 3, 5), (1, 4), (2,))
SECT = (0, 1, 3, 4)


def two_blocks(nc, x, cond_t, ident, cols_main, cols_tail, ada, rows, wqkv, wqkv_tail, wo,
               w1, w1_tail, gate, gate_tail, w2, b1_cols, out):
    ctx = ExitStack()
    with ctx:
        def sb(name, shape, dt=fp32):
            return ctx.enter_context(nc.sbuf_tensor(name, shape, dt))

        def sem(name):
            return ctx.enter_context(nc.semaphore(name))

        A_PROB, A_KT, A_QT, A_QK = 0, 16384, 16384 + 8192, 16384 + 8192 + 4096
        arena = sb("arena", [P, A_QK + 8192])

        def f32(off, n):
            return arena[:, off:off + n]

        def b16(off, n):
            return arena[:, off:off + n].bitcast(bf16)

        prob = f32(A_PROB, 16384).rearrange("p (u h c q) -> p u h c q", u=2, h=G4, c=T)
        kT = b16(A_KT, 8192).rearrange("p (b h s) -> p b h s", b=B, h=NH)
        qT = b16(A_QT, 4096).rearrange("p (b r s) -> p b r s", b=B, r=NH // 2)
        qk = b16(A_QK, 8192).rearrange("p (k b t h c) -> p k b t h c", k=2, b=B, t=T, h=NH)
        o = A_PROB + NM1 * S
        z = f32(o, C * 224).rearrange("p (b t d) -> p b t d", b=B, t=T)
        o += C * 224
        hT = f32(o, C * P).rearrange("p (b s) -> p b s", b=B)
        o += C * P
        hR = b16(o, C * P // 2).rearrange("p (b s) -> p b s", b=B)
        o += C * P // 2
        t_h = f32(o, C * P).rearrange("p (b s) -> p b s", b=B)
        o += C * P
        t_a = b16(o, C * P // 2).rearrange("p (b s) -> p b s", b=B)
        o += C * P // 2
        t_b = f32(o, C * P).rearrange("p (b s) -> p b s", b=B)
        o += C * P
        t_c = b16(o, C * P // 2).rearrange("p (b s) -> p b s", b=B)
        o += C * P // 2
        assert o <= A_KT
        big = f32(A_PROB + NM1 * S, 3 * C * E * E).rearrange("p (n c e j) -> p n c e j", n=3, c=C, e=E)
        o = A_PROB
        ada_m = f32(o, 2 * NA).rearrange("p (l f) -> p l f", l=2)
        o += 2 * NA
        ada_t = f32(o, 2 * NA).rearrange("p (l f) -> p l f", l=2)
        o += 2 * NA
        rows_s = f32(o, 7 * D)
        o += 7 * D
        wo_m = f32(o, 2 * D).rearrange("p (l d) -> p l d", l=2)
        o += 2 * D
        wo_t = f32(o, 2 * D).rearrange("p (l d) -> p l d", l=2)
        o += 2 * D
        w2_raw = f32(o, NM0 * D).rearrange("p (m d) -> p m d", m=NM0)
        o += NM0 * D
        cb_m = f32(o, B * P).rearrange("p (b s) -> p b s", b=B)
        o += B * P
        cb_t = f32(o, B * P).rearrange("p (b s) -> p b s", b=B)
        o += B * P
        gates_raw = f32(o, 9 * D).rearrange("p (n f) -> p n f", n=3)
        graw = f32(o, 8 * D).rearrange("p (s b d) -> p s b d", s=4, b=B)
        o += 9 * D
        assert o <= A_PROB + NM1 * S
        NW = 2 * 3 * D + HID + E
        w_src = f32(A_QT, NW)
        NS = NW - 3 * D
        w_a = b16(A_QT + NW, NS // 2)
        w_b = f32(A_QT + NW + NS // 2, NS)
        w_c = b16(A_QT + NW + NS // 2 + NS, NS // 2)
        assert NW + 2 * NS <= 4096
        NE = E * HID
        e_src = f32(A_QT, NE)
        e_a = b16(A_QT + NE, HID // 2)
        e_b = f32(A_QT + NE + HID // 2, HID)
        e_c = b16(A_QT + NE + HID // 2 + HID, HID // 2)
        hm0 = f32(A_PROB, B * NM0 * S).rearrange("p (b m s) -> p b m s", b=B, m=NM0)
        hm1 = [f32(A_PROB, NM1 * S).rearrange("p (m s) -> p m s", m=NM1),
               f32(A_KT, NM1 * S).rearrange("p (m s) -> p m s", m=NM1)]
        w1e = f32(A_QK, NE)
        w2e = f32(A_QK + NE, NM1 * D).rearrange("p (m d) -> p m d", m=NM1)
        b2_row = f32(A_QK + NE + NM1 * D, E * D).rearrange("p (e d) -> p e d", e=E)

        X = sb("X", [P, C, D])
        qkv = sb("qkv", [P, C, 3 * D])
        o_tok = sb("o_tok", [P, C, D])
        wq_m = sb("wq_m", [P, 2, 3 * D])
        w_tail = sb("w_tail", [P, NW], bf16)
        we_tail = sb("we_tail", [P, NE], bf16)
        w1d = sb("w1d", [P, HID])
        gate_m = sb("gate_m", [P, E])
        wog_m = sb("wog_m", [P, 2, B, D])
        wog_t = sb("wog_t", [DT, 2, B, D])
        w2g = sb("w2g", [P, NM0, B, D])
        gbias = sb("gbias", [P, 3, B, D])
        g_last = sb("g_last", [P, B, D])
        bqkv_row = sb("bqkv_row", [P, 3 * D])
        b1c = sb("b1c", [P, NM0 + NM1])
        vS = sb("vS", [P, 2, T, G4, 32])
        oS = sb("oS", [P, S])
        idf = sb("idf", [P, P])
        idb = sb("idb", [P, P], bf16)
        cm = sb("cm", [P, 12])
        ct = sb("ct", [TR_, 16])
        c_m = sb("c_m", [P, 5, B])
        c_t = sb("c_t", [DT, 5, B])
        mod_m = sb("mod_m", [P, 2, 4, B])
        mod_t = sb("mod_t", [TR_, 2, 4, B])
        sc1_m = sb("sc1_m", [P, 2, 2, B])
        sc1_t = sb("sc1_t", [TR_, 2, 2, B])
        ab_m = sb("ab_m", [P, 2, 2, 2, B])
        ab_t = sb("ab_t", [TR_, 2, 2, 2, B])
        st6 = sb("st6", [P, B, T, 6])
        mv = sb("mv", [P, B, T, 2])
        ln4 = sb("ln4", [P, 2, B, T])
        minus_half = sb("minus_half", [P, T])
        mx = sb("mx", [P, 2, T, 2])
        nmx = sb("nmx", [P, T, 2])
        rc = sb("rc", [P, T, G4])
        spl = sb("spl", [P, 2, T, G4 * HD])
        spg = sb("spg", [P, 2, T, G4 * HD])
        lg = sb("lg", [P, C, E])
        lw = sb("lw", [P, C, E])
        cw = sb("cw", [P, C, E])
        sm = sb("sm", [P, 4, C])
        below = sb("below", [P, E, E])
        acc = o_tok
        oT = hT
        oTt = t_h
        ps = ctx.enter_context(nc.psum_tensor("ps", [P, 8, 512], fp32))
        psb = [ps[:, n, :].bitcast(bf16) for n in range(8)]
        TRB, PVB = 7, 6

        NAMES = """x_in0 x_in1 cond_in consts_in ada_in rows_in wo_in w2d_in wq_in wt_in w1d_in misc_in et_in
        we_in out_done id_b silu_a silu_v mod_mm mod_v cb_v gate_mm gates_v gated kt_zero qk_pad vs_pad
        wt_v et_v half_set ln_stats ln_aggr ln_ve ln_y ln_z ln_zt ln_ht ln_r
        qkv_mm qkv_ev xb o_tr oT_ev oTt_ev proj_mm x_new fc1_mm gelu fc2_mm lg_mm route ln_tail gates_a bias2 moe_mm
        moe_acc fin""".split()
        s = {n: sem(n) for n in NAMES}
        AT = """st ex sm mx nstep tq tk evq evk pv oev ot on vs spv spa spp qz""".split()
        a = [{n: sem(f"{n}{l}") for n in AT} for l in range(2)]
        block = ctx.enter_context(nc.Block())

        def pos(i, k):
            q, r = divmod(k, 4)
            hg = i + q
            return min(max(hg, 0), NHG - 1) if isinstance(i, int) else hg, r // 2, r % 2

        LOOP0, LOOPN = 4, 8

        def halves(eng, half):
            for h in range(-3, LOOP0):
                half(0, h, True)
            with eng.Fori(0, LOOPN // 4) as i:
                for k in range(LOOP0, LOOP0 + 4):
                    half(i, k, False)
            for h in range(LOOP0 + LOOPN, NPAIR + 4):
                half(0, h, True)

        def has(i, k, peeled, lo=0):
            return not peeled or lo <= 4 * i + k < NPAIR

        @block.sync
        def _(sp):
            sp.dma_start(X[:, 0:T, :], x[0:S, :].rearrange("(c p) d -> p c d", p=P)).then_inc(s["x_in0"], 16)
            sp.dma_start(X[:, T:C, :], x[S:B * S, :].rearrange("(c p) d -> p c d", p=P)).then_inc(s["x_in1"], 16)
            sp.dma_start(ada_m[:, :, :], ada[:, 0:P, :].rearrange("l p f -> p l f")).then_inc(s["ada_in"], 16)
            sp.dma_start(ada_t[0:DT, :, :], ada[:, P:D, :].rearrange("l p f -> p l f")).then_inc(s["ada_in"], 16)
            sp.dma_start(idf[:, :], ident).then_inc(s["consts_in"], 16)
            sp.dma_start(wq_m[:, :, :], wqkv.rearrange("l p f -> p l f")).then_inc(s["wq_in"], 16)
            sp.dma_start(w1d[:, :], w1[0:P, 0:HID]).then_inc(s["w1d_in"], 16)
            sp.dma_start(w2_raw[:, 0:NM0 - 1, :], w2[0:(NM0 - 1) * P, :].rearrange("(m p) d -> p m d", p=P)).then_inc(s["w2d_in"], 16)
            sp.dma_start(w2_raw[0:64, NM0 - 1, :], w2[(NM0 - 1) * P:HID, :]).then_inc(s["w2d_in"], 16)
            sp.wait_ge(a[0]["on"], 16)
            sp.dma_start(e_src[0:TR_, :], w1_tail[:, HID:HID + NE]).then_inc(s["et_in"], 16)
            sp.wait_ge(a[1]["tq"], NPAIR)
            sp.dma_start(w1e, w1[0:P, HID:HID + NE]).then_inc(s["we_in"], 16)
            sp.dma_start(w2e, w2[HID:HID + NE, :].rearrange("(m p) d -> p m d", p=P)).then_inc(s["we_in"], 16)
            sp.dma_start(b2_row.rearrange("p e d -> p (e d)"), rows[:, 7 * D:11 * D].partition_broadcast(P)).then_inc(s["we_in"], 16)
            for c in range(C):
                sp.wait_ge(s["fin"], 2 * (c + 1))
                sp.dma_start(out[c * P:(c + 1) * P, :], X[:, c, :]).then_inc(s["out_done"], 16)
            sp.wait_ge(s["out_done"], 16 * C)

        def split_pool(pool, l, hg, b):
            for kq, where in ((0, Q_PART), (1, K_PART)):
                v = qkv[:, b * T:(b + 1) * T, bass.ds(kq * D + hg * (G4 * HD), G4 * HD)]
                v4 = v.rearrange("p t (h d) -> p t h d", h=G4)
                r = spg[:, kq]
                r4 = r.rearrange("p t (h d) -> p t h d", h=G4)

                def put(g):
                    return qk[:, kq, b, :, bass.ds(hg * G4, G4), g * HD:(g + 1) * HD]
                yield v4, r4, put, where

        @block.gpsimd
        def _(pool):
            def rstd(n, b):
                pool.wait_ge(s["ln_ve"], 2 * n + b + 1)
                pool.tensor_tensor(ln4[:, 1, b, :], ln4[:, 0, b, :], minus_half[:, :], ALU.pow).then_inc(s["ln_y"], 1)

            pool.dma_start(rows_s[:, :], rows[:, 0:7 * D].partition_broadcast(P)).then_inc(s["rows_in"], 16)
            pool.dma_start(wo_m[:, :, :], wo[:, 0:P, :].rearrange("l p f -> p l f")).then_inc(s["wo_in"], 16)
            pool.dma_start(wo_t[0:DT, :, :], wo[:, P:D, :].rearrange("l p f -> p l f")).then_inc(s["wo_in"], 16)
            pool.dma_start(bqkv_row[:, :], rows[:, 11 * D:14 * D].partition_broadcast(P)).then_inc(s["rows_in"], 16)
            pool.memset(minus_half[:, :], -0.5).then_inc(s["half_set"], 1)
            pool.wait_ge(s["half_set"], 1)
            rstd(0, 0)
            rstd(0, 1)
            kz = kT.rearrange("p b (r two) s -> p (b r) two s", two=2)
            pool.wait_ge(s["ln_y"], 2)
            pool.memset(kz[64:128, :, 0, :].bitcast(fp32), 0.0).then_inc(s["kt_zero"], 1)
            pool.wait_ge(s["kt_zero"], 1)
            pool.memset(kz[0:64, :, 1, :].bitcast(fp32), 0.0).then_inc(s["kt_zero"], 1)
            pool.wait_ge(s["kt_zero"], 2)
            pool.memset(vS[:, :, :, :, :], 0.0).then_inc(s["vs_pad"], 1)
            pool.wait_ge(s["vs_pad"], 1)
            pool.memset(vS[:, :, :, :, 0:1], 1.0).then_inc(s["vs_pad"], 1)
            pool.wait_ge(s["gates_a"], 3)
            pool.wait_ge(s["rows_in"], 32)
            for g in range(4):
                for b in range(B):
                    pool.tensor_tensor(graw[:, g, b, :], graw[:, g, b, :], rows_s[:, g * D:(g + 1) * D], ALU.add).then_inc(s["gates_v"], 1)
            pool.wait_ge(s["gates_v"], 8)
            pool.wait_ge(s["wo_in"], 32)
            for l in range(2):
                for b in range(B):
                    pool.tensor_tensor(wog_m[:, l, b, :], wo_m[:, l, :], graw[:, 2 * l, b, :], ALU.mult).then_inc(s["gated"], 1)
                    pool.tensor_tensor(wog_t[:, l, b, :], wo_t[0:DT, l, :], graw[0:DT, 2 * l, b, :], ALU.mult).then_inc(s["gated"], 1)
            for n, sec in enumerate((0, 2, 1)):
                for b in range(B):
                    pool.tensor_tensor(gbias[:, n, b, :], rows_s[:, (4 + n) * D:(5 + n) * D], graw[:, sec, b, :], ALU.mult).then_inc(s["gated"], 1)
            pool.wait_ge(s["w2d_in"], 32)
            for b in range(B):
                for m in range(NM0):
                    r = P if m < NM0 - 1 else HID - P * (NM0 - 1)
                    pool.tensor_tensor(w2g[0:r, m, b, :], w2_raw[0:r, m, :], graw[0:r, 1, b, :], ALU.mult).then_inc(s["gated"], 1)
            pool.tensor_copy(g_last[:, :, :], graw[:, 3, :, :]).then_inc(s["gated"], 1)

            def add_bias(n):
                for c in range(C):
                    pool.tensor_tensor(X[:, c, :], X[:, c, :], gbias[:, n, c // T, :], ALU.add).then_inc(s["xb"], 1)

            for l in range(2):
                q = a[l]

                def stage_v(i, u, first):
                    if not first:
                        pool.wait_ge(q["pv"], 8 * i + 4 * u - 4)
                    v = qkv[:, u * T:(u + 1) * T, bass.ds(2 * D + i * (G4 * HD), G4 * HD)]
                    pool.tensor_copy(vS[:, u, :, :, 1:1 + HD], v.rearrange("p t (h d) -> p t h d", h=G4)).then_inc(q["vs"], 1)

                def split_group(i, u, n):
                    at = 14 * n
                    for v4, r4, put, w in split_pool(pool, l, i, u):
                        p0, p1, p2 = w
                        pool.tensor_copy(put(p0[0]), v4).then_inc(q["spp"], 1)
                        pool.tensor_copy(put(p0[1]), v4).then_inc(q["spp"], 1)
                        pool.wait_ge(q["spp"], at + 1)
                        pool.tensor_copy(put(p0[2]), v4).then_inc(q["spp"], 1)
                        pool.tensor_tensor(r4, v4, put(p0[0]), ALU.subtract).then_inc(q["spp"], 1)
                        pool.wait_ge(q["spp"], at + 4)
                        pool.tensor_copy(put(p1[0]), r4).then_inc(q["spp"], 1)
                        pool.wait_ge(q["spp"], at + 5)
                        pool.tensor_copy(put(p1[1]), r4).then_inc(q["spp"], 1)
                        pool.tensor_tensor(put(p2[0]), r4, put(p1[0]), ALU.subtract).then_inc(q["spp"], 1)
                        at = at + 7

                pool.wait_ge(s["qk_pad"], 2)

                def round_of(i):
                    for u in range(B):
                        split_group(i, u, 2 * i + (u - 2))
                        stage_v(i - 1, u, False)

                for u in range(B):
                    pool.wait_ge(s["qkv_ev"], 8 * l + 4 * u + 4)
                    split_group(1, u, u)
                    stage_v(0, u, True)
                pool.wait_ge(s["ln_z"], 32 * l + 16)
                if l == 0:
                    pool.wait_ge(s["gated"], GATED)
                add_bias(l)
                with pool.Fori(2, NHG) as i:
                    round_of(i)
                for u in range(B):
                    stage_v(NHG - 1, u, False)
                rstd(2 * l + 1, 0)
                rstd(2 * l + 1, 1)
                if l == 0:
                    pool.wait_ge(s["ln_z"], 32)
                    add_bias(2)
                    rstd(2, 0)
                    rstd(2, 1)

        @block.scalar
        def _(act):
            act.dma_start(c_m[:, 0, :], cond_t[0:P, :]).then_inc(s["cond_in"], 16)
            act.dma_start(c_t[:, 0, :], cond_t[P:D, :]).then_inc(s["cond_in"], 16)
            act.dma_start(cm[:, :], cols_main).then_inc(s["consts_in"], 16)
            act.dma_start(ct[:, :], cols_tail).then_inc(s["consts_in"], 16)
            act.dma_start(w_src[0:TR_, 0:2 * 3 * D].rearrange("p (l f) -> p l f", l=2), wqkv_tail.rearrange("l p f -> p l f")).then_inc(s["wt_in"], 16)
            act.dma_start(w_src[0:TR_, 6 * D:6 * D + HID], w1_tail[:, 0:HID]).then_inc(s["wt_in"], 16)
            act.dma_start(w_src[0:TR_, 6 * D + HID:NW], gate_tail).then_inc(s["wt_in"], 16)
            act.dma_start(b1c[:, :], b1_cols).then_inc(s["misc_in"], 16)
            act.dma_start(gate_m[:, :], gate).then_inc(s["misc_in"], 16)
            act.wait_ge(s["cond_in"], 32)
            act.activation(c_m[:, 1, :], c_m[:, 0, :], ACT.Exp, scale=-1.0).then_inc(s["silu_a"], 1)
            act.activation(c_t[:, 1, :], c_t[:, 0, :], ACT.Exp, scale=-1.0).then_inc(s["silu_a"], 1)

            def modulate(n, b):
                if n == 0:
                    act.wait_ge(s["mod_v"], 8)
                elif n == 1:
                    act.wait_ge(s["mod_v"], MODV)
                act.wait_ge(s["ln_zt"], 4 * n + 2 * b + 1)
                act.activation(hT[:, b, :], ps[:, b, :], ACT.Identity,
                               scale=ab_m[:, n // 2, n % 2, 0, b:b + 1],
                               bias=ab_m[:, n // 2, n % 2, 1, b:b + 1]).then_inc(s["ln_ht"], 1)
                act.wait_ge(s["ln_zt"], 4 * n + 2 * b + 2)
                for d in (t_a, t_h):
                    act.activation(d[0:TR_, b, :], ps[0:TR_, 2 + b, :], ACT.Identity,
                                   scale=ab_t[:, n // 2, n % 2, 0, b:b + 1],
                                   bias=ab_t[:, n // 2, n % 2, 1, b:b + 1]).then_inc(s["ln_tail"], 1)

            for l in range(2):
                q = a[l]
                modulate(2 * l, 0)
                modulate(2 * l, 1)
                if l == 0:
                    for n in range(3):
                        act.wait_ge(s["gate_mm"], 1)
                        w = min(3, 8 - 3 * n) * D
                        act.activation(gates_raw[:, n, 0:w], ps[:, 5 + n, 0:w], ACT.Copy).then_inc(s["gates_a"], 1)
                    for c in range(C):
                        act.wait_ge(s["qkv_mm"], c + 1)
                        act.activation(qkv[:, c, :], ps[:, 4 + c % 4, 0:3 * D], ACT.Copy).then_inc(s["qkv_ev"], 1)
                for b in range(B):
                    for kq, where in ((0, Q_PART), (1, K_PART)):
                        v4 = qkv[:, b * T:(b + 1) * T, kq * D:kq * D + G4 * HD].rearrange("p t (h d) -> p t h d", h=G4)
                        act.wait_ge(s["qkv_ev"], 8 * l + 4 * b + 4)
                        for g in where[0][1:]:
                            act.activation(qk[:, kq, b, :, 0:G4, g * HD:(g + 1) * HD], v4, ACT.Copy).then_inc(q["spa"], 1)
                        act.wait_ge(q["spv"], 8 * b + 4 * kq + 2)
                        g = where[1][1]
                        act.activation(qk[:, kq, b, :, 0:G4, g * HD:(g + 1) * HD],
                                       spl[:, kq].rearrange("p t (h d) -> p t h d", h=G4), ACT.Copy).then_inc(q["spa"], 1)

                def half(i, k, peeled):
                    hg, b, pp = pos(i, k)
                    for j in range(T):
                        if has(i, k, peeled):
                            if j == 0 and not (peeled and 4 * i + k < 4):
                                act.wait_ge(q["pv"], 8 * i + 2 * (k - pp) - 4)
                            if l == 0 and peeled and k == 0 and j == 0:
                                act.wait_ge(s["gated"], GATED)
                            act.wait_ge(q["st"], 16 * i + 4 * k + j + 1)
                            act.activation(prob[:, b, 2 * pp:2 * pp + 2, j, :], ps[:, 2 * (j % 2):2 * (j % 2) + 2, :],
                                           ACT.Exp, scale=1.0 / 3.0).then_inc(q["ex"], 1)
                        if j == 0 and k % 2 == 0 and (not peeled or 4 <= 4 * i + k <= NPAIR + 2):
                            g = 2 * i + (k - 4) // 2
                            act.wait_ge(q["pv"], 4 * g + 4)
                            act.activation(oS[:, :], ps[:, PVB, :], ACT.Copy).then_inc(q["oev"], 1)
                        if j == 0 and has(i, k + 3, peeled):
                            hg3, b3, p3 = pos(i, k + 3)
                            act.wait_ge(q["tk"], 4 * i + k + 4)
                            if l == 0 and peeled and k == -3:
                                act.wait_ge(s["kt_zero"], 2)
                                act.wait_ge(s["wt_v"], 8)
                            for hh in range(2):
                                act.activation(kT[64 * hh:64 * hh + 64, b3, bass.ds(4 * hg3 + 2 * p3 + hh, 1), :],
                                               psb[TRB][64 * hh:64 * hh + 64, 0:S].rearrange("p (a s) -> p a s", a=1),
                                               ACT.Copy).then_inc(q["evk"], 1)
                            act.activation(qT[:, b3, bass.ds(2 * hg3 + p3, 1), :],
                                           psb[TRB][:, S:2 * S].rearrange("p (a s) -> p a s", a=1),
                                           ACT.Copy).then_inc(q["evk"], 1)

                halves(act, half)
                for b in range(B):
                    act.wait_ge(s["o_tr"], 4 * l + 2 * b + 1)
                    act.activation(oT[:, b, :], ps[:, b, :], ACT.Copy).then_inc(s["oT_ev"], 1)
                modulate(2 * l + 1, 0)
                modulate(2 * l + 1, 1)
                if l == 0:
                    for n in range(B * NM0):
                        b, m = divmod(n, NM0)
                        r = P if m < NM0 - 1 else HID - P * (NM0 - 1)
                        act.wait_ge(s["fc1_mm"], n + 1)
                        if n == 0:
                            act.wait_ge(s["misc_in"], 32)
                        act.activation(hm0[0:r, b, m, :], ps[0:r, 4 + n % 4, :], ACT.Gelu, bias=b1c[0:r, m:m + 1]).then_inc(s["gelu"], 1)
                else:
                    act.wait_ge(s["route"], 2)
                    act.activation(lw[:, :, :], lw[:, :, :], ACT.Exp).then_inc(s["route"], 1)
                    for n in range(B * NM1):
                        b, m = divmod(n, NM1)
                        act.wait_ge(s["fc1_mm"], B * NM0 + n + 1)
                        act.activation(hm1[b][:, m, :], ps[:, 4 + n % 4, :], ACT.Gelu_apprx_tanh,
                                       bias=b1c[:, NM0 + m:NM0 + m + 1]).then_inc(s["gelu"], 1)

        @block.vector
        def _(v):
            def parts_of_weights(src, ta, tb, tc, dst, name, at):
                v.tensor_copy(ta, src).then_inc(s[name], 1)
                v.wait_ge(s[name], at + 1)
                v.scalar_tensor_tensor(tb, ta, ct[:, 14:15], src, ALU.mult, ALU.add).then_inc(s[name], 1)
                v.wait_ge(s[name], at + 2)
                v.tensor_copy(tc, tb).then_inc(s[name], 1)
                v.wait_ge(s[name], at + 3)
                v.scalar_tensor_tensor(dst, tc, ct[:, 15:16], tb, ALU.mult, ALU.add).then_inc(s[name], 1)

            v.wait_ge(s["silu_a"], 2)
            v.tensor_scalar(c_m[:, 2, :], c_m[:, 1, :], 1.0, None, ALU.add).then_inc(s["silu_v"], 1)
            v.tensor_scalar(c_t[:, 2, :], c_t[:, 1, :], 1.0, None, ALU.add).then_inc(s["silu_v"], 1)
            v.wait_ge(s["silu_v"], 2)
            v.reciprocal(c_m[:, 3, :], c_m[:, 2, :]).then_inc(s["silu_v"], 1)
            v.reciprocal(c_t[:, 3, :], c_t[:, 2, :]).then_inc(s["silu_v"], 1)
            v.wait_ge(s["silu_v"], 4)
            v.tensor_tensor(c_m[:, 4, :], c_m[:, 0, :], c_m[:, 3, :], ALU.mult).then_inc(s["silu_v"], 1)
            v.tensor_tensor(c_t[:, 4, :], c_t[:, 0, :], c_t[:, 3, :], ALU.mult).then_inc(s["silu_v"], 1)

            def stats(n, b):
                for t in range(T):
                    if n == 0:
                        v.wait_ge(s[f"x_in{b}"], 16)
                    else:
                        v.wait_ge(s["x_new"], 8 * (n - 1) + b * T + t + 1)
                    v.bn_stats(st6[:, b, t, :], X[:, b * T + t, :]).then_inc(s["ln_stats"], 1)
                for t in range(T):
                    v.wait_ge(s["ln_stats"], 8 * n + 4 * b + t + 1)
                    v.bn_aggr(mv[:, b, t, :], st6[:, b, t, :]).then_inc(s["ln_aggr"], 1)
                v.wait_ge(s["ln_aggr"], 8 * n + 4 * b + 4)
                v.tensor_scalar(ln4[:, 0, b, :], mv[:, b, :, 1], EPS[n // 2], None, ALU.add).then_inc(s["ln_ve"], 1)

            def normalise(n, b):
                v.wait_ge(s["ln_y"], 2 * n + b + 1)
                for t in range(T):
                    v.tensor_scalar(z[:, b, t, 0:P], X[:, b * T + t, 0:P], mv[:, b, t, 0:1], ln4[:, 1, b, t:t + 1],
                                    ALU.subtract, ALU.mult).then_inc(s["ln_z"], 1)
                for t in range(T):
                    v.tensor_scalar(z[:, b, t, P:P + TR_].rearrange("p (g d) -> p g d", g=NPART),
                                    X[:, b * T + t, P:D].rearrange("p (g d) -> p g d", g=1).to_broadcast([P, NPART, DT]),
                                    mv[:, b, t, 0:1], ln4[:, 1, b, t:t + 1],
                                    ALU.subtract, ALU.mult).then_inc(s["ln_z"], 1)

            def tails(n, b):
                at = 6 * n + 3 * b
                v.wait_ge(s["ln_tail"], 4 * n + 2 * b + 2)
                v.scalar_tensor_tensor(t_b[0:TR_, b, :], t_a[0:TR_, b, :], ct[:, 12:13], t_h[0:TR_, b, :],
                                       ALU.mult, ALU.add).then_inc(s["ln_r"], 1)
                v.wait_ge(s["ln_r"], at + 1)
                v.tensor_copy(t_c[0:TR_, b, :], t_b[0:TR_, b, :]).then_inc(s["ln_r"], 1)
                v.wait_ge(s["ln_r"], at + 2)
                v.scalar_tensor_tensor(hR[0:TR_, b, :], t_c[0:TR_, b, :], ct[:, 13:14], t_b[0:TR_, b, :],
                                       ALU.mult, ALU.add).then_inc(s["ln_r"], 1)

            def modulation(l, n, at):
                bank = 4 if (l, n) == (0, 0) else 5
                g = 4 * l + 2 * n
                for d, bias, o, r in ((mod_m, cm, 0, P), (mod_t, ct, 16, TR_)):
                    v.tensor_tensor(d[:, l, 2 * n:2 * n + 2, :],
                                    ps[0:r, bank, o + g * B:o + (g + 2) * B].rearrange("p (g b) -> p g b", b=B),
                                    bias[:, g:g + 2].rearrange("p (g b) -> p g b", b=1).to_broadcast([r, 2, B]),
                                    ALU.add).then_inc(s["mod_v"], 1)
                v.wait_ge(s["mod_v"], at + 2)
                for d, sc in ((mod_m, sc1_m), (mod_t, sc1_t)):
                    v.tensor_scalar(sc[:, l, n, :], d[:, l, 2 * n + 1, :], 1.0, None, ALU.add).then_inc(s["mod_v"], 1)
                v.wait_ge(s["mod_v"], at + 4)
                for d, sc, ab, col in ((mod_m, sc1_m, ab_m, cm), (mod_t, sc1_t, ab_t, ct)):
                    if l == 0:
                        v.tensor_scalar(ab[:, 0, n, 0, :], sc[:, 0, n, :], col[:, 8 + 2 * n:9 + 2 * n], None,
                                        ALU.mult).then_inc(s["mod_v"], 1)
                        v.scalar_tensor_tensor(ab[:, 0, n, 1, :], sc[:, 0, n, :], col[:, 9 + 2 * n:10 + 2 * n],
                                               d[:, 0, 2 * n, :], ALU.mult, ALU.add).then_inc(s["mod_v"], 1)
                    else:
                        v.tensor_copy(ab[:, 1, n, 0, :], sc[:, 1, n, :]).then_inc(s["mod_v"], 1)
                        v.tensor_copy(ab[:, 1, n, 1, :], d[:, 1, 2 * n, :]).then_inc(s["mod_v"], 1)

            def split_tails(at, lo, hi):
                cs, n = slice(lo, hi), hi - lo
                parts_of_weights(w_src[0:TR_, cs], w_a[0:TR_, 0:n], w_b[0:TR_, 0:n], w_c[0:TR_, 0:n], w_tail[0:TR_, cs], "wt_v", at)

            stats(0, 0)
            stats(0, 1)
            v.wait_ge(s["silu_v"], 6)
            v.tensor_copy(cb_m, c_m[:, 4, :].rearrange("p (b o) -> p b o", o=1).to_broadcast([P, B, P])).then_inc(s["cb_v"], 1)
            v.tensor_copy(cb_t[0:DT], c_t[:, 4, :].rearrange("p (b o) -> p b o", o=1).to_broadcast([DT, B, P])).then_inc(s["cb_v"], 1)
            normalise(0, 0)
            normalise(0, 1)
            v.wait_ge(s["mod_mm"], 1)
            v.wait_ge(s["consts_in"], 48)
            modulation(0, 0, 0)
            v.tensor_copy(idb[:, :], idf[:, :]).then_inc(s["id_b"], 1)
            v.wait_ge(s["wt_in"], 48)
            split_tails(0, 0, 3 * D)

            def rest_of_setup():
                v.memset(qk.rearrange("p k b t h c -> p (k b t h) c")[:, :, MXC:PW], 0.0).then_inc(s["qk_pad"], 1)
                v.wait_ge(s["qk_pad"], 1)
                v.memset(qk[:, 1].rearrange("p b t h c -> p (b t h) c")[:, :, MXC:MXC + 3], 1.0).then_inc(s["qk_pad"], 1)
                v.wait_ge(s["mod_mm"], 2)
                modulation(0, 1, 8)
                modulation(1, 0, 16)
                modulation(1, 1, 24)
                v.wait_ge(s["wt_v"], 4)
                split_tails(4, 3 * D, NW)

            for l in range(2):
                q = a[l]
                if l == 0:
                    tails(0, 0)
                    tails(0, 1)
                    rest_of_setup()
                else:
                    normalise(2, 1)
                    tails(2, 0)
                    tails(2, 1)
                    v.memset(qk[:, 0].rearrange("p b t h c -> p (b t h) c")[:, :, MXC:MXC + 3], 0.0).then_inc(q["qz"], 1)
                    for c in range(C):
                        v.wait_ge(s["qkv_mm"], 8 + c + 1)
                        if c == 0:
                            v.wait_ge(s["rows_in"], 32)
                        v.tensor_tensor(qkv[:, c, :], ps[:, 4 + c % 4, 0:3 * D], bqkv_row[:, :], ALU.add).then_inc(s["qkv_ev"], 1)
                for b in range(B):
                    v.wait_ge(s["qkv_ev"], 8 * l + 4 * b + 4)
                    for kq, where in ((0, Q_PART), (1, K_PART)):
                        at = 8 * b + 4 * kq
                        v4 = qkv[:, b * T:(b + 1) * T, kq * D:kq * D + G4 * HD].rearrange("p t (h d) -> p t h d", h=G4)
                        r4 = spl[:, kq].rearrange("p t (h d) -> p t h d", h=G4)

                        def put(g):
                            return qk[:, kq, b, :, 0:G4, g * HD:(g + 1) * HD]
                        v.tensor_copy(put(where[0][0]), v4).then_inc(q["spv"], 1)
                        v.wait_ge(q["spv"], at + 1)
                        if b == 1:
                            v.wait_ge(q["spa"], 3 * (kq + 1))
                        v.tensor_tensor(r4, v4, put(where[0][0]), ALU.subtract).then_inc(q["spv"], 1)
                        v.wait_ge(q["spv"], at + 2)
                        v.tensor_copy(put(where[1][0]), r4).then_inc(q["spv"], 1)
                        v.wait_ge(q["spv"], at + 3)
                        v.tensor_tensor(put(where[2][0]), r4, put(where[1][0]), ALU.subtract).then_inc(q["spv"], 1)

                def half(i, k, peeled):
                    n4 = 4 * i + k
                    hg1, b1, p1 = pos(i, k + 1)
                    qm = qk[:, 0, b1, :, bass.ds(4 * hg1 + 2 * p1, 2), :]
                    m1 = mx[:, (k + 1) % 2]
                    do_q = has(i, k + 1, peeled)
                    at = 16 * i + 4 * (k + 1)
                    do_o = k % 2 == 1 and (not peeled or 5 <= n4 <= NPAIR + 3)
                    if do_o:
                        hgo, bo, _ = pos(i, k - 5)
                        g = 2 * i + (k - 5) // 2
                        ot = ps[:, TRB, :].rearrange("p (t h c) -> p t h c", t=T, h=G4)
                        v.wait_ge(q["ot"], g + 1)
                        v.reciprocal(rc[:, :, :], ot[:, :, :, 0]).then_inc(q["on"], 1)
                    for n in range(8):
                        if has(i, k + 2, peeled):
                            v.wait_ge(q["sm"], 32 * i + 8 * (k + 2) + n + 1)
                            v.reduce_max(mx[:, k % 2, n // 2, n % 2:n % 2 + 1], ps[:, 4 + n % 2, :], AX.X).then_inc(q["mx"], 1)
                        if do_o and n == 0:
                            v.wait_ge(q["on"], 2 * g + 1)
                            v.tensor_tensor(o_tok[:, bo * T:(bo + 1) * T, bass.ds(hgo * (G4 * HD), G4 * HD)].rearrange("p t (h d) -> p t h d", h=G4),
                                            ot[:, :, :, 1:1 + HD],
                                            rc[:, :, :].rearrange("p t (h o) -> p t h o", o=1).to_broadcast([P, T, G4, HD]),
                                            ALU.mult).then_inc(q["on"], 1)
                        if do_q and n == 0:
                            v.wait_ge(q["mx"], 32 * i + 8 * (k + 1) + 8)
                            v.tensor_scalar(qm[:, :, :, MXC], m1, -1.0, None, ALU.mult).then_inc(q["nstep"], 1)
                        if do_q and n == 1:
                            v.wait_ge(q["nstep"], at + 1)
                            v.scalar_tensor_tensor(nmx[:, :, :], m1, -1.0, qm[:, :, :, MXC], ALU.mult, ALU.subtract).then_inc(q["nstep"], 1)
                        if do_q and n == 2:
                            v.wait_ge(q["nstep"], at + 2)
                            v.tensor_copy(qm[:, :, :, MXC + 1], nmx[:, :, :]).then_inc(q["nstep"], 1)
                        if do_q and n == 3:
                            v.wait_ge(q["nstep"], at + 3)
                            v.tensor_tensor(qm[:, :, :, MXC + 2], nmx[:, :, :], qm[:, :, :, MXC + 1], ALU.subtract).then_inc(q["nstep"], 1)
                        if do_q and n == 5:
                            v.wait_ge(q["tq"], n4 + 2)
                            v.tensor_copy(qT[:, b1, bass.ds(2 * hg1 + p1, 1), :],
                                          psb[TRB][:, 0:S].rearrange("p (a s) -> p a s", a=1)).then_inc(q["evq"], 1)

                halves(v, half)
                for b in range(B):
                    v.wait_ge(s["o_tr"], 4 * l + 2 * b + 2)
                    v.tensor_copy(oTt[0:DT, b, :], ps[0:DT, 2 + b, :]).then_inc(s["oTt_ev"], 1)
                for b in range(B):
                    for c in range(b * T, (b + 1) * T):
                        v.wait_ge(s["proj_mm"], 8 * l + c + 1)
                        v.wait_ge(s["xb"], 16 * l + c + 1)
                        v.tensor_tensor(X[:, c, :], ps[:, 4 + c % 4, 0:D], X[:, c, :], ALU.add).then_inc(s["x_new"], 1)
                    stats(2 * l + 1, b)
                for b in range(B):
                    normalise(2 * l + 1, b)
                for b in range(B):
                    tails(2 * l + 1, b)
                if l == 0:
                    v.wait_ge(s["et_in"], 16)
                    for e in range(E):
                        cs = slice(e * HID, (e + 1) * HID)
                        parts_of_weights(e_src[0:TR_, cs], e_a[0:TR_], e_b[0:TR_], e_c[0:TR_], we_tail[0:TR_, cs], "et_v", 4 * e)
                        v.wait_ge(s["et_v"], 4 * e + 4)
                    for b in range(B):
                        for c in range(b * T, (b + 1) * T):
                            v.wait_ge(s["fc2_mm"], c + 1)
                            v.wait_ge(s["xb"], 8 + c + 1)
                            v.tensor_tensor(X[:, c, :], ps[:, 4 + (c + 2) % 4, 0:D], X[:, c, :], ALU.add).then_inc(s["x_new"], 1)
                        stats(2, b)
                        if b == 0:
                            normalise(2, 0)

            v.memset(below[:, :, :], 0.0).then_inc(s["bias2"], 1)
            for e in range(1, E):
                v.wait_ge(s["bias2"], e)
                v.memset(below[:, e, 0:e], 1.0).then_inc(s["bias2"], 1)
            v.wait_ge(s["lg_mm"], 1)
            v.tensor_copy(lg[:, :, :], ps[:, 0, 0:C * E].rearrange("p (c e) -> p c e", c=C)).then_inc(s["route"], 1)
            v.wait_ge(s["route"], 1)
            v.reduce_max(sm[:, 0, :], lg[:, :, :], AX.X).then_inc(s["moe_acc"], 1)
            v.wait_ge(s["moe_acc"], 1)
            v.tensor_tensor(lw[:, :, :], lg[:, :, :], sm[:, 0, :].rearrange("p (c o) -> p c o", o=1).to_broadcast([P, C, E]),
                            ALU.subtract).then_inc(s["route"], 1)
            r = 1

            def chain(ins):
                nonlocal r
                ins.then_inc(s["moe_acc"], 1)
                r += 1
                v.wait_ge(s["moe_acc"], r)
            v.wait_ge(s["bias2"], E)
            for e in range(E):
                other = lg[:, :, :]
                own = lg[:, :, e:e + 1].to_broadcast([P, C, E])
                chain(v.tensor_tensor(big[:, 0, :, e, :], other, own, ALU.is_gt))
                chain(v.tensor_tensor(big[:, 1, :, e, :], other, own, ALU.is_equal))
                chain(v.tensor_tensor(big[:, 1, :, e, :], big[:, 1, :, e, :],
                                      below[:, e:e + 1, :].to_broadcast([P, C, E]), ALU.mult))
            chain(v.tensor_tensor(big[:, 2, :, :, :], big[:, 0, :, :, :], big[:, 1, :, :, :], ALU.add))
            chain(v.reduce_sum(cw[:, :, :], big[:, 2, :, :, :], AX.X))
            chain(v.tensor_scalar(cw[:, :, :], cw[:, :, :], 2.0, None, ALU.is_lt))
            v.wait_ge(s["route"], 3)
            chain(v.tensor_tensor(cw[:, :, :], cw[:, :, :], lw[:, :, :], ALU.mult))
            chain(v.reduce_sum(sm[:, 1, :], cw[:, :, :], AX.X))
            chain(v.reciprocal(sm[:, 2, :], sm[:, 1, :]))
            chain(v.tensor_tensor(cw[:, :, :], cw[:, :, :], sm[:, 2, :].rearrange("p (c o) -> p c o", o=1).to_broadcast([P, C, E]), ALU.mult))
            v.wait_ge(s["we_in"], 48)
            for e in range(E):
                for c in range(C):
                    if e == 0:
                        v.tensor_scalar(acc[:, c, :], b2_row[:, 0, :], cw[:, c, 0:1], None, ALU.mult).then_inc(s["bias2"], 1)
                    else:
                        v.wait_ge(s["bias2"], E + (e - 1) * C + c + 1)
                        v.scalar_tensor_tensor(acc[:, c, :], b2_row[:, e, :], cw[:, c, e:e + 1], acc[:, c, :],
                                               ALU.mult, ALU.add).then_inc(s["bias2"], 1)
            for c in range(C):
                v.wait_ge(s["bias2"], E + (E - 1) * C + c + 1)
                for e in range(E):
                    n = c * E + e
                    v.wait_ge(s["moe_mm"], n + 1)
                    if e:
                        v.wait_ge(s["moe_acc"], r + n)
                    v.scalar_tensor_tensor(acc[:, c, :], ps[:, e, 0:D],
                                           cw[:, c, e:e + 1], acc[:, c, :], ALU.mult, ALU.add).then_inc(s["moe_acc"], 1)
                v.wait_ge(s["moe_acc"], r + (c + 1) * E)
                v.tensor_tensor(acc[:, c, :], acc[:, c, :], g_last[:, c // T, :], ALU.mult).then_inc(s["fin"], 1)
                v.wait_ge(s["fin"], 2 * c + 1)
                v.tensor_tensor(X[:, c, :], acc[:, c, :], X[:, c, :], ALU.add).then_inc(s["fin"], 1)

        @block.tensor
        def _(pe):
            mm = nc.tensor.matmul
            pe.wait_ge(s["ada_in"], 32)
            pe.wait_ge(s["silu_v"], 6)
            def columns(l, n):
                bank = 4 if (l, n) == (0, 0) else 5
                for m in (2 * n, 2 * n + 1):
                    at = (4 * l + m) * B
                    cs = slice(SECT[m] * D, SECT[m] * D + P)
                    mm(ps[:, bank, at:at + B], ada_m[:, l, cs], c_m[:, 4, :], start=True, stop=False)
                    mm(ps[:, bank, at:at + B], ada_t[0:DT, l, cs], c_t[:, 4, :], start=False, stop=True)
                for m in (2 * n, 2 * n + 1):
                    at = 16 + (4 * l + m) * B
                    cs = slice(6 * D + m * TR_, 6 * D + (m + 1) * TR_)
                    mm(ps[0:TR_, bank, at:at + B], ada_m[:, l, cs], c_m[:, 4, :], start=True, stop=False)
                    last = mm(ps[0:TR_, bank, at:at + B], ada_t[0:DT, l, cs], c_t[:, 4, :], start=False, stop=True)
                return last

            columns(0, 0).then_inc(s["mod_mm"], 1)

            def transpose_z(n, b):
                pe.wait_ge(s["ln_z"], 16 * n + 8 * b + 4)
                if n == 0:
                    pe.wait_ge(s["consts_in"], 48)
                for t in range(T):
                    last = pe.transpose(ps[:, b, t * P:(t + 1) * P], z[:, b, t, 0:P], idf[:, :])
                last.then_inc(s["ln_zt"], 1)
                pe.wait_ge(s["ln_z"], 16 * n + 8 * b + 8)
                for t in range(T):
                    last = pe.transpose(ps[0:TR_, 2 + b, t * P:(t + 1) * P], z[:, b, t, P:P + TR_], idf[:, :])
                last.then_inc(s["ln_zt"], 1)

            def normed(n, b):
                pe.wait_ge(s["ln_ht"], 2 * n + b + 1)
                pe.wait_ge(s["ln_r"], 3 * (2 * n + b + 1))

            for l in range(2):
                q = a[l]
                transpose_z(2 * l, 0)
                transpose_z(2 * l, 1)
                if l == 0:
                    pe.wait_ge(s["cb_v"], 2)
                    for n in range(8):
                        g, b = divmod(n, B)
                        cs = slice((2 + 3 * (g % 2)) * D, (3 + 3 * (g % 2)) * D)
                        to = ps[:, 5 + n // 3, (n % 3) * D:(n % 3 + 1) * D]
                        mm(to, cb_m[:, b, :], ada_m[:, g // 2, cs], start=True, stop=False)
                        last = mm(to, cb_t[0:DT, b, :], ada_t[0:DT, g // 2, cs], start=False, stop=True)
                    last.then_inc(s["gate_mm"], 1)
                    pe.wait_ge(s["wq_in"], 16)
                    pe.wait_ge(s["wt_v"], 4)
                    pe.wait_ge(s["gates_a"], 3)
                    pe.wait_ge(s["mod_v"], 2)
                else:
                    pe.wait_ge(s["x_new"], 16)
                for c in range(C):
                    b, t = divmod(c, T)
                    normed(2 * l, b)
                    if c >= 4:
                        pe.wait_ge(s["qkv_ev"], 8 * l + c - 3)
                    mm(ps[:, 4 + c % 4, 0:3 * D], hT[:, b, t * P:(t + 1) * P], wq_m[:, l, :], start=True, stop=False)
                    mm(ps[:, 4 + c % 4, 0:3 * D], hR[0:TR_, b, t * P:(t + 1) * P],
                       w_tail[0:TR_, 3 * D * l:3 * D * (l + 1)], start=False, stop=True).then_inc(s["qkv_mm"], 1)
                if l == 0:
                    pe.wait_ge(s["qkv_ev"], 6)
                    columns(0, 1)
                    columns(1, 0)
                    columns(1, 1).then_inc(s["mod_mm"], 1)

                def ready_kq(i, k, peeled):
                    n3 = 4 * i + k + 3
                    if not has(i, k + 3, peeled):
                        return
                    if not (peeled and n3 == 0):
                        pe.wait_ge(q["evk"], 12 * i + 3 * (k + 3))
                    if not (peeled and n3 < 3):
                        pe.wait_ge(q["evq"], 4 * i + k + 1)
                    if k % 2 == 1 and (not peeled or n3 >= 8):
                        pe.wait_ge(q["on"], 4 * i + 2 * ((k - 3) // 2))
                    if peeled and n3 < 4:
                        b3 = n3 // 2
                        pe.wait_ge(q["spv"], 8 * b3 + 8)
                        pe.wait_ge(q["spa"], 6 * b3 + 6)
                        if l == 1:
                            pe.wait_ge(q["qz"], 1)
                        else:
                            pe.wait_ge(s["qk_pad"], 2)
                        pe.wait_ge(s["qkv_ev"], 8 * l + 8)
                        pe.wait_ge(s["id_b"], 1)
                    else:
                        pe.wait_ge(q["spp"], 14 * (2 * i + (k + 3) // 2 - 1))

                def ready_max(i, k, peeled):
                    if not has(i, k + 1, peeled):
                        return
                    pe.wait_ge(q["nstep"], 16 * i + 4 * (k + 1) + 4)
                    if peeled and k % 2 == 1 and k + 3 >= NPAIR:
                        pe.wait_ge(q["on"], 2 * ((k - 3) // 2))
                    pe.wait_ge(q["evk"], min(12 * i + 3 * (k + 4), 3 * NPAIR) if peeled else 12 * i + 3 * (k + 4))

                def half(i, k, peeled):
                    n4 = 4 * i + k
                    hg, b, pp = pos(i, k)
                    hg1, b1, p1 = pos(i, k + 1)
                    hg2, b2, p2 = pos(i, k + 2)
                    hg3, b3, p3 = pos(i, k + 3)
                    odd = k % 2 == 1

                    def score_for_max(j, hh):
                        n = 2 * j + hh
                        if not (peeled and n4 == -2 and n < 2):
                            pe.wait_ge(q["mx"], 32 * i + 8 * (k + 2) + n - 1)
                        mm(ps[:, 4 + hh, :], qT[:, b2, bass.ds(2 * hg2 + p2, 1), j * P:(j + 1) * P],
                           kT[:, b2, bass.ds(4 * hg2 + 2 * p2 + hh, 1), :], start=True, stop=True).then_inc(q["sm"], 1)

                    def head_outputs(m, g, u):
                        c, h0 = m // 2, (m % 2) * (S // 2)
                        if m == 0:
                            pe.wait_ge(q["vs"], g + 1)
                            if l == 0 and peeled:
                                pe.wait_ge(s["vs_pad"], 2)
                            if not (peeled and n4 == 2):
                                pe.wait_ge(q["oev"], g)
                        if m % 2 == 0:
                            pe.wait_ge(q["ex"], 8 * g + 5 + c)
                        for h in range(G4):
                            last = mm(ps[32 * h:32 * h + 32, PVB, h0:h0 + S // 2], vS[:, u, c, h, :],
                                      prob[:, u, h, c, h0:h0 + S // 2], start=(m == 0), stop=(c == T - 1),
                                      tile_position=(0, 32 * h), skip_group_check=True)
                        if m % 2:
                            last.then_inc(q["pv"], 1)

                    for j in range(T):
                        if has(i, k + 2, peeled):
                            if j == 0:
                                pe.wait_ge(q["evk"], 12 * i + 3 * (k + 3))
                            score_for_max(j, 0)
                        if has(i, k, peeled):
                            if j == 0:
                                pe.wait_ge(q["evq"], n4 + 1)
                            if not (peeled and n4 == 0 and j < 2):
                                pe.wait_ge(q["ex"], 16 * i + 4 * k + j - 1)
                            for hh in range(2):
                                last = mm(ps[:, 2 * (j % 2) + hh, :],
                                          kT[:, b, bass.ds(4 * hg + 2 * pp + hh, 1), j * P:(j + 1) * P],
                                          qT[:, b, bass.ds(2 * hg + pp, 1), :], start=True, stop=True)
                            last.then_inc(q["st"], 1)
                        if has(i, k + 2, peeled):
                            if j == 0:
                                ready_kq(i, k, peeled)
                            if j == 2:
                                ready_max(i, k, peeled)
                            score_for_max(j, 1)
                        sl = 4 * odd + j
                        if sl and (not peeled or 2 + odd <= n4 <= NPAIR + 1):
                            g = 2 * i + (k - 2 - odd) // 2
                            u = ((k - 2 - odd) // 2) % 2
                            for m in ((6, 7) if sl == 7 else (sl - 1,)):
                                head_outputs(m, g, u)
                        if j == 0 and has(i, k + 3, peeled):
                            if not has(i, k + 2, peeled):
                                ready_kq(i, k, peeled)
                            for w, kq in ((0, 1), (1, 0)):
                                for t in range(T):
                                    last = pe.transpose(psb[TRB][:, w * S + t * P:w * S + (t + 1) * P],
                                                        qk[:, kq, b3, t, bass.ds(4 * hg3 + 2 * p3, 2), :], idb[:, :])
                            last.then_inc(q["tk"], 1)
                        if j == 2 and has(i, k + 1, peeled):
                            if not has(i, k + 2, peeled):
                                ready_max(i, k, peeled)
                            for t in range(T):
                                last = pe.transpose(psb[TRB][:, t * P:(t + 1) * P],
                                                    qk[:, 0, b1, t, bass.ds(4 * hg1 + 2 * p1, 2), :], idb[:, :])
                            last.then_inc(q["tq"], 1)
                        if j == 3 and not odd and (not peeled or 4 <= n4 <= NPAIR + 2):
                            g = 2 * i + (k - 4) // 2
                            pe.wait_ge(q["evq"], min(n4 + 2, NPAIR) if peeled else n4 + 2)
                            if peeled and n4 >= NPAIR:
                                pe.wait_ge(q["on"], 2 * g)
                            pe.wait_ge(q["oev"], g + 1)
                            for t in range(T):
                                last = pe.transpose(ps[:, TRB, t * P:(t + 1) * P], oS[:, t * P:(t + 1) * P], idf[:, :])
                            last.then_inc(q["ot"], 1)

                halves(pe, half)
                pe.wait_ge(q["on"], 16)
                for b in range(B):
                    for t in range(T):
                        last = pe.transpose(ps[:, b, t * P:(t + 1) * P], o_tok[:, b * T + t, 0:P], idf[:, :])
                    last.then_inc(s["o_tr"], 1)
                    for t in range(T):
                        last = pe.transpose(ps[0:DT, 2 + b, t * P:(t + 1) * P], o_tok[:, b * T + t, P:D], idf[:, :])
                    last.then_inc(s["o_tr"], 1)
                pe.wait_ge(s["gated"], 8)
                for c in range(C):
                    b, t = divmod(c, T)
                    pe.wait_ge(s["oT_ev"], 2 * l + b + 1)
                    pe.wait_ge(s["oTt_ev"], 2 * l + b + 1)
                    if c >= 4:
                        pe.wait_ge(s["x_new"], 16 * l + c - 3)
                    mm(ps[:, 4 + c % 4, 0:D], oT[:, b, t * P:(t + 1) * P], wog_m[:, l, b, :], start=True, stop=False)
                    mm(ps[:, 4 + c % 4, 0:D], oTt[0:DT, b, t * P:(t + 1) * P], wog_t[:, l, b, :],
                       start=False, stop=True).then_inc(s["proj_mm"], 1)
                transpose_z(2 * l + 1, 0)
                transpose_z(2 * l + 1, 1)

                if l == 0:
                    pe.wait_ge(s["w1d_in"], 16)
                    pe.wait_ge(s["wt_v"], 8)
                    for n in range(B * NM0):
                        b, m = divmod(n, NM0)
                        r = P if m < NM0 - 1 else HID - P * (NM0 - 1)
                        normed(1, b)
                        pe.wait_ge(s["x_new"], 8)
                        if n >= 4:
                            pe.wait_ge(s["gelu"], n - 3)
                        mm(ps[0:r, 4 + n % 4, :], w1d[:, m * P:m * P + r], hT[:, b, :], start=True, stop=False)
                        mm(ps[0:r, 4 + n % 4, :], w_tail[0:TR_, 6 * D + m * P:6 * D + m * P + r], hR[0:TR_, b, :],
                           start=False, stop=True).then_inc(s["fc1_mm"], 1)
                    pe.wait_ge(s["gated"], 8 + 6 + 2 * NM0)
                    for c in range(C):
                        b, t = divmod(c, T)
                        pe.wait_ge(s["gelu"], max(NM0 * (b + 1), min(NM0 + 2 + c, B * NM0)))
                        if c >= 4:
                            pe.wait_ge(s["x_new"], 8 + c - 3)
                        for m in range(NM0):
                            r = P if m < NM0 - 1 else HID - P * (NM0 - 1)
                            last = mm(ps[:, 4 + (c + 2) % 4, 0:D], hm0[0:r, b, m, t * P:(t + 1) * P], w2g[0:r, m, b, :],
                                      start=(m == 0), stop=(m == NM0 - 1))
                        last.then_inc(s["fc2_mm"], 1)
                else:
                    pe.wait_ge(s["misc_in"], 32)
                    for c in range(C):
                        b, t = divmod(c, T)
                        normed(3, b)
                        normed(3, 1)
                        mm(ps[:, 0, c * E:(c + 1) * E], hT[:, b, t * P:(t + 1) * P], gate_m[:, :], start=True, stop=False)
                        last = mm(ps[:, 0, c * E:(c + 1) * E], hR[0:TR_, b, t * P:(t + 1) * P],
                                  w_tail[0:TR_, 6 * D + HID:NW], start=False, stop=True)
                    last.then_inc(s["lg_mm"], 1)
                    pe.wait_ge(s["we_in"], 48)
                    pe.wait_ge(s["et_v"], 4 * E)
                    pe.wait_ge(s["x_new"], 24)

                    def up(b):
                        for m in range(NM1):
                            n = b * NM1 + m
                            if n >= 4:
                                pe.wait_ge(s["gelu"], B * NM0 + n - 3)
                            mm(ps[:, 4 + n % 4, :], w1e[:, m * P:(m + 1) * P], hT[:, b, :], start=True, stop=False)
                            mm(ps[:, 4 + n % 4, :], we_tail[0:TR_, m * P:(m + 1) * P], hR[0:TR_, b, :],
                               start=False, stop=True).then_inc(s["fc1_mm"], 1)

                    def down(b):
                        for c in range(b * T, (b + 1) * T):
                            t = c % T
                            for e in range(E):
                                if c >= 1:
                                    pe.wait_ge(s["moe_acc"], ROUTE + (c - 1) * E + e + 1)
                                else:
                                    pe.wait_ge(s["route"], 1)
                                lo, hi = e * HID, (e + 1) * HID
                                while lo < hi:
                                    m, r0 = divmod(lo, P)
                                    r1 = min(P, r0 + hi - lo)
                                    pe.wait_ge(s["gelu"], B * NM0 + b * NM1 + m + 1)
                                    last = mm(ps[:, e, 0:D],
                                              hm1[b][r0:r1, m, t * P:(t + 1) * P], w2e[r0:r1, m, :],
                                              start=(lo == e * HID), stop=(lo + r1 - r0 == hi))
                                    lo += r1 - r0
                                last.then_inc(s["moe_mm"], 1)
                    up(0)
                    down(0)
                    up(1)
                    down(1)


GATED = 8 + 6 + 2 * NM0 + 1
MODV = 32
ROUTE = 1 + 3 * E + 7


_INS = ["x", "cond_t", "ident", "cols_main", "cols_tail", "ada", "rows", "wqkv", "wqkv_tail", "wo",
        "w1", "w1_tail", "gate", "gate_tail", "w2", "b1_cols"]


def _lay_out(i):
    import numpy as np
    f = {k: np.asarray(v) for k, v in i.items()}
    L0, L1 = "L0_cond_", "L1_cond_"

    def tail(w):
        return np.tile(w[P:D], (NPART, 1))

    def columns(vs):
        w = np.stack(vs, axis=1)
        return w[0:P], tail(w)

    ada_b = [f[L0 + "ada_b"], f[L1 + "b_adaln"]]
    vs = [v[sec * D:(sec + 1) * D] for v in ada_b for sec in SECT]
    vs += [f[L0 + n] for n in ("ln1_w", "ln1_b", "ln2_w", "ln2_b")]
    main, tails = columns(vs)
    part = np.repeat(np.arange(NPART), DT)
    x_of, w_of = np.zeros(NPART, int), np.zeros(NPART, int)
    for n in range(3):
        x_of[list(Q_PART[n])] = n
        w_of[list(K_PART[n])] = n
    pick = np.stack([-(k[part] >= n).astype(np.float32) for k in (x_of, w_of) for n in (1, 2)], axis=1)
    wq0 = np.concatenate([f[L0 + n] for n in ("wq", "wk", "wv")], axis=1)
    wqkv = [wq0, f[L1 + "w_qkv"]]
    w1 = np.concatenate([f[L0 + "fc1_w"], f[L1 + "w1"].transpose(1, 0, 2).reshape(D, E * HID)], axis=1)
    b1 = np.concatenate([f[L0 + "fc1_b"], np.zeros(NM0 * P - HID, np.float32), f[L1 + "b1"].reshape(-1)])
    rows = np.concatenate([ada_b[0][2 * D:3 * D], ada_b[0][5 * D:6 * D], ada_b[1][2 * D:3 * D], ada_b[1][5 * D:6 * D],
                           f[L0 + "wo_b"], f[L1 + "b_proj"], f[L0 + "fc2_b"], f[L1 + "b2"].reshape(-1),
                           f[L1 + "b_qkv"]])[None]
    ada = [np.concatenate([w] + [np.tile(w[:, sec * D + P:(sec + 1) * D], (1, NPART)) for sec in SECT], axis=1)
           for w in (f[L0 + "ada_w"], f[L1 + "w_adaln"])]
    return {
        "x": f["x"].reshape(B * S, D), "cond_t": f["cond_1152"].T, "ident": np.eye(P, dtype=np.float32),
        "cols_main": main, "cols_tail": np.concatenate([tails, pick], axis=1),
        "ada": np.stack(ada), "rows": rows,
        "wqkv": np.stack([w[0:P] for w in wqkv]), "wqkv_tail": np.stack([tail(w) for w in wqkv]),
        "wo": np.stack([f[L0 + "wo"], f[L1 + "w_proj"]]), "w1": w1, "w1_tail": tail(w1),
        "gate": f[L1 + "w_gate"][0:P], "gate_tail": tail(f[L1 + "w_gate"]),
        "w2": np.concatenate([f[L0 + "fc2_w"], f[L1 + "w2"].reshape(E * HID, D)], axis=0),
        "b1_cols": b1.reshape(-1, P).T,
    }


def kernel(**inputs):
    import numpy as _np
    import concourse.bacc as _bacc
    from concourse import mybir as _mybir
    from concourse.bass_utils import run_bass_kernel_spmd as _run

    nc = _bacc.Bacc("TRN2", target_bir_lowering=False, num_devices=1)
    laid = _lay_out(inputs)
    arrays, args = {}, []
    for name in _INS:
        arr = _np.ascontiguousarray(laid[name])
        arrays[f"in_{name}"] = arr
        args.append(nc.dram_tensor(f"in_{name}", arr.shape, _mybir.dt.from_np(arr.dtype), kind="ExternalInput").ap())
    args.append(nc.dram_tensor("out_0", (B * S, D), _mybir.dt.float32, kind="ExternalOutput").ap())
    two_blocks(nc, *args)
    r = _run(nc, [arrays], core_ids=[0])
    return r.results[0]["out_0"].reshape(B, S, D)
```

```python
import concourse.bass as bass
from concourse import mybir
from contextlib import ExitStack

fp32 = mybir.dt.float32
bf16 = mybir.dt.bfloat16
ALU = mybir.AluOpType
ACT = mybir.ActivationFunctionType
AX = mybir.AxisListType

P = 128
B, S, D = 2, 512, 144
T = S // P
C = B * T
NH, HD = 16, 9
G4 = 4
NHG = NH // G4
NPAIR = B * NH // 2
DT = D - P
NPART = 6
TR_ = NPART * DT
TB_ = TR_ + 3
HID = 4 * D
E = 4
NM0 = -(-HID // P)
NM1 = E * HID // P
PW = 64
MXC = NPART * HD
NN = 2 * D + 2 * TR_
NG = 4 * D
NA = 4 * NN + NG
EPS = (1e-5, 1e-6)
Q_PART = ((0, 1, 2), (3, 4), (5,))
K_PART = ((0, 3, 5), (1, 4), (2,))


def two_blocks(nc, x, cond_t, consts, ada, rows, wqkv, w_tails, wo, w1, we_tails, w2, out):
    ctx = ExitStack()
    with ctx:
        def sb(name, shape, dt=fp32):
            return ctx.enter_context(nc.sbuf_tensor(name, shape, dt))

        def sem(name):
            return ctx.enter_context(nc.semaphore(name))

        A_PROB, A_KT, A_QT, A_QK = 0, 16384, 16384 + 8192, 16384 + 8192 + 4096
        arena = sb("arena", [P, A_QK + 8192])

        def f32(off, n):
            return arena[:, off:off + n]

        def b16(off, n):
            return arena[:, off:off + n].bitcast(bf16)

        prob = f32(A_PROB, 16384).rearrange("p (u h c q) -> p u h c q", u=2, h=G4, c=T)
        kT = b16(A_KT, 8192).rearrange("p (b h s) -> p b h s", b=B, h=NH)
        qT = b16(A_QT, 4096).rearrange("p (b r s) -> p b r s", b=B, r=NH // 2)
        qk = b16(A_QK, 8192).rearrange("p (k b t h c) -> p k b t h c", k=2, b=B, t=T, h=NH)
        o = A_PROB + NM1 * S
        z = f32(o, C * 224).rearrange("p (b t d) -> p b t d", b=B, t=T)
        o += C * 224
        hT = f32(o, C * P).rearrange("p (b s) -> p b s", b=B)
        o += C * P
        hR = b16(o, C * P // 2).rearrange("p (b s) -> p b s", b=B)
        o += C * P // 2
        t_h = f32(o, C * P).rearrange("p (b s) -> p b s", b=B)
        o += C * P
        t_a = b16(o, C * P // 2).rearrange("p (b s) -> p b s", b=B)
        o += C * P // 2
        t_b = f32(o, C * P).rearrange("p (b s) -> p b s", b=B)
        o += C * P
        t_c = b16(o, C * P // 2).rearrange("p (b s) -> p b s", b=B)
        o += C * P // 2
        assert o <= A_KT
        big = f32(A_PROB + NM1 * S, 3 * C * E * E).rearrange("p (n c e j) -> p n c e j", n=3, c=C, e=E)
        o = A_PROB
        ada_m = f32(o, NA)
        o += NA
        ada_t = f32(o, NA)
        o += NA
        assert o <= A_PROB + NM1 * S
        A_W = o
        NW = 2 * 3 * D + HID + E
        w_src = f32(A_W, NW)
        NS = NW - 3 * D
        w_a = b16(A_W + NW, NS // 2)
        w_b = f32(A_W + NW + NS // 2, NS)
        w_c = b16(A_QT + NW + NS // 2 + NS, NS // 2)
        assert A_W + NW + 2 * NS <= A_PROB + NM1 * S
        NE = E * HID
        e_src = f32(A_QT, NE)
        e_a = b16(A_QT + NE, HID // 2)
        e_b = f32(A_QT + NE + HID // 2, HID)
        e_c = b16(A_QT + NE + HID // 2 + HID, HID // 2)
        hm0 = f32(A_PROB, B * NM0 * S).rearrange("p (b m s) -> p b m s", b=B, m=NM0)
        hm1 = [f32(A_PROB, NM1 * S).rearrange("p (m s) -> p m s", m=NM1),
               f32(A_KT, NM1 * S).rearrange("p (m s) -> p m s", m=NM1)]
        w1e = f32(A_QK, NE)
        w2e = f32(A_QK + NE, NM1 * D).rearrange("p (m d) -> p m d", m=NM1)
        b2_row = f32(A_QK + NE + NM1 * D, E * D).rearrange("p (e d) -> p e d", e=E)

        X = sb("X", [P, C, D])
        qkv = sb("qkv", [P, C, 3 * D])
        o_tok = sb("o_tok", [P, C, D])
        wq_m = sb("wq_m", [P, 2, 3 * D])
        w_tail = sb("w_tail", [P, NW], bf16)
        we_tail = sb("we_tail", [P, NE], bf16)
        w1d = sb("w1d", [P, HID])
        wog_m = sb("wog_m", [P, B, 2, D])
        wog_t = sb("wog_t", [DT, B, 2, D])
        w2g = sb("w2g", [P, B, NM0, D])
        gbias = sb("gbias", [P, B, 3, D])
        graw = we_tail[:, :].bitcast(fp32)[:, 0:3 * B * D].rearrange("p (s b d) -> p s b d", s=3, b=B)
        g_last = sb("g_last", [P, B, D])
        NC_ = (P, 4, 4, 4, NM0 + NM1, E)
        cst = sb("cst", [P, sum(NC_)])
        idf, cm, ct, pick, b1c, gate_m = [cst[:, sum(NC_[:n]):sum(NC_[:n + 1])] for n in range(6)]
        vS = sb("vS", [P, 2, T, G4, 32])
        oS = sb("oS", [P, S])
        idb = sb("idb", [P, P], bf16)
        c_m = sb("c_m", [P, 5, B])
        c_t = sb("c_t", [DT + 1, 5, B])
        sc1_m = sb("sc1_m", [P, 2, B])
        sc1_t = sb("sc1_t", [TR_, 2, B])
        ab_m = sb("ab_m", [P, 2, 2, 2, B])
        ab_t = sb("ab_t", [TR_, 2, 2, 2, B])
        st6 = sb("st6", [P, B, T, 6])
        mv = sb("mv", [P, B, T, 2])
        ln4 = sb("ln4", [P, 2, B, T])
        minus_half = sb("minus_half", [P, T])
        idle = sb("idle", [P, 2])
        mx = sb("mx", [P, 2, T, 2])
        nmx = sb("nmx", [P, T, 2])
        rc = sb("rc", [P, T, G4])
        ou = sb("ou", [P, T, G4, 1 + HD])
        spl = sb("spl", [P, 2, T, G4 * HD])
        spg = sb("spg", [P, 2, T, G4 * HD])
        lg = sb("lg", [P, C, E])
        lw = sb("lw", [P, C, E])
        cw = sb("cw", [P, C, E])
        sm = sb("sm", [P, 4, C])
        below = sb("below", [P, E, E])
        acc = o_tok
        oT = hT
        oTt = t_h
        ada_g = o_tok[:, :, :].rearrange("p c d -> p (c d)")
        cb_m = oS[:, 0:B * P].rearrange("p (b s) -> p b s", b=B)
        cb_t = oS[:, B * P:2 * B * P].rearrange("p (b s) -> p b s", b=B)
        ps = ctx.enter_context(nc.psum_tensor("ps", [P, 8, 512], fp32))
        psb = [ps[:, n, :].bitcast(bf16) for n in range(8)]
        TRB, PVB = 7, 6

        NAMES = """x_in0 x_in1 cond_in consts_in ada1_in adat_in adag_in adar_in gb_in wo_in w2d_in wq_in wt_in
        wt2_in w1d_in et_in one_v ones_h wt_p table
        we_in out_done id_b silu_a silu_v mod_mm mod_v cb_v gate_mm gates_v gated kt_zero qk_pad vs_pad
        wt_v et_v half_set ln_stats ln_aggr ln_ve ln_y ln_z ln_zt ln_ht ln_r
        qkv_mm qkv_ev xb o_tr oT_ev oTt_ev proj_mm x_new fc1_mm gelu fc2_mm lg_mm route ln_tail gates_a bias2 moe_mm
        moe_acc fin""".split()
        s = {n: sem(n) for n in NAMES}
        AT = """st ex sm mx nstep tq tk evq evk pv oev ot ou on vs spv spa spp qz""".split()
        a = [{n: sem(f"{n}{l}") for n in AT} for l in range(2)]
        block = ctx.enter_context(nc.Block())

        def pos(i, k):
            q, r = divmod(k, 4)
            hg = i + q
            return min(max(hg, 0), NHG - 1) if isinstance(i, int) else hg, r // 2, r % 2

        def output_bank(g):
            return g - 2 if isinstance(g, int) and g >= 6 else PVB

        LOOP0, LOOPN = 4, 8

        def halves(eng, half, start):
            for h in range(start, LOOP0):
                half(0, h, True)
            with eng.Fori(0, LOOPN // 4) as i:
                for k in range(LOOP0, LOOP0 + 4):
                    half(i, k, False)
            for h in range(LOOP0 + LOOPN, NPAIR):
                half(0, h, True)

        def has(i, k, peeled, lo=0):
            return not peeled or lo <= 4 * i + k < NPAIR

        @block.sync
        def _(sp):
            sp.dma_start(X[:, 0:T, :], x[0:S, :].rearrange("(c p) d -> p c d", p=P)).then_inc(s["x_in0"], 16)
            sp.dma_start(ada_m[:, 0:NN], ada[0:P, 0:NN]).then_inc(s["ada1_in"], 16)
            sp.dma_start(ada_t[0:DT + 1, :], ada[P:D + 1, :]).then_inc(s["adat_in"], 16)
            sp.dma_start(cst[:, :], consts).then_inc(s["consts_in"], 16)
            sp.dma_start(X[:, T:C, :], x[S:B * S, :].rearrange("(c p) d -> p c d", p=P)).then_inc(s["x_in1"], 16)
            sp.dma_start(w_src[0:TB_, 0:3 * D], w_tails[:, 0:3 * D]).then_inc(s["wt_in"], 16)
            sp.dma_start(wq_m[:, :, :], wqkv.rearrange("l p f -> p l f")).then_inc(s["wq_in"], 16)
            sp.dma_start(ada_m[:, NN + NG:NA], ada[0:P, NN + NG:NA]).then_inc(s["adar_in"], 16)
            sp.dma_start(w_src[0:TB_, 3 * D:NW], w_tails[:, 3 * D:NW]).then_inc(s["wt2_in"], 16)
            sp.dma_start(ada_g[:, 0:NG], ada[0:P, NN:NN + NG]).then_inc(s["adag_in"], 16)
            sp.dma_start(ada_g[0:DT + 1, NG:2 * NG], ada[P:D + 1, NN:NN + NG]).then_inc(s["adag_in"], 16)
            sp.dma_start(w1d[:, :], w1[0:P, 0:HID]).then_inc(s["w1d_in"], 16)
            sp.dma_start(w2g[:, 1, 0:NM0 - 1, :], w2[0:(NM0 - 1) * P, :].rearrange("(m p) d -> p m d", p=P)).then_inc(s["w2d_in"], 16)
            sp.dma_start(w2g[0:64, 1, NM0 - 1, :], w2[(NM0 - 1) * P:HID, :]).then_inc(s["w2d_in"], 16)
            sp.dma_start(wog_m[:, 1], wo[:, 0:P, :].rearrange("l p f -> p l f")).then_inc(s["wo_in"], 16)
            sp.dma_start(wog_t[:, 1], wo[:, P:D, :].rearrange("l p f -> p l f")).then_inc(s["wo_in"], 16)
            sp.dma_start(gbias[:, 1].rearrange("p n d -> p (n d)"), rows[:, 0:3 * D].partition_broadcast(P)).then_inc(s["gb_in"], 16)
            sp.wait_ge(a[0]["on"], 16)
            sp.dma_start(e_src[0:TR_, :], we_tails).then_inc(s["et_in"], 16)
            sp.wait_ge(a[1]["tq"], NPAIR)
            sp.dma_start(w1e, w1[0:P, HID:HID + NE]).then_inc(s["we_in"], 16)
            sp.dma_start(w2e, w2[HID:HID + NE, :].rearrange("(m p) d -> p m d", p=P)).then_inc(s["we_in"], 16)
            sp.dma_start(b2_row.rearrange("p e d -> p (e d)"), rows[:, 3 * D:7 * D].partition_broadcast(P)).then_inc(s["we_in"], 16)
            for c in range(C):
                sp.wait_ge(s["fin"], 2 * (c + 1))
                sp.dma_start(out[c * P:(c + 1) * P, :], X[:, c, :]).then_inc(s["out_done"], 16)
            sp.wait_ge(s["out_done"], 16 * C)

        def split_pool(pool, l, hg, b):
            for kq, where in ((0, Q_PART), (1, K_PART)):
                v = qkv[:, b * T:(b + 1) * T, bass.ds(kq * D + hg * (G4 * HD), G4 * HD)]
                v4 = v.rearrange("p t (h d) -> p t h d", h=G4)
                r = spg[:, kq]
                r4 = r.rearrange("p t (h d) -> p t h d", h=G4)

                def put(g):
                    return qk[:, kq, b, :, bass.ds(hg * G4, G4), g * HD:(g + 1) * HD]
                yield v4, r4, put, where

        @block.gpsimd
        def _(pool):
            def rstd(n, b):
                pool.wait_ge(s["ln_ve"], 2 * n + b + 1)
                pool.tensor_tensor(ln4[:, 1, b, :], ln4[:, 0, b, :], minus_half[:, :], ALU.pow).then_inc(s["ln_y"], 1)

            pool.memset(minus_half[:, :], -0.5).then_inc(s["half_set"], 1)
            pool.memset(idle[:, 0:1], 0.0).then_inc(s["half_set"], 1)
            kz = kT.rearrange("p b (r two) s -> p (b r) two s", two=2)
            pool.wait_ge(s["half_set"], 2)
            pool.memset(kz[64:128, :, 0, :].bitcast(fp32), 0.0).then_inc(s["kt_zero"], 1)
            pool.wait_ge(s["kt_zero"], 1)
            rstd(0, 0)
            rstd(0, 1)
            pool.wait_ge(s["ln_y"], 2)
            pool.memset(vS[:, :, :, :, :], 0.0).then_inc(s["vs_pad"], 1)
            pool.wait_ge(s["vs_pad"], 1)
            pool.memset(vS[:, :, :, :, 0:1], 1.0).then_inc(s["vs_pad"], 1)
            pool.memset(qk.rearrange("p k b t h c -> p (k b t h) c")[:, :, MXC:PW], 0.0).then_inc(s["qk_pad"], 1)
            pool.wait_ge(s["qk_pad"], 1)
            pool.memset(qk[:, 1].rearrange("p b t h c -> p (b t h) c")[:, :, MXC:MXC + 3], 1.0).then_inc(s["qk_pad"], 1)
            pool.wait_ge(s["qk_pad"], 2)
            pool.memset(kz[0:64, :, 1, :].bitcast(fp32), 0.0).then_inc(s["kt_zero"], 1)
            pool.wait_ge(s["kt_zero"], 2)

            def fold_gates():
                pool.wait_ge(s["gates_a"], 3)
                pool.wait_ge(s["wo_in"], 32)
                pool.wait_ge(s["gb_in"], 16)
                for b in range(B):
                    for l in range(2):
                        pool.tensor_tensor(wog_m[:, b, l, :], wog_m[:, 1, l, :], graw[:, 2 * l, b, :], ALU.mult).then_inc(s["gated"], 1)
                        pool.tensor_tensor(wog_t[:, b, l, :], wog_t[:, 1, l, :], graw[0:DT, 2 * l, b, :], ALU.mult).then_inc(s["gated"], 1)
                for b in range(B):
                    for n, sec in enumerate((0, 2, 1)):
                        pool.tensor_tensor(gbias[:, b, n, :], gbias[:, 1, n, :], graw[:, sec, b, :], ALU.mult).then_inc(s["gated"], 1)
                pool.wait_ge(s["gated"], 14)

            def fold_fc2():
                pool.wait_ge(s["w2d_in"], 32)
                for b in range(B):
                    for m in range(NM0):
                        r = P if m < NM0 - 1 else HID - P * (NM0 - 1)
                        pool.tensor_tensor(w2g[0:r, b, m, :], w2g[0:r, 1, m, :], graw[0:r, 1, b, :], ALU.mult).then_inc(s["gated"], 1)

            def add_bias(n):
                for c in range(C):
                    pool.tensor_tensor(X[:, c, :], X[:, c, :], gbias[:, c // T, n, :], ALU.add).then_inc(s["xb"], 1)

            for l in range(2):
                q = a[l]

                def stage_v(i, u, first):
                    if not first:
                        pool.wait_ge(q["pv"], 8 * i + 4 * u - 4)
                    v = qkv[:, u * T:(u + 1) * T, bass.ds(2 * D + i * (G4 * HD), G4 * HD)]
                    pool.tensor_copy(vS[:, u, :, :, 1:1 + HD], v.rearrange("p t (h d) -> p t h d", h=G4)).then_inc(q["vs"], 1)

                def split_group(i, u, n):
                    at = 14 * n
                    for v4, r4, put, w in split_pool(pool, l, i, u):
                        p0, p1, p2 = w
                        pool.tensor_copy(put(p0[0]), v4).then_inc(q["spp"], 1)
                        pool.tensor_copy(put(p0[1]), v4).then_inc(q["spp"], 1)
                        pool.wait_ge(q["spp"], at + 1)
                        pool.tensor_copy(put(p0[2]), v4).then_inc(q["spp"], 1)
                        pool.tensor_tensor(r4, v4, put(p0[0]), ALU.subtract).then_inc(q["spp"], 1)
                        pool.wait_ge(q["spp"], at + 4)
                        pool.tensor_copy(put(p1[0]), r4).then_inc(q["spp"], 1)
                        pool.wait_ge(q["spp"], at + 5)
                        pool.tensor_copy(put(p1[1]), r4).then_inc(q["spp"], 1)
                        pool.tensor_tensor(put(p2[0]), r4, put(p1[0]), ALU.subtract).then_inc(q["spp"], 1)
                        at = at + 7

                def round_of(i):
                    for u in range(B):
                        split_group(i, u, 2 * i + (u - 2))
                        stage_v(i - 1, u, False)

                for u in range(B):
                    pool.wait_ge(s["qkv_ev"], 8 * l + 4 * u + 4)
                    split_group(1, u, u)
                    stage_v(0, u, True)
                with pool.Fori(2, NHG) as i:
                    round_of(i)
                if l == 0:
                    fold_gates()
                pool.wait_ge(s["ln_z"], 32 * l + 16)
                add_bias(l)
                for u in range(B):
                    stage_v(NHG - 1, u, False)
                if l == 0:
                    fold_fc2()
                rstd(2 * l + 1, 0)
                rstd(2 * l + 1, 1)
                if l == 0:
                    pool.wait_ge(s["ln_ve"], 2 * l + 4)
                    pool.wait_ge(s["ln_y"], 4)
                    pool.memset(hR[TR_:TB_, :, :], 1.0).then_inc(s["ones_h"], 1)
                    pool.wait_ge(s["ones_h"], 1)
                    pool.memset(qk[:, 0].rearrange("p b t h c -> p (b t h) c")[:, :, MXC:MXC + 3], 0.0).then_inc(a[1]["qz"], 1)
                    pool.wait_ge(s["ln_z"], 32)
                    add_bias(2)
                    rstd(2, 0)
                    rstd(2, 1)

        @block.scalar
        def _(act):
            act.dma_start(c_m[:, 0, :], cond_t[0:P, :]).then_inc(s["cond_in"], 16)
            act.dma_start(c_t[0:DT, 0, :], cond_t[P:D, :]).then_inc(s["cond_in"], 16)
            def preload(func):
                act.activation(idle[:, 1:2], idle[:, 0:1], func).then_inc(s["table"], 1)

            act.wait_ge(s["half_set"], 2)
            preload(ACT.Exp)
            act.wait_ge(s["cond_in"], 32)
            act.activation(c_m[:, 1, :], c_m[:, 0, :], ACT.Exp, scale=-1.0).then_inc(s["silu_a"], 1)
            act.activation(c_t[0:DT, 1, :], c_t[0:DT, 0, :], ACT.Exp, scale=-1.0).then_inc(s["silu_a"], 1)

            def modulate_tails(n, b):
                if n == 0:
                    act.wait_ge(s["mod_v"], 6)
                elif n == 1:
                    act.wait_ge(s["mod_v"], MODV)
                act.wait_ge(s["ln_zt"], 4 * n + 2 * b + 1)
                for d in (t_a, t_h):
                    act.activation(d[0:TR_, b, :], ps[0:TR_, 2 + b, :], ACT.Identity,
                                   scale=ab_t[:, n // 2, n % 2, 0, b:b + 1],
                                   bias=ab_t[:, n // 2, n % 2, 1, b:b + 1]).then_inc(s["ln_tail"], 1)

            def modulate_main(n, b):
                act.wait_ge(s["ln_zt"], 4 * n + 2 * b + 2)
                act.activation(hT[:, b, :], ps[:, b, :], ACT.Identity,
                               scale=ab_m[:, n // 2, n % 2, 0, b:b + 1],
                               bias=ab_m[:, n // 2, n % 2, 1, b:b + 1]).then_inc(s["ln_ht"], 1)

            def modulate(n, b):
                modulate_tails(n, b)
                modulate_main(n, b)

            act.wait_ge(s["wt_in"], 16)
            act.activation(w_a[0:TR_, 0:3 * D], w_src[0:TR_, 0:3 * D], ACT.Copy).then_inc(s["wt_p"], 1)
            for l in range(2):
                q = a[l]
                modulate(2 * l, 0)
                if l == 0:
                    act.wait_ge(s["wt_p"], 2)
                    act.activation(w_c[0:TR_, 0:3 * D], w_b[0:TR_, 0:3 * D], ACT.Copy).then_inc(s["wt_p"], 1)
                def copies(b, kq, where):
                    v4 = qkv[:, b * T:(b + 1) * T, kq * D:kq * D + G4 * HD].rearrange("p t (h d) -> p t h d", h=G4)
                    act.wait_ge(s["qkv_ev"], 8 * l + 4 * b + 4)
                    for g in where[0][1:]:
                        act.activation(qk[:, kq, b, :, 0:G4, g * HD:(g + 1) * HD], v4, ACT.Copy).then_inc(q["spa"], 1)
                    act.wait_ge(q["spv"], 8 * b + 4 * kq + 2)
                    g = where[1][1]
                    act.activation(qk[:, kq, b, :, 0:G4, g * HD:(g + 1) * HD],
                                   spl[:, kq].rearrange("p t (h d) -> p t h d", h=G4), ACT.Copy).then_inc(q["spa"], 1)

                def projected(lo, hi):
                    for c in range(lo, hi):
                        act.wait_ge(s["qkv_mm"], 8 * l + c + 1)
                        act.activation(qkv[:, c, :], ps[:, QKV_BANK[c], 0:3 * D], ACT.Copy).then_inc(s["qkv_ev"], 1)

                def outputs_out(g):
                    act.wait_ge(q["pv"], 4 * g + 4)
                    if isinstance(g, int) and g >= 6:
                        act.wait_ge(q["ot"], g)
                    act.activation(oS[:, :], ps[:, output_bank(g), :], ACT.Copy).then_inc(q["oev"], 1)

                def half(i, k, peeled):
                    hg, b, pp = pos(i, k)
                    for j in range(T):
                        if has(i, k, peeled):
                            if j == 0 and not (peeled and 4 * i + k < 4):
                                act.wait_ge(q["pv"], 8 * i + 2 * (k - pp) - 4)
                            act.wait_ge(q["st"], 16 * i + 4 * k + j + 1)
                            act.activation(prob[:, b, 2 * pp:2 * pp + 2, j, :], ps[:, 2 * (j % 2):2 * (j % 2) + 2, :],
                                           ACT.Exp, scale=1.0 / 3.0).then_inc(q["ex"], 1)
                        if l == 0 and peeled and j == 0 and k in (0, 1, 2):
                            n = (k + 2) % 3
                            w = (2 if n == 2 else 3) * D
                            act.wait_ge(s["gate_mm"], 3 * k + 2)
                            to = (g_last[:, :, :].rearrange("p b d -> p (b d)") if n == 2 else
                                  we_tail[:, :].bitcast(fp32)[:, n * w:(n + 1) * w])
                            act.activation(to, ps[:, PVB, 0:w], ACT.Copy).then_inc(s["gates_a"], 1)
                        if j == 0 and k % 2 == 0 and (not peeled or 4 <= 4 * i + k):
                            outputs_out(2 * i + (k - 4) // 2)
                        if j == 0 and peeled and k == NPAIR - 1:
                            outputs_out(6)
                        if j == 0 and has(i, k + 3, peeled):
                            hg3, b3, p3 = pos(i, k + 3)
                            act.wait_ge(q["tk"], 4 * i + k + 4)
                            if l == 0 and peeled and k == -3:
                                act.wait_ge(s["kt_zero"], 2)
                                act.wait_ge(s["wt_v"], 1)
                            for hh in range(2):
                                act.activation(kT[64 * hh:64 * hh + 64, b3, bass.ds(4 * hg3 + 2 * p3 + hh, 1), :],
                                               psb[TRB][64 * hh:64 * hh + 64, 0:S].rearrange("p (a s) -> p a s", a=1),
                                               ACT.Copy).then_inc(q["evk"], 1)
                            act.activation(qT[:, b3, bass.ds(2 * hg3 + p3, 1), :],
                                           psb[TRB][:, S:2 * S].rearrange("p (a s) -> p a s", a=1),
                                           ACT.Copy).then_inc(q["evk"], 1)

                if l == 1:
                    preload(ACT.Exp)
                if l == 0:
                    act.wait_ge(s["wt2_in"], 16)
                    act.wait_ge(s["wt_p"], 4)
                    act.activation(w_a[0:TB_, 0:NS], w_src[0:TB_, 3 * D:NW], ACT.Copy).then_inc(s["wt_p"], 1)
                    projected(0, 2)
                    act.wait_ge(s["wt_p"], 6)
                    act.activation(w_c[0:TB_, 0:NS], w_b[0:TB_, 0:NS], ACT.Copy).then_inc(s["wt_p"], 1)
                projected(2 - 2 * l, T)
                copies(0, 0, Q_PART)
                copies(0, 1, K_PART)
                modulate_tails(2 * l, 1)
                half(0, -3, True)
                modulate_main(2 * l, 1)
                half(0, -2, True)
                projected(T, C)
                v4 = [qkv[:, T:C, kq * D:kq * D + G4 * HD].rearrange("p t (h d) -> p t h d", h=G4) for kq in range(2)]
                r4 = [spl[:, kq].rearrange("p t (h d) -> p t h d", h=G4) for kq in range(2)]

                def copy(kq, where, n, src):
                    g = where[n[0]][n[1]]
                    act.activation(qk[:, kq, 1, :, 0:G4, g * HD:(g + 1) * HD], src[kq], ACT.Copy).then_inc(q["spa"], 1)
                act.wait_ge(s["qkv_ev"], 8 * l + 8)
                copy(0, Q_PART, (0, 0), v4)
                copy(1, K_PART, (0, 0), v4)
                for n in (1, 2):
                    copy(0, Q_PART, (0, n), v4)
                    copy(1, K_PART, (0, n), v4)
                act.wait_ge(q["spv"], 9)
                copy(0, Q_PART, (1, 0), r4)
                act.wait_ge(q["spv"], 10)
                copy(1, K_PART, (1, 0), r4)
                copy(0, Q_PART, (1, 1), r4)
                copy(1, K_PART, (1, 1), r4)
                half(0, -1, True)
                halves(act, half, 0)
                for b in range(B):
                    act.wait_ge(s["o_tr"], 4 * l + 2 * b + 1)
                    act.activation(oT[:, b, :], ps[:, HEADS_BANK[b][0], :], ACT.Copy).then_inc(s["oT_ev"], 1)
                    if b == 0:
                        outputs_out(7)
                act.wait_ge(s["o_tr"], 4 * l + 4)
                act.activation(oTt[0:DT, 1, :], ps[0:DT, HEADS_BANK[1][1], :], ACT.Copy).then_inc(s["oTt_ev"], 1)
                preload(ACT.Gelu if l == 0 else ACT.Gelu_apprx_tanh)
                modulate(2 * l + 1, 0)
                if l == 0:
                    for n in range(B * NM0):
                        b, m = divmod(n, NM0)
                        r = P if m < NM0 - 1 else HID - P * (NM0 - 1)
                        act.wait_ge(s["fc1_mm"], n + 1)
                        act.activation(hm0[0:r, b, m, :], ps[0:r, 4 + n % 4, :], ACT.Gelu, bias=b1c[0:r, m:m + 1]).then_inc(s["gelu"], 1)
                        if n == NM0 - 1:
                            modulate(1, 1)
                else:
                    for n in range(B * NM1):
                        b, m = divmod(n, NM1)
                        if n == UP0:
                            modulate(3, 1)
                        if n == UP0 + 8:
                            act.wait_ge(s["route"], 2)
                            act.activation(lw[:, :, :], lw[:, :, :], ACT.Exp).then_inc(s["route"], 1)
                        act.wait_ge(s["fc1_mm"], B * NM0 + n + 1)
                        act.activation(hm1[b][:, m, :], ps[:, 4 + n % 4, :], ACT.Gelu_apprx_tanh,
                                       bias=b1c[:, NM0 + m:NM0 + m + 1]).then_inc(s["gelu"], 1)

        @block.vector
        def _(v):
            def parts_of_weights(src, ta, tb, tc, dst, name, at, rows=TR_):
                v.tensor_copy(ta, src).then_inc(s[name], 1)
                v.wait_ge(s[name], at + 1)
                v.scalar_tensor_tensor(tb, ta, pick[0:rows, 2:3], src, ALU.mult, ALU.add).then_inc(s[name], 1)
                v.wait_ge(s[name], at + 2)
                v.tensor_copy(tc, tb).then_inc(s[name], 1)
                v.wait_ge(s[name], at + 3)
                v.scalar_tensor_tensor(dst, tc, pick[0:rows, 3:4], tb, ALU.mult, ALU.add).then_inc(s[name], 1)

            def silu():
                v.wait_ge(s["silu_a"], 2)
                v.tensor_scalar(c_m[:, 2, :], c_m[:, 1, :], 1.0, None, ALU.add).then_inc(s["silu_v"], 1)
                v.tensor_scalar(c_t[0:DT, 2, :], c_t[0:DT, 1, :], 1.0, None, ALU.add).then_inc(s["silu_v"], 1)
                v.wait_ge(s["silu_v"], 2)
                v.reciprocal(c_m[:, 3, :], c_m[:, 2, :]).then_inc(s["silu_v"], 1)
                v.reciprocal(c_t[0:DT, 3, :], c_t[0:DT, 2, :]).then_inc(s["silu_v"], 1)
                v.wait_ge(s["silu_v"], 4)
                v.wait_ge(s["one_v"], 1)
                v.tensor_tensor(c_m[:, 4, :], c_m[:, 0, :], c_m[:, 3, :], ALU.mult).then_inc(s["silu_v"], 1)
                v.tensor_tensor(c_t[0:DT, 4, :], c_t[0:DT, 0, :], c_t[0:DT, 3, :], ALU.mult).then_inc(s["silu_v"], 1)

            def stats(n, b):
                for t in range(T):
                    if n == 0:
                        v.wait_ge(s[f"x_in{b}"], 16)
                    else:
                        v.wait_ge(s["x_new"], 8 * (n - 1) + b * T + t + 1)
                    v.bn_stats(st6[:, b, t, :], X[:, b * T + t, :]).then_inc(s["ln_stats"], 1)
                for t in range(T):
                    v.wait_ge(s["ln_stats"], 8 * n + 4 * b + t + 1)
                    v.bn_aggr(mv[:, b, t, :], st6[:, b, t, :]).then_inc(s["ln_aggr"], 1)
                v.wait_ge(s["ln_aggr"], 8 * n + 4 * b + 4)
                v.tensor_scalar(ln4[:, 0, b, :], mv[:, b, :, 1], EPS[n // 2], None, ALU.add).then_inc(s["ln_ve"], 1)

            def normalise_tails(n, b):
                v.wait_ge(s["ln_y"], 2 * n + b + 1)
                for t in range(T):
                    v.tensor_scalar(z[:, b, t, P:P + TR_].rearrange("p (g d) -> p g d", g=NPART),
                                    X[:, b * T + t, P:D].rearrange("p (g d) -> p g d", g=1).to_broadcast([P, NPART, DT]),
                                    mv[:, b, t, 0:1], ln4[:, 1, b, t:t + 1],
                                    ALU.subtract, ALU.mult).then_inc(s["ln_z"], 1)

            def normalise_main(n, b):
                for t in range(T):
                    v.tensor_scalar(z[:, b, t, 0:P], X[:, b * T + t, 0:P], mv[:, b, t, 0:1], ln4[:, 1, b, t:t + 1],
                                    ALU.subtract, ALU.mult).then_inc(s["ln_z"], 1)

            def normalise(n, b):
                normalise_tails(n, b)
                normalise_main(n, b)

            def tails(n, b):
                at = 6 * n + 3 * b
                v.wait_ge(s["ln_tail"], 4 * n + 2 * b + 2)
                v.scalar_tensor_tensor(t_b[0:TR_, b, :], t_a[0:TR_, b, :], pick[0:TR_, 0:1], t_h[0:TR_, b, :],
                                       ALU.mult, ALU.add).then_inc(s["ln_r"], 1)
                v.wait_ge(s["ln_r"], at + 1)
                v.tensor_copy(t_c[0:TR_, b, :], t_b[0:TR_, b, :]).then_inc(s["ln_r"], 1)
                v.wait_ge(s["ln_r"], at + 2)
                v.scalar_tensor_tensor(hR[0:TR_, b, :], t_c[0:TR_, b, :], pick[0:TR_, 1:2], t_b[0:TR_, b, :],
                                       ALU.mult, ALU.add).then_inc(s["ln_r"], 1)

            def modulation0(n, at):
                halves_ = ((sc1_m, ab_m, cm, 0, P), (sc1_t, ab_t, ct, 16, TR_))
                bank = 4
                for sc, ab, col, o, r in halves_:
                    v.tensor_scalar(sc[:, n, :], ps[0:r, bank, o + (2 * n + 1) * B:o + (2 * n + 2) * B], 1.0, None, ALU.add).then_inc(s["mod_v"], 1)
                v.wait_ge(s["mod_v"], at + 2)
                for sc, ab, col, o, r in halves_:
                    v.tensor_scalar(ab[:, 0, n, 0, :], sc[:, n, :], col[0:r, 2 * n:2 * n + 1], None, ALU.mult).then_inc(s["mod_v"], 1)
                    v.scalar_tensor_tensor(ab[:, 0, n, 1, :], sc[:, n, :], col[0:r, 2 * n + 1:2 * n + 2],
                                           ps[0:r, bank, o + 2 * n * B:o + (2 * n + 1) * B], ALU.mult, ALU.add).then_inc(s["mod_v"], 1)

            def modulation1():
                for ab, o, r in ((ab_m, 0, P), (ab_t, 16, TR_)):
                    cols = ps[0:r, 5, o + 4 * B:o + 8 * B].rearrange("p (n m b) -> p n m b", n=2, m=2)
                    v.tensor_scalar(ab[:, 1, :, 0, :], cols[:, :, 1, :], 1.0, None, ALU.add).then_inc(s["mod_v"], 1)
                    v.tensor_copy(ab[:, 1, :, 1, :], cols[:, :, 0, :]).then_inc(s["mod_v"], 1)

            v.memset(c_t[0:DT + 1, 4, :], 1.0).then_inc(s["one_v"], 1)
            silu()
            stats(0, 0)
            normalise_tails(0, 0)
            v.wait_ge(s["mod_mm"], 1)
            v.wait_ge(s["consts_in"], 16)
            modulation0(0, 0)
            normalise_main(0, 0)
            v.wait_ge(s["wt_p"], 1)
            v.scalar_tensor_tensor(w_b[0:TR_, 0:3 * D], w_a[0:TR_, 0:3 * D], pick[0:TR_, 2:3],
                                   w_src[0:TR_, 0:3 * D], ALU.mult, ALU.add).then_inc(s["wt_p"], 1)

            for l in range(2):
                q = a[l]
                if l == 0:
                    tails(0, 0)
                    v.wait_ge(s["wt_p"], 3)
                    v.scalar_tensor_tensor(w_tail[0:TR_, 0:3 * D], w_c[0:TR_, 0:3 * D], pick[0:TR_, 3:4],
                                           w_b[0:TR_, 0:3 * D], ALU.mult, ALU.add).then_inc(s["wt_p"], 1)
                    stats(0, 1)
                    v.tensor_copy(idb[:, :], idf[:, :]).then_inc(s["id_b"], 1)
                    v.wait_ge(s["wt_p"], 5)
                    v.scalar_tensor_tensor(w_b[0:TB_, 0:NS], w_a[0:TB_, 0:NS], pick[0:TB_, 2:3],
                                           w_src[0:TB_, 3 * D:NW], ALU.mult, ALU.add).then_inc(s["wt_p"], 1)
                    normalise(0, 1)
                    v.wait_ge(s["wt_p"], 7)
                    v.scalar_tensor_tensor(w_tail[0:TB_, 3 * D:NW], w_c[0:TB_, 0:NS], pick[0:TB_, 3:4],
                                           w_b[0:TB_, 0:NS], ALU.mult, ALU.add).then_inc(s["wt_v"], 1)

                def first_group(b):
                    v.wait_ge(s["qkv_ev"], 8 * l + 4 * b + 4)
                    for kq, where in ((0, Q_PART), (1, K_PART)):
                        at = 8 * b + 4 * kq
                        v4 = qkv[:, b * T:(b + 1) * T, kq * D:kq * D + G4 * HD].rearrange("p t (h d) -> p t h d", h=G4)
                        r4 = spl[:, kq].rearrange("p t (h d) -> p t h d", h=G4)

                        def put(g):
                            return qk[:, kq, b, :, 0:G4, g * HD:(g + 1) * HD]
                        v.tensor_copy(put(where[0][0]), v4).then_inc(q["spv"], 1)
                        v.wait_ge(q["spv"], at + 1)
                        v.tensor_tensor(r4, v4, put(where[0][0]), ALU.subtract).then_inc(q["spv"], 1)
                        v.wait_ge(q["spv"], at + 2)
                        v.tensor_copy(put(where[1][0]), r4).then_inc(q["spv"], 1)
                        v.wait_ge(q["spv"], at + 3)
                        v.tensor_tensor(put(where[2][0]), r4, put(where[1][0]), ALU.subtract).then_inc(q["spv"], 1)
                def outputs_read(g):
                    v.wait_ge(q["ot"], g + 1)
                    if isinstance(g, int) and g >= 6:
                        v.wait_ge(q["on"], 2 * g)
                    v.tensor_copy(ou[:, :, :, :], ps[:, TRB, :].rearrange("p (t h c) -> p t h c", t=T, h=G4)[:, :, :, 0:1 + HD]).then_inc(q["ou"], 1)

                def over_sum(g):
                    v.wait_ge(q["ou"], g + 1)
                    v.reciprocal(rc[:, :, :], ou[:, :, :, 0]).then_inc(q["on"], 1)

                def scaled(g, hg, b):
                    v.wait_ge(q["on"], 2 * g + 1)
                    v.tensor_tensor(o_tok[:, b * T:(b + 1) * T, bass.ds(hg * (G4 * HD), G4 * HD)].rearrange("p t (h d) -> p t h d", h=G4),
                                    ou[:, :, :, 1:1 + HD],
                                    rc[:, :, :].rearrange("p t (h o) -> p t h o", o=1).to_broadcast([P, T, G4, HD]),
                                    ALU.mult).then_inc(q["on"], 1)

                def half(i, k, peeled):
                    n4 = 4 * i + k
                    hg1, b1, p1 = pos(i, k + 1)
                    qm = qk[:, 0, b1, :, bass.ds(4 * hg1 + 2 * p1, 2), :]
                    m1 = mx[:, (k + 1) % 2]
                    do_q = has(i, k + 1, peeled)
                    at = 16 * i + 4 * (k + 1)
                    do_o = k % 2 == 1 and (not peeled or 5 <= n4 < NPAIR - 1)
                    g = 2 * i + (k - 5) // 2
                    if do_o:
                        outputs_read(g)
                    for n in range(8):
                        if has(i, k + 2, peeled):
                            v.wait_ge(q["sm"], 32 * i + 8 * (k + 2) + n + 1)
                            v.reduce_max(mx[:, k % 2, n // 2, n % 2:n % 2 + 1], ps[:, 4 + n % 2, :], AX.X).then_inc(q["mx"], 1)
                        if peeled and k == -1 and n in (2, 4):
                            for kq, where in ((0, Q_PART), (1, K_PART)):
                                v4 = qkv[:, T:C, kq * D:kq * D + G4 * HD].rearrange("p t (h d) -> p t h d", h=G4)
                                r4 = spl[:, kq].rearrange("p t (h d) -> p t h d", h=G4)

                                def put(g):
                                    return qk[:, kq, 1, :, 0:G4, g * HD:(g + 1) * HD]
                                if n == 2:
                                    v.wait_ge(q["spa"], 7 + kq)
                                    v.tensor_tensor(r4, v4, put(where[0][0]), ALU.subtract).then_inc(q["spv"], 1)
                                else:
                                    v.wait_ge(q["spa"], 13 + kq)
                                    v.tensor_tensor(put(where[2][0]), r4, put(where[1][0]), ALU.subtract).then_inc(q["spv"], 1)
                        if do_o and n == 0:
                            over_sum(g)
                        if do_o and n == 1:
                            scaled(g, *pos(i, k - 5)[0:2])
                        if do_q and n == 0:
                            v.wait_ge(q["mx"], 32 * i + 8 * (k + 1) + 8)
                            v.tensor_scalar(qm[:, :, :, MXC], m1, -1.0, None, ALU.mult).then_inc(q["nstep"], 1)
                        if do_q and n == 1:
                            v.wait_ge(q["nstep"], at + 1)
                            v.scalar_tensor_tensor(nmx[:, :, :], m1, -1.0, qm[:, :, :, MXC], ALU.mult, ALU.subtract).then_inc(q["nstep"], 1)
                        if do_q and n == 2:
                            v.wait_ge(q["nstep"], at + 2)
                            v.tensor_copy(qm[:, :, :, MXC + 1], nmx[:, :, :]).then_inc(q["nstep"], 1)
                        if do_q and n == 3:
                            v.wait_ge(q["nstep"], at + 3)
                            v.tensor_tensor(qm[:, :, :, MXC + 2], nmx[:, :, :], qm[:, :, :, MXC + 1], ALU.subtract).then_inc(q["nstep"], 1)
                        if do_q and n == 5:
                            v.wait_ge(q["tq"], n4 + 2)
                            v.tensor_copy(qT[:, b1, bass.ds(2 * hg1 + p1, 1), :],
                                          psb[TRB][:, 0:S].rearrange("p (a s) -> p a s", a=1)).then_inc(q["evq"], 1)
                    if peeled and n4 >= NPAIR - 2:
                        g = n4 - NPAIR + 7
                        outputs_read(g)
                        over_sum(g)
                        scaled(g, g // 2, g % 2)

                first_group(0)
                if l == 0:
                    v.wait_ge(s["mod_mm"], 2)
                    modulation0(1, 6)
                tails(2 * l, 1)
                if l == 0:
                    v.wait_ge(s["mod_mm"], 3)
                    modulation1()
                    v.tensor_copy(cb_m, c_m[:, 4, :].rearrange("p (b o) -> p b o", o=1).to_broadcast([P, B, P])).then_inc(s["cb_v"], 1)
                    v.tensor_copy(cb_t[0:DT + 1], c_t[:, 4, :].rearrange("p (b o) -> p b o", o=1).to_broadcast([DT + 1, B, P])).then_inc(s["cb_v"], 1)
                half(0, -3, True)
                half(0, -2, True)
                def projected(b):
                    for c in range(b * T, (b + 1) * T):
                        v.wait_ge(s["proj_mm"], 8 * l + c + 1)
                        v.wait_ge(s["xb"], 16 * l + c + 1)
                        v.tensor_tensor(X[:, c, :], ps[:, PROJ_BANK[c], 0:D], X[:, c, :], ALU.add).then_inc(s["x_new"], 1)

                halves(v, half, -1)
                v.wait_ge(s["o_tr"], 4 * l + 2)
                v.tensor_copy(oTt[0:DT, 0, :], ps[0:DT, HEADS_BANK[0][1], :]).then_inc(s["oTt_ev"], 1)
                n = 2 * l + 1
                projected(0)
                outputs_read(7)
                over_sum(7)
                scaled(7, 3, 1)
                stats(n, 0)
                normalise(n, 0)
                projected(1)
                tails(n, 0)
                stats(n, 1)
                normalise(n, 1)
                if l == 1:
                    tails(3, 1)
                else:
                    def expert_tails(lo, hi):
                        for e in range(lo, hi):
                            cs = slice(e * HID, (e + 1) * HID)
                            if e:
                                v.wait_ge(s["et_v"], 4 * e)
                            parts_of_weights(e_src[0:TR_, cs], e_a[0:TR_], e_b[0:TR_], e_c[0:TR_], we_tail[0:TR_, cs], "et_v", 4 * e)

                    def mlp_out(lo, hi):
                        for c in range(lo, hi):
                            v.wait_ge(s["fc2_mm"], c + 1)
                            v.wait_ge(s["xb"], 8 + c + 1)
                            v.tensor_tensor(X[:, c, :], ps[:, FC2_BANK[c], 0:D], X[:, c, :], ALU.add).then_inc(s["x_new"], 1)
                    v.wait_ge(s["et_in"], 16)
                    v.wait_ge(s["gated"], GATED)
                    expert_tails(0, 2)
                    mlp_out(0, 2)
                    tails(1, 1)
                    mlp_out(2, T)
                    stats(2, 0)
                    expert_tails(2, 3)
                    normalise(2, 0)
                    expert_tails(3, E)
                    tails(2, 0)
                    mlp_out(T, C)
                    stats(2, 1)
                    normalise(2, 1)

            v.memset(below[:, :, :], 0.0).then_inc(s["bias2"], 1)
            for e in range(1, E):
                v.wait_ge(s["bias2"], e)
                v.memset(below[:, e, 0:e], 1.0).then_inc(s["bias2"], 1)
            v.wait_ge(s["lg_mm"], 1)
            v.tensor_copy(lg[:, :, :], ps[:, 0, 0:C * E].rearrange("p (c e) -> p c e", c=C)).then_inc(s["route"], 1)
            v.wait_ge(s["route"], 1)
            v.reduce_max(sm[:, 0, :], lg[:, :, :], AX.X).then_inc(s["moe_acc"], 1)
            v.wait_ge(s["moe_acc"], 1)
            v.tensor_tensor(lw[:, :, :], lg[:, :, :], sm[:, 0, :].rearrange("p (c o) -> p c o", o=1).to_broadcast([P, C, E]),
                            ALU.subtract).then_inc(s["route"], 1)
            r = 1

            def chain(ins):
                nonlocal r
                ins.then_inc(s["moe_acc"], 1)
                r += 1
                v.wait_ge(s["moe_acc"], r)
            v.wait_ge(s["bias2"], E)
            for e in range(E):
                other = lg[:, :, :]
                own = lg[:, :, e:e + 1].to_broadcast([P, C, E])
                chain(v.tensor_tensor(big[:, 0, :, e, :], other, own, ALU.is_gt))
                chain(v.tensor_tensor(big[:, 1, :, e, :], other, own, ALU.is_equal))
                chain(v.tensor_tensor(big[:, 1, :, e, :], big[:, 1, :, e, :],
                                      below[:, e:e + 1, :].to_broadcast([P, C, E]), ALU.mult))
            chain(v.tensor_tensor(big[:, 2, :, :, :], big[:, 0, :, :, :], big[:, 1, :, :, :], ALU.add))
            chain(v.reduce_sum(cw[:, :, :], big[:, 2, :, :, :], AX.X))
            chain(v.tensor_scalar(cw[:, :, :], cw[:, :, :], 2.0, None, ALU.is_lt))
            v.wait_ge(s["route"], 3)
            chain(v.tensor_tensor(cw[:, :, :], cw[:, :, :], lw[:, :, :], ALU.mult))
            chain(v.reduce_sum(sm[:, 1, :], cw[:, :, :], AX.X))
            chain(v.reciprocal(sm[:, 2, :], sm[:, 1, :]))
            chain(v.tensor_tensor(cw[:, :, :], cw[:, :, :], sm[:, 2, :].rearrange("p (c o) -> p c o", o=1).to_broadcast([P, C, E]), ALU.mult))
            v.wait_ge(s["we_in"], 48)
            for e in range(E):
                for c in range(C):
                    if e == 0:
                        v.tensor_scalar(acc[:, c, :], b2_row[:, 0, :], cw[:, c, 0:1], None, ALU.mult).then_inc(s["bias2"], 1)
                    else:
                        v.wait_ge(s["bias2"], E + (e - 1) * C + c + 1)
                        v.scalar_tensor_tensor(acc[:, c, :], b2_row[:, e, :], cw[:, c, e:e + 1], acc[:, c, :],
                                               ALU.mult, ALU.add).then_inc(s["bias2"], 1)
            for c in range(C):
                v.wait_ge(s["bias2"], E + (E - 1) * C + c + 1)
                for e in range(E):
                    n = c * E + e
                    v.wait_ge(s["moe_mm"], n + 1)
                    if e:
                        v.wait_ge(s["moe_acc"], r + n)
                    v.scalar_tensor_tensor(acc[:, c, :], ps[:, e, 0:D],
                                           cw[:, c, e:e + 1], acc[:, c, :], ALU.mult, ALU.add).then_inc(s["moe_acc"], 1)
                v.wait_ge(s["moe_acc"], r + (c + 1) * E)
                v.tensor_tensor(acc[:, c, :], acc[:, c, :], g_last[:, c // T, :], ALU.mult).then_inc(s["fin"], 1)
                v.wait_ge(s["fin"], 2 * c + 1)
                v.tensor_tensor(X[:, c, :], acc[:, c, :], X[:, c, :], ALU.add).then_inc(s["fin"], 1)

        @block.tensor
        def _(pe):
            mm = nc.tensor.matmul
            def columns(l, n):
                bank = 4 + l
                o = 0 if (l, n) == (0, 0) else NG + (2 * l + n) * NN
                for m in range(2):
                    at = (4 * l + 2 * n + m) * B
                    cs = slice(o + m * D, o + m * D + P)
                    mm(ps[:, bank, at:at + B], ada_m[:, cs], c_m[:, 4, :], start=True, stop=False)
                    mm(ps[:, bank, at:at + B], ada_t[0:DT + 1, cs], c_t[:, 4, :], start=False, stop=True)
                for m in range(2):
                    at = 16 + (4 * l + 2 * n + m) * B
                    cs = slice(o + 2 * D + m * TR_, o + 2 * D + (m + 1) * TR_)
                    mm(ps[0:TR_, bank, at:at + B], ada_m[:, cs], c_m[:, 4, :], start=True, stop=False)
                    last = mm(ps[0:TR_, bank, at:at + B], ada_t[0:DT + 1, cs], c_t[:, 4, :], start=False, stop=True)
                return last

            pe.wait_ge(s["ada1_in"], 16)
            pe.wait_ge(s["adat_in"], 16)
            pe.wait_ge(s["silu_v"], 6)
            columns(0, 0).then_inc(s["mod_mm"], 1)

            def gate_row(n):
                pe.wait_ge(s["cb_v"], 2)
                pe.wait_ge(s["adag_in"], 32)
                g, b = divmod(n, B)
                to = ps[:, PVB, (n % 3) * D:(n % 3 + 1) * D]
                mm(to, cb_m[:, b, :], ada_g[:, g * D:(g + 1) * D], start=True, stop=False)
                mm(to, cb_t[0:DT + 1, b, :], ada_g[0:DT + 1, NG + g * D:NG + (g + 1) * D],
                   start=False, stop=True).then_inc(s["gate_mm"], 1)

            def transpose_z(n, b):
                pe.wait_ge(s["ln_z"], 16 * n + 8 * b + 4)
                if n == 0:
                    pe.wait_ge(s["consts_in"], 16)
                for t in range(T):
                    last = pe.transpose(ps[0:TR_, 2 + b, t * P:(t + 1) * P], z[:, b, t, P:P + TR_], idf[:, :])
                last.then_inc(s["ln_zt"], 1)
                pe.wait_ge(s["ln_z"], 16 * n + 8 * b + 8)
                for t in range(T):
                    last = pe.transpose(ps[:, b, t * P:(t + 1) * P], z[:, b, t, 0:P], idf[:, :])
                last.then_inc(s["ln_zt"], 1)

            def normed_main(n, b):
                pe.wait_ge(s["ln_ht"], 2 * n + b + 1)

            def normed_tail(n, b):
                pe.wait_ge(s["ln_r"], 3 * (2 * n + b + 1))


            for l in range(2):
                q = a[l]
                if l == 0:
                    transpose_z(0, 0)
                    pe.wait_ge(s["wq_in"], 16)
                    pe.wait_ge(s["mod_v"], 6)
                else:
                    pe.wait_ge(s["gelu"], B * NM0)
                    pe.wait_ge(s["ones_h"], 1)

                def project(lo, hi):
                    kr = TB_ if l else TR_
                    for c in range(lo, hi):
                        b, t = divmod(c, T)
                        normed_main(2 * l, b)
                        if l == 1 and c == 2:
                            pe.wait_ge(s["x_new"], 16)
                        to = ps[:, QKV_BANK[c], 0:3 * D]
                        mm(to, hT[:, b, t * P:(t + 1) * P], wq_m[:, l, :], start=True, stop=False)
                        normed_tail(2 * l, b)
                        if l == 0:
                            pe.wait_ge(s["wt_p"], 4)
                        mm(to, hR[0:kr, b, t * P:(t + 1) * P],
                           w_tail[0:kr, 3 * D * l:3 * D * (l + 1)], start=False, stop=True).then_inc(s["qkv_mm"], 1)

                project(0, T)
                transpose_z(2 * l, 1)
                if l == 0:
                    pe.wait_ge(s["adar_in"], 16)
                    pe.wait_ge(s["qkv_ev"], 2)
                    columns(0, 1).then_inc(s["mod_mm"], 1)
                    columns(1, 0)

                def ready_kq(i, k, peeled):
                    n3 = 4 * i + k + 3
                    if not has(i, k + 3, peeled):
                        return
                    if not (peeled and n3 == 0):
                        pe.wait_ge(q["evk"], 12 * i + 3 * (k + 3))
                    if not (peeled and n3 < 2):
                        pe.wait_ge(q["evq"], 1 if peeled and n3 == 2 else 4 * i + k + 1)
                    if k % 2 == 1 and (not peeled or n3 >= 8):
                        pe.wait_ge(q["ou"], 2 * i + (k - 3) // 2)
                    if peeled and n3 < 4:
                        b3 = n3 // 2
                        pe.wait_ge(q["spv"], 4 * b3 + 8)
                        pe.wait_ge(q["spa"], 10 * b3 + 6)
                        if l == 1:
                            pe.wait_ge(q["qz"], 1)
                        else:
                            pe.wait_ge(s["qk_pad"], 2)
                        pe.wait_ge(s["qkv_ev"], 8 * l + 4 * b3 + 4)
                        pe.wait_ge(s["id_b"], 1)
                    else:
                        pe.wait_ge(q["spp"], 14 * (2 * i + (k + 3) // 2 - 1))

                def ready_max(i, k, peeled):
                    if not has(i, k + 1, peeled):
                        return
                    pe.wait_ge(q["nstep"], 16 * i + 4 * (k + 1) + 4)
                    if peeled and k % 2 == 1 and k + 3 >= NPAIR:
                        pe.wait_ge(q["ou"], (k - 3) // 2)
                    n = 12 * i + 3 * (k + 4)
                    pe.wait_ge(q["evk"], (6 if k == -1 else min(n, 3 * NPAIR)) if peeled else n)

                def transpose_heads(b):
                    pe.wait_ge(q["on"], 14 + 2 * b)
                    if b == 0:
                        pe.wait_ge(q["oev"], 7)
                    else:
                        pe.wait_ge(q["ex"], 4 * NPAIR)
                    for t in range(T):
                        last = pe.transpose(ps[:, HEADS_BANK[b][0], t * P:(t + 1) * P], o_tok[:, b * T + t, 0:P], idf[:, :])
                    last.then_inc(s["o_tr"], 1)
                    for t in range(T):
                        last = pe.transpose(ps[0:DT, HEADS_BANK[b][1], t * P:(t + 1) * P], o_tok[:, b * T + t, P:D], idf[:, :])
                    last.then_inc(s["o_tr"], 1)

                def outputs_to_tokens(g):
                    last_ = isinstance(g, int) and g >= 5
                    pe.wait_ge(q["evq"], NPAIR if last_ else 2 * g + 6)
                    if last_:
                        pe.wait_ge(q["ou"], g)
                    if last_ and g == 7:
                        pe.wait_ge(s["oTt_ev"], 2 * l + 1)
                    pe.wait_ge(q["oev"], g + 1)
                    for t in range(T):
                        last = pe.transpose(ps[:, TRB, t * P:(t + 1) * P], oS[:, t * P:(t + 1) * P], idf[:, :])
                    last.then_inc(q["ot"], 1)

                def head_outputs(m, g, u):
                    c, h0 = m // 2, (m % 2) * (S // 2)
                    bank = output_bank(g)
                    if m == 0:
                        pe.wait_ge(q["vs"], g + 1)
                        if isinstance(g, int):
                            if l == 0:
                                pe.wait_ge(s["vs_pad"], 2)
                                pe.wait_ge(s["gates_a"], 3)
                        if bank != PVB:
                            pe.wait_ge(q["mx"], 8 * NPAIR)
                        elif not (isinstance(g, int) and g == 0):
                            pe.wait_ge(q["oev"], g)
                    if m % 2 == 0:
                        pe.wait_ge(q["ex"], 8 * g + 5 + c)
                    for h in range(G4):
                        last = mm(ps[32 * h:32 * h + 32, bank, h0:h0 + S // 2], vS[:, u, c, h, :],
                                  prob[:, u, h, c, h0:h0 + S // 2], start=(m == 0), stop=(c == T - 1),
                                  tile_position=(0, 32 * h), skip_group_check=True)
                    if m % 2:
                        last.then_inc(q["pv"], 1)

                def half(i, k, peeled):
                    n4 = 4 * i + k
                    hg, b, pp = pos(i, k)
                    hg1, b1, p1 = pos(i, k + 1)
                    hg2, b2, p2 = pos(i, k + 2)
                    hg3, b3, p3 = pos(i, k + 3)
                    odd = k % 2 == 1

                    def score_for_max(j, hh):
                        n = 2 * j + hh
                        if not (peeled and n4 == -2 and n < 2):
                            pe.wait_ge(q["mx"], 32 * i + 8 * (k + 2) + n - 1)
                        mm(ps[:, 4 + hh, :], qT[:, b2, bass.ds(2 * hg2 + p2, 1), j * P:(j + 1) * P],
                           kT[:, b2, bass.ds(4 * hg2 + 2 * p2 + hh, 1), :], start=True, stop=True).then_inc(q["sm"], 1)

                    kq_at = 3 if peeled and k == -1 else 0

                    def transposes_kq():
                        if has(i, k + 3, peeled):
                            if not has(i, k + 2, peeled):
                                ready_kq(i, k, peeled)
                            for w, kq in ((0, 1), (1, 0)):
                                for t in range(T):
                                    last = pe.transpose(psb[TRB][:, w * S + t * P:w * S + (t + 1) * P],
                                                        qk[:, kq, b3, t, bass.ds(4 * hg3 + 2 * p3, 2), :], idb[:, :])
                            last.then_inc(q["tk"], 1)

                    def scores_less_max(j):
                        if j == 0:
                            pe.wait_ge(q["evq"], n4 + 1)
                        if not (peeled and n4 == 0 and j < 2):
                            pe.wait_ge(q["ex"], 16 * i + 4 * k + j - 1)
                        for hh in range(2):
                            last = mm(ps[:, 2 * (j % 2) + hh, :],
                                      kT[:, b, bass.ds(4 * hg + 2 * pp + hh, 1), j * P:(j + 1) * P],
                                      qT[:, b, bass.ds(2 * hg + pp, 1), :], start=True, stop=True)
                        last.then_inc(q["st"], 1)

                    if peeled and k == 0:
                        scores_less_max(0)
                        scores_less_max(1)
                    for j in range(T):
                        if has(i, k + 2, peeled):
                            if j == 0:
                                pe.wait_ge(q["evk"], 12 * i + 3 * (k + 3))
                                if l == 0 and peeled and k == -2:
                                    pe.wait_ge(s["mod_v"], MODV)
                            score_for_max(j, 0)
                        if has(i, k, peeled) and not (peeled and k == 0 and j < 2):
                            scores_less_max(j)
                        if l == 0 and peeled and k in (-1, 0, 1) and 1 <= j <= (2 if k == -1 else 3):
                            if k >= 0:
                                pe.wait_ge(s["gates_a"], k + 1)
                            gate_row(3 * (k % 3) + j - 1)
                        if has(i, k + 2, peeled):
                            if j == kq_at:
                                ready_kq(i, k, peeled)
                            if j == 2:
                                ready_max(i, k, peeled)
                            score_for_max(j, 1)
                        if peeled and k >= NPAIR - 2:
                            if j == 3 and k == NPAIR - 2:
                                outputs_to_tokens(5)
                            if j == 2 and k == NPAIR - 1:
                                outputs_to_tokens(6)
                            for m in LAST_PIECES[k - NPAIR + 2][j]:
                                head_outputs(m, k - NPAIR + 8, k % 2)
                            if j == 3 and k == NPAIR - 1:
                                transpose_heads(0)
                        elif 4 * odd + j and (not peeled or n4 >= 2 + odd):
                            sl = 4 * odd + j
                            g = 2 * i + (k - 2 - odd) // 2
                            u = ((k - 2 - odd) // 2) % 2
                            for m in ((6, 7) if sl == 7 else (sl - 1,)):
                                head_outputs(m, g, u)
                        if peeled and (k == -2 and j >= 1 or k == -1 and j == 0):
                            c = T + (j + 3) % 4
                            project(c, c + 1)
                        if j == kq_at:
                            transposes_kq()
                        if j == 2 and has(i, k + 1, peeled):
                            if not has(i, k + 2, peeled):
                                ready_max(i, k, peeled)
                            for t in range(T):
                                last = pe.transpose(psb[TRB][:, t * P:(t + 1) * P],
                                                    qk[:, 0, b1, t, bass.ds(4 * hg1 + 2 * p1, 2), :], idb[:, :])
                            last.then_inc(q["tq"], 1)

                        if j == 3 and not odd and (not peeled or 4 <= n4 < NPAIR - 2):
                            outputs_to_tokens(2 * i + (k - 4) // 2)

                def project_heads(b):
                    pe.wait_ge(s["oT_ev"], 2 * l + b + 1)
                    pe.wait_ge(s["oTt_ev"], 2 * l + b + 1)
                    for c in range(b * T, (b + 1) * T):
                        t = c % T
                        if t >= 2:
                            pe.wait_ge(s["x_new"], 16 * l + min(c - 1, 4))
                        to = ps[:, PROJ_BANK[c], 0:D]
                        mm(to, oT[:, b, t * P:(t + 1) * P], wog_m[:, b, l, :], start=True, stop=False)
                        mm(to, oTt[0:DT, b, t * P:(t + 1) * P], wog_t[:, b, l, :],
                           start=False, stop=True).then_inc(s["proj_mm"], 1)

                half(0, -3, True)
                if l == 0:
                    columns(1, 1).then_inc(s["mod_mm"], 1)
                halves(pe, half, -2)
                head_outputs(6, 7, 1)
                head_outputs(7, 7, 1)
                pe.wait_ge(s["gated"], 8)
                project_heads(0)
                outputs_to_tokens(7)
                transpose_heads(1)
                project_heads(1)
                transpose_z(2 * l + 1, 0)

                if l == 0:
                    pe.wait_ge(s["w1d_in"], 16)
                    pe.wait_ge(s["wt_v"], 1)

                    def mlp_up(b):
                        normed_main(1, b)
                        if b == 0:
                            pe.wait_ge(s["x_new"], 8)
                        for m in range(NM0):
                            n = b * NM0 + m
                            r = P if m < NM0 - 1 else HID - P * (NM0 - 1)
                            if n >= 4:
                                pe.wait_ge(s["gelu"], n - 3)
                            mm(ps[0:r, 4 + n % 4, :], w1d[:, m * P:m * P + r], hT[:, b, :], start=True, stop=False)
                            normed_tail(1, b)
                            mm(ps[0:r, 4 + n % 4, :], w_tail[0:TR_, 6 * D + m * P:6 * D + m * P + r], hR[0:TR_, b, :],
                               start=False, stop=True).then_inc(s["fc1_mm"], 1)

                    def mlp_down(b):
                        pe.wait_ge(s["gated"], GATED)
                        for c in range(b * T, (b + 1) * T):
                            t = c % T
                            if b == 0 and t >= 2:
                                pe.wait_ge(s["x_new"], 8 + c - 1)
                            for m in range(NM0):
                                r = P if m < NM0 - 1 else HID - P * (NM0 - 1)
                                if t == 0:
                                    pe.wait_ge(s["gelu"], NM0 * b + m + 1)
                                    if b == 0:
                                        normed_tail(1, 0)
                                last = mm(ps[:, FC2_BANK[c], 0:D], hm0[0:r, b, m, t * P:(t + 1) * P], w2g[0:r, b, m, :],
                                          start=(m == 0), stop=(m == NM0 - 1))
                            last.then_inc(s["fc2_mm"], 1)
                    mlp_up(0)
                    transpose_z(1, 1)
                    mlp_down(0)
                    mlp_up(1)
                    transpose_z(2, 0)
                    mlp_down(1)
                else:
                    pe.wait_ge(s["we_in"], 48)
                    pe.wait_ge(s["et_v"], 4 * E)
                    pe.wait_ge(s["x_new"], 24)

                    def up(b, lo, hi):
                        for m in range(lo, hi):
                            n = b * NM1 + m
                            normed_main(3, b)
                            if n >= 4:
                                pe.wait_ge(s["gelu"], B * NM0 + n - 3)
                            mm(ps[:, 4 + n % 4, :], w1e[:, m * P:(m + 1) * P], hT[:, b, :], start=True, stop=False)
                            normed_tail(3, b)
                            mm(ps[:, 4 + n % 4, :], we_tail[0:TR_, m * P:(m + 1) * P], hR[0:TR_, b, :],
                               start=False, stop=True).then_inc(s["fc1_mm"], 1)

                    def gate_logits():
                        for c in range(C):
                            b, t = divmod(c, T)
                            mm(ps[:, 0, c * E:(c + 1) * E], hT[:, b, t * P:(t + 1) * P], gate_m[:, :], start=True, stop=False)
                            last = mm(ps[:, 0, c * E:(c + 1) * E], hR[0:TR_, b, t * P:(t + 1) * P],
                                      w_tail[0:TR_, 6 * D + HID:NW], start=False, stop=True)
                        last.then_inc(s["lg_mm"], 1)

                    def down(b):
                        for c in range(b * T, (b + 1) * T):
                            t = c % T
                            for e in range(E):
                                if c >= 1:
                                    pe.wait_ge(s["moe_acc"], ROUTE + (c - 1) * E + e + 1)
                                else:
                                    pe.wait_ge(s["route"], 1)
                                lo, hi = e * HID, (e + 1) * HID
                                while lo < hi:
                                    m, r0 = divmod(lo, P)
                                    r1 = min(P, r0 + hi - lo)
                                    pe.wait_ge(s["gelu"], B * NM0 + b * NM1 + m + 1)
                                    last = mm(ps[:, e, 0:D],
                                              hm1[b][r0:r1, m, t * P:(t + 1) * P], w2e[r0:r1, m, :],
                                              start=(lo == e * HID), stop=(lo + r1 - r0 == hi))
                                    lo += r1 - r0
                                last.then_inc(s["moe_mm"], 1)
                    up(0, 0, UP0)
                    transpose_z(3, 1)
                    up(0, UP0, UP0 + 4)
                    normed_main(3, 1)
                    normed_tail(3, 1)
                    gate_logits()
                    up(0, UP0 + 4, NM1)
                    down(0)
                    up(1, 0, NM1)
                    down(1)


GATED = 8 + 6 + 2 * NM0
UP0 = 4
FC2_BANK = (0, 2, 0, 2, 1, 3, 6, 7)
HEADS_BANK = ((6, 7), (1, 3))
PROJ_BANK = (4, 6, 4, 6, 5, 7, 4, 6)
QKV_BANK = (4, 5, 6, 7, 0, 1, 2, 3)
LAST_PIECES = (((), (0, 1), (2, 3, 4), (5, 6, 7)), ((), (0, 1), (2, 3), (4, 5)))
MODV = 16
ROUTE = 1 + 3 * E + 7


_INS = ["x", "cond_t", "consts", "ada", "rows", "wqkv", "w_tails", "wo", "w1", "we_tails", "w2"]


def _lay_out(i):
    import numpy as np
    f = {k: np.asarray(v) for k, v in i.items()}
    L0, L1 = "L0_cond_", "L1_cond_"

    def tail(w):
        return np.tile(w[P:D], (NPART, 1))

    ada_w = [f[L0 + "ada_w"], f[L1 + "w_adaln"]]
    ada_b = [f[L0 + "ada_b"], f[L1 + "b_adaln"]]
    ada = [np.concatenate([w, v[None]]) for w, v in zip(ada_w, ada_b)]
    norms = []
    for w in ada:
        for lo in (0, 3):
            norms += [w[:, lo * D:(lo + 2) * D]] + [np.tile(w[:, m * D + P:(m + 1) * D], (1, NPART)) for m in (lo, lo + 1)]
    gates = [w[:, m * D:(m + 1) * D] for w in ada for m in (2, 5)]
    ln = np.stack([f[L0 + n] for n in ("ln1_w", "ln1_b", "ln2_w", "ln2_b")], axis=1)
    part = np.repeat(np.arange(NPART), DT)
    x_of, w_of = np.zeros(NPART, int), np.zeros(NPART, int)
    for n in range(3):
        x_of[list(Q_PART[n])] = n
        w_of[list(K_PART[n])] = n
    x_of, w_of = x_of[part], np.concatenate([w_of[part], np.arange(3)])
    x_of = np.concatenate([x_of, np.zeros(3, int)])
    pick = np.stack([-(k >= n).astype(np.float32) for k in (x_of, w_of) for n in (1, 2)], axis=1)
    wq0 = np.concatenate([f[L0 + n] for n in ("wq", "wk", "wv")], axis=1)
    wqkv = [wq0, f[L1 + "w_qkv"]]
    w1 = np.concatenate([f[L0 + "fc1_w"], f[L1 + "w1"].transpose(1, 0, 2).reshape(D, E * HID)], axis=1)
    b1 = np.concatenate([f[L0 + "fc1_b"], np.zeros(NM0 * P - HID, np.float32), f[L1 + "b1"].reshape(-1)])
    rows = np.concatenate([f[L0 + "wo_b"], f[L1 + "b_proj"], f[L0 + "fc2_b"], f[L1 + "b2"].reshape(-1),
                           ])[None]
    consts = np.zeros((P, P + 12 + NM0 + NM1 + E), np.float32)
    consts[:, 0:P] = np.eye(P, dtype=np.float32)
    consts[:, P:P + 4] = ln[0:P]
    consts[0:TR_, P + 4:P + 8] = tail(ln)
    consts[0:TB_, P + 8:P + 12] = pick
    consts[:, P + 12:P + 12 + NM0 + NM1] = b1.reshape(-1, P).T
    consts[:, P + 12 + NM0 + NM1:] = f[L1 + "w_gate"][0:P]
    w_tails = np.concatenate([tail(w) for w in (wqkv[0], wqkv[1], f[L0 + "fc1_w"], f[L1 + "w_gate"])], axis=1)
    bias = np.zeros((3, w_tails.shape[1]), np.float32)
    bias[:, 3 * D:6 * D] = f[L1 + "b_qkv"]
    return {
        "x": f["x"].reshape(B * S, D), "cond_t": f["cond_1152"].T, "consts": consts,
        "ada": np.concatenate(norms[0:3] + gates + norms[3:], axis=1), "rows": rows,
        "wqkv": np.stack([w[0:P] for w in wqkv]),
        "w_tails": np.concatenate([w_tails, bias]),
        "wo": np.stack([f[L0 + "wo"], f[L1 + "w_proj"]]), "w1": w1, "we_tails": tail(w1[:, HID:]),
        "w2": np.concatenate([f[L0 + "fc2_w"], f[L1 + "w2"].reshape(E * HID, D)], axis=0),
    }


def kernel(**inputs):
    import numpy as _np
    import concourse.bacc as _bacc
    from concourse import mybir as _mybir
    from concourse.bass_utils import run_bass_kernel_spmd as _run

    nc = _bacc.Bacc("TRN2", target_bir_lowering=False, num_devices=1)
    laid = _lay_out(inputs)
    arrays, args = {}, []
    for name in _INS:
        arr = _np.ascontiguousarray(laid[name])
        arrays[f"in_{name}"] = arr
        args.append(nc.dram_tensor(f"in_{name}", arr.shape, _mybir.dt.from_np(arr.dtype), kind="ExternalInput").ap())
    args.append(nc.dram_tensor("out_0", (B * S, D), _mybir.dt.float32, kind="ExternalOutput").ap())
    two_blocks(nc, *args)
    r = _run(nc, [arrays], core_ids=[0])
    return r.results[0]["out_0"].reshape(B, S, D)
```
